# Optimizing a Trainium2 kernel written in Bass

```python
import numpy as np
import jax
import jax.numpy as jnp

def _softmax(x, axis=-1):
    return jax.nn.softmax(x, axis=axis)

def _gelu(x):
    return jax.nn.gelu(x, approximate=True)

def _silu(x):
    return jax.nn.silu(x)

def _sigmoid(x):
    return jax.nn.sigmoid(x)

def _layernorm(x, axis=-1, eps=1e-05):
    m = jnp.mean(x, axis=axis, keepdims=True)
    v = jnp.var(x, axis=axis, keepdims=True)
    return (x - m) / jnp.sqrt(v + eps)

def _scatter_add(tgt, idx, src, axis=0):
    return tgt.at[idx].add(src)

def _segment_sum(src, seg, n):
    return jax.ops.segment_sum(src, seg, n)
kernel_name = 'mk_flamingo_gated_d2_seqx_r4_cd7c8f'

def setup_inputs(seed: int=0):
    np.random.seed(seed)
    _w = jnp.asarray

    def _rec_inputs():
        import jax
        import jax.numpy as jnp
        _rk = jax.random.key(seed)
        x = -0.0003929 + 0.9999 * jax.random.normal(jax.random.fold_in(_rk, 1), (2, 1024, 256), jnp.float32)
        _lenS = 1024 - jax.random.randint(jax.random.fold_in(_rk, 7), (2,), 0, max(1, 1024 // 4) + 1, jnp.int32)
        _lenS2 = 154 - jax.random.randint(jax.random.fold_in(_rk, 8), (2,), 0, max(1, 154 // 4) + 1, jnp.int32)
        _ctx_1024P = jax.random.normal(jax.random.fold_in(_rk, 11), (2, 16, 256), jnp.float32)
        _ctx_1024c = jax.random.dirichlet(jax.random.fold_in(_rk, 511), 0.3 * jnp.ones((16,), jnp.float32), (2, 154))
        _ctx_1024t = jnp.einsum('bsk,bkd->bsd', _ctx_1024c, _ctx_1024P)
        _ctx_1024t = _ctx_1024t * jax.lax.rsqrt(jnp.mean(jnp.square(_ctx_1024t)) + 1e-12) * 0.953939
        ctx_1024 = 2.81802e-05 + 1.00001 * (_ctx_1024t + 0.3 * jax.random.normal(jax.random.fold_in(_rk, 611), (2, 154, 256), jnp.float32))
        _validS = jnp.arange(1024)[None, :] < _lenS[:, None]
        _validS2 = jnp.arange(154)[None, :] < _lenS2[:, None]
        _causal = jnp.tril(jnp.ones((1024, 1024), dtype=bool))
        mask_BxS2_bk0 = jnp.logical_not(jnp.broadcast_to(_validS2[:, :], (2, 154)))
        _g = jax.random.normal(jax.random.fold_in(_rk, 9001), (2, 2), jnp.float32)
        _g = jnp.sign(_g) * jnp.maximum(jnp.abs(_g), 1.0) + (_g == 0) * 1.0
        g_xattn = _g[0]
        g_ffn = _g[1]
        return (x, ctx_1024, mask_BxS2_bk0, g_xattn, g_ffn)
    x, ctx_1024, mask_BxS2_bk0, g_xattn, g_ffn = _rec_inputs()

    def _L0_xattn_setup():
        import jax, jax.numpy as jnp
        import numpy as np
        B, S1, S2, E, P = (8, 512, 512, 256, 256)
        key = jax.random.key(seed)
        k1, k2, k3, k4, k5 = jax.random.split(key, 5)
        query = jax.random.normal(k1, (B, S1, E), dtype=jnp.float32)
        key_t = jax.random.normal(k2, (B, S2, E), dtype=jnp.float32)
        value = jax.random.normal(k3, (B, S2, E), dtype=jnp.float32)
        bound = 1.0 / np.sqrt(E)
        W = jax.random.uniform(k4, (P, E), minval=-bound, maxval=bound, dtype=jnp.float32)
        b = jax.random.uniform(k5, (P,), minval=-bound, maxval=bound, dtype=jnp.float32)
        return {'query': query, 'key': key_t, 'value': value, 'W': W, 'b': b}
    _L0_xattn_all = _L0_xattn_setup()
    _L0_xattn_in = {k: v for k, v in _L0_xattn_all.items() if k in ('W', 'b')}
    del _L0_xattn_all

    def _L0_ffn_setup():
        import jax, jax.numpy as jnp
        import numpy as np
        NUM_EXPERTS = 8
        HIDDEN = 256
        FFN = 1024
        BATCH = 2
        SEQ = 512
        key = jax.random.key(seed)
        k_x, k_g, k_u, k_d = jax.random.split(key, 4)
        scale_in = 1.0 / np.sqrt(HIDDEN)
        scale_mid = 1.0 / np.sqrt(FFN)
        return {'hidden_states': jax.random.normal(k_x, (BATCH, SEQ, HIDDEN), dtype=jnp.float32), 'Wg': jax.random.normal(k_g, (NUM_EXPERTS, HIDDEN, FFN), dtype=jnp.float32) * scale_in, 'Wu': jax.random.normal(k_u, (NUM_EXPERTS, HIDDEN, FFN), dtype=jnp.float32) * scale_in, 'Wd': jax.random.normal(k_d, (NUM_EXPERTS, FFN, HIDDEN), dtype=jnp.float32) * scale_mid}
    _L0_ffn_all = _L0_ffn_setup()
    _L0_ffn_in = {k: v for k, v in _L0_ffn_all.items() if k in ('Wg', 'Wu', 'Wd')}
    del _L0_ffn_all

    def _L1_xattn_setup():
        import jax, jax.numpy as jnp
        import numpy as np
        DIM = 256
        DIM_MEDIA = 256
        DIM_HEAD = 64
        HEADS = 8
        INNER = DIM_HEAD * HEADS
        B, N_TOK, N_LAT = (4, 1024, 256)
        LN_EPS = 1e-05
        key = jax.random.key(seed)
        ks = jax.random.split(key, 6)
        x = jax.random.normal(ks[0], (B, N_TOK, DIM), dtype=jnp.float32)
        media = jax.random.normal(ks[1], (B, N_LAT, DIM_MEDIA), dtype=jnp.float32)
        media_mask = jax.random.randint(ks[2], (B, N_LAT), 0, 2).astype(bool)
        media_mask = media_mask.at[:, 0].set(True)
        ln_gamma = jnp.ones((DIM,), jnp.float32)
        ln_beta = jnp.zeros((DIM,), jnp.float32)
        Wq = jax.random.normal(ks[3], (DIM, INNER), jnp.float32) * DIM ** (-0.5)
        Wkv = jax.random.normal(ks[4], (DIM_MEDIA, 2 * INNER), jnp.float32) * DIM_MEDIA ** (-0.5)
        Wout = jax.random.normal(ks[5], (INNER, DIM), jnp.float32) * INNER ** (-0.5)
        return {'x': x, 'media': media, 'media_mask': media_mask, 'ln_gamma': ln_gamma, 'ln_beta': ln_beta, 'Wq': Wq, 'Wkv': Wkv, 'Wout': Wout}
    _L1_xattn_all = _L1_xattn_setup()
    _L1_xattn_in = {k: v for k, v in _L1_xattn_all.items() if k in ('ln_gamma', 'ln_beta', 'Wq', 'Wkv', 'Wout')}
    del _L1_xattn_all

    def _L1_ffn_setup():
        import jax, jax.numpy as jnp
        import numpy as np
        H = 256
        E = 8
        B, S = (4, 512)
        key = jax.random.key(seed)
        k1, k2, k3, k4 = jax.random.split(key, 4)
        x = jax.random.normal(k1, (B, S, H), dtype=jnp.float32)
        wg = jax.random.normal(k2, (H, E), dtype=jnp.float32) * 0.02
        W = jax.random.normal(k3, (E, H, H), dtype=jnp.float32) * 0.02
        b = jax.random.normal(k4, (E, H), dtype=jnp.float32) * 0.02
        return {'x': x, 'wg': wg, 'W': W, 'b': b}
    _L1_ffn_all = _L1_ffn_setup()
    _L1_ffn_in = {k: v for k, v in _L1_ffn_all.items() if k in ('wg', 'W', 'b')}
    del _L1_ffn_all
    return {'x': x, 'ctx_1024': ctx_1024, 'mask_BxS2_bk0': mask_BxS2_bk0, 'g_xattn': g_xattn, 'g_ffn': g_ffn, 'L0_xattn_W': _L0_xattn_in['W'], 'L0_xattn_b': _L0_xattn_in['b'], 'L0_ffn_Wg': _L0_ffn_in['Wg'], 'L0_ffn_Wu': _L0_ffn_in['Wu'], 'L0_ffn_Wd': _L0_ffn_in['Wd'], 'L1_xattn_ln_gamma': _L1_xattn_in['ln_gamma'], 'L1_xattn_ln_beta': _L1_xattn_in['ln_beta'], 'L1_xattn_Wq': _L1_xattn_in['Wq'], 'L1_xattn_Wkv': _L1_xattn_in['Wkv'], 'L1_xattn_Wout': _L1_xattn_in['Wout'], 'L1_ffn_wg': _L1_ffn_in['wg'], 'L1_ffn_W': _L1_ffn_in['W'], 'L1_ffn_b': _L1_ffn_in['b']}

def reference(x, ctx_1024, mask_BxS2_bk0, g_xattn, g_ffn, L0_xattn_W, L0_xattn_b, L0_ffn_Wg, L0_ffn_Wu, L0_ffn_Wd, L1_xattn_ln_gamma, L1_xattn_ln_beta, L1_xattn_Wq, L1_xattn_Wkv, L1_xattn_Wout, L1_ffn_wg, L1_ffn_W, L1_ffn_b):
    import jax
    import jax.numpy as jnp

    def _L0_xattn_ref(query, key, value, W, b):
        import jax, jax.numpy as jnp
        import numpy as np
        B, S1, S2, E, P = (8, 512, 512, 256, 256)
        q = jnp.einsum('bse,pe->bsp', query, W) + b
        k = jnp.einsum('bse,pe->bsp', key, W) + b
        v = jnp.einsum('bse,pe->bsp', value, W) + b
        scale = 1.0 / jnp.sqrt(jnp.float32(k.shape[-1]))
        scores = jnp.einsum('bqp,bkp->bqk', q, k) * scale
        weights = jax.nn.softmax(scores, axis=-1)
        return jnp.einsum('bqk,bkp->bqp', weights, v)

    def _L0_ffn_ref(hidden_states, Wg, Wu, Wd):
        import jax, jax.numpy as jnp
        import numpy as np
        NUM_EXPERTS = 8
        HIDDEN = 256
        FFN = 1024
        BATCH = 2
        SEQ = 512
        B, S, H = hidden_states.shape
        x = hidden_states.reshape(-1, H)

        def expert_step(acc, w):
            wg, wu, wd = w
            h = jax.nn.silu(x @ wg) * (x @ wu)
            return (acc + h @ wd, None)
        acc, _ = jax.lax.scan(expert_step, jnp.zeros_like(x), (Wg, Wu, Wd))
        return acc.reshape(B, S, H)

    def _L1_xattn_ref(x, media, media_mask, ln_gamma, ln_beta, Wq, Wkv, Wout):
        import jax, jax.numpy as jnp
        import numpy as np
        DIM = 256
        DIM_MEDIA = 256
        DIM_HEAD = 64
        HEADS = 8
        INNER = DIM_HEAD * HEADS
        B, N_TOK, N_LAT = (4, 1024, 256)
        LN_EPS = 1e-05
        scale = DIM_HEAD ** (-0.5)
        mu = jnp.mean(x, axis=-1, keepdims=True)
        var = jnp.mean(jnp.square(x - mu), axis=-1, keepdims=True)
        xn = (x - mu) * jax.lax.rsqrt(var + LN_EPS) * ln_gamma + ln_beta
        q = xn @ Wq * scale
        kv = media @ Wkv
        k, v = jnp.split(kv, 2, axis=-1)

        def to_heads(t):
            b, n, _ = t.shape
            return t.reshape(b, n, HEADS, DIM_HEAD).transpose(0, 2, 1, 3)
        q, k, v = (to_heads(q), to_heads(k), to_heads(v))
        sim = jnp.einsum('bhid,bhjd->bhij', q, k)
        neg_inf = jnp.float32(-jnp.inf)
        sim = jnp.where(media_mask[:, None, None, :], sim, neg_inf)
        sim = sim - jax.lax.stop_gradient(jnp.max(sim, axis=-1, keepdims=True))
        attn = jax.nn.softmax(sim, axis=-1)
        out = jnp.einsum('bhij,bhjd->bhid', attn, v)
        out = out.transpose(0, 2, 1, 3).reshape(out.shape[0], out.shape[2], INNER)
        return out @ Wout

    def _L1_ffn_ref(x, wg, W, b):
        import jax, jax.numpy as jnp
        import numpy as np
        H = 256
        E = 8
        B, S = (4, 512)
        Bb, Ss, Hh = x.shape
        Ee = wg.shape[1]
        T = Bb * Ss
        C = T // Ee
        xt = x.reshape(T, Hh)
        logits = xt @ wg
        probs = jax.nn.softmax(logits, axis=-1)
        idx = jnp.argmax(probs, axis=-1)
        mask = jax.nn.one_hot(idx, Ee, dtype=xt.dtype)
        locations = jnp.cumsum(mask, axis=0) - mask
        mask = mask * (locations < C).astype(xt.dtype)
        gate = jnp.sum(probs * mask, axis=-1)
        loc_s = jnp.sum(locations * mask, axis=-1).astype(jnp.int32)
        loc_oh = jax.nn.one_hot(loc_s, C, dtype=xt.dtype)
        dispatch = mask[:, :, None] * loc_oh[:, None, :]
        combine = gate[:, None, None] * dispatch
        exp_in = jnp.einsum('tec,th->ech', dispatch, xt)
        exp_out = jnp.einsum('ech,efh->ecf', exp_in, W) + b[:, None, :]
        out = jnp.einsum('tec,ecf->tf', combine, exp_out)
        return out.reshape(Bb, Ss, Hh)
    x = x + jnp.tanh(g_xattn[0]) * _L0_xattn_ref(_layernorm(x, axis=-1), ctx_1024, ctx_1024, L0_xattn_W, L0_xattn_b)
    x = x + jnp.tanh(g_ffn[0]) * _L0_ffn_ref(_layernorm(x, axis=-1), L0_ffn_Wg, L0_ffn_Wu, L0_ffn_Wd)
    x = x + jnp.tanh(g_xattn[1]) * _L1_xattn_ref(_layernorm(x, axis=-1), ctx_1024, mask_BxS2_bk0, L1_xattn_ln_gamma, L1_xattn_ln_beta, L1_xattn_Wq, L1_xattn_Wkv, L1_xattn_Wout)
    x = x + jnp.tanh(g_ffn[1]) * _L1_ffn_ref(_layernorm(x, axis=-1), L1_ffn_wg, L1_ffn_W, L1_ffn_b)
    return x

_drawn_inputs = setup_inputs


def setup_inputs(seed=0):
    import zlib

    import numpy as np

    out = dict(_drawn_inputs(seed))
    spreads = {'g_ffn': (-1.0, 0.6), 'L1_xattn_ln_gamma': (1.0, 0.2), 'L1_xattn_ln_beta': (0.0, 0.486)}
    factors = {'L1_ffn_b': 30.53}
    for name, (base, spread) in spreads.items():
        noise = np.random.default_rng([zlib.crc32(name.encode()), seed]).standard_normal(out[name].shape)
        drawn = base * np.exp(spread * noise) if base else spread * noise
        out[name] = jnp.asarray(drawn.astype(out[name].dtype))
    for name, factor in factors.items():
        out[name] = (out[name] * factor).astype(out[name].dtype)
    return out
```

```python
import numpy as np
import concourse.bass as bass
from concourse import mybir
from contextlib import ExitStack

F32 = mybir.dt.float32
F32R = mybir.dt.float32r
U32 = mybir.dt.uint32
U8 = mybir.dt.uint8
ALU = mybir.AluOpType
ACT = mybir.ActivationFunctionType
AX = mybir.AxisListType

P = 128
EPS = 1e-5
MASKED = -1e30


class Arena:

    def __init__(self, nc, start, end):
        self.nc, self.at, self.end = nc, start, end

    def take(self, name, shape, dt, size=4):
        n = size
        for d in shape[1:]:
            n *= d
        t = self.nc.alloc_sbuf_tensor_at(name, shape, dt, offset=self.at)
        self.at += -(-n // 32) * 32
        assert self.at <= self.end, (name, self.at, self.end)
        return t


class Steps:

    def __init__(self, sem):
        self.sem, self.base, self.n = sem, 0, 0

    def did(self, ins):
        ins.then_inc(self.sem, 1)
        self.n += 1

    def value(self):
        return self.base + self.n

    def enter(self, trip, per_trip):
        self.start = self.base + self.n
        self.per_trip = per_trip
        self.base, self.n = trip * per_trip + self.start, 0

    def leave(self, trips):
        assert self.n == self.per_trip, (self.n, self.per_trip)
        self.base, self.n = self.start + trips * self.per_trip, 0


def flamingo_kernel(nc, x, ctx, mask, g_xattn, g_ffn, W0, b0, Wg, Wu, Wd, gamma, beta, Wq, Wkv, Wout, wgate, We, be, out):
    B, S, D = x.shape
    KEYS = ctx.shape[1]
    KH = KEYS // 2
    NE0, _, F = Wg.shape
    INNER = Wq.shape[1]
    HD = 64
    HEADS = INNER // HD
    E = wgate.shape[1]
    T = B * S
    NT = T // P
    CT = 4
    CH = CT * P
    NC = NT // CT
    CB = S // CH
    CAP = T // E
    KB = D // P
    HF = F // 2
    FB = HF // P
    HB = INNER // P
    AK = B * KEYS
    HPB = 2
    SIM = (2, 3, 4, 6)
    DROPPED = 4 * T
    assert KH * 2 == KEYS and KB == 2 and CB == 2 and CAP == 2 * P and HB == 4

    x_v = x.rearrange("b (t p) d -> p (b t) d", p=P)
    out_v = out.rearrange("b (t p) d -> p (b t) d", p=P)
    ctx_v = ctx.rearrange("b (k r) d -> r (b k) d", r=KH)
    Wg_v = Wg.rearrange("e (k p) f -> e p k f", p=P)
    Wu_v = Wu.rearrange("e (k p) f -> e p k f", p=P)
    Wd_v = Wd.rearrange("e (k p) d -> e p k d", p=P)
    We_v = We.rearrange("e (k p) h -> e p k h", p=P)
    slots_in = nc.dram_tensor("slots_in", [T, D], F32).ap()
    slots_out = nc.dram_tensor("slots_out", [T, D], F32).ap()
    slots_in_v = slots_in.rearrange("(e k p) d -> e p k d", p=P, k=CAP // P)
    slots_out_v = slots_out.rearrange("(e k p) d -> e p k d", p=P, k=CAP // P)
    slots_zero_v = slots_in.rearrange("(n p) d -> p n d", p=P)

    with ExitStack() as stack:
        def sem(name):
            return stack.enter_context(nc.semaphore(name))

        base = -(-nc.sbuf_base // 32) * 32
        end = nc.sbuf_usable_end // 32 * 32
        keep = Arena(nc, base, end)
        x_res = keep.take("x_res", [P, NT, D], F32)
        ident = keep.take("ident", [P, P], F32)
        before = keep.take("before", [P, P], F32)
        ones = keep.take("ones", [P, P], F32)
        ones_r = keep.take("ones_r", [1, P], F32R)
        A0 = keep.take("A0", [P, KB, AK], F32)
        r0 = keep.take("r0", [1, AK], F32)
        V0 = keep.take("V0", [KH, 2 * B, D], F32)
        ctxT = keep.take("ctxT", [P, KB, AK], F32)
        graw = keep.take("graw", [P, 4], F32)
        tg = keep.take("tg", [P, 4], F32)
        mhalf = keep.take("mhalf", [P, 8], F32)
        gammac = keep.take("gammac", [P, KB], F32)
        betac = keep.take("betac", [P, KB], F32)
        stats = keep.take("stats", [P, 8, 6], F32)
        mv = keep.take("mv", [P, 8, 2], F32)
        ve = keep.take("ve", [P, 8], F32)
        rstd = keep.take("rstd", [P, 8], F32)
        wgr = keep.take("wgr", [P, KB, E], F32)
        mask8 = keep.take("mask8", [P, AK], U8, size=1)
        maskf = keep.take("maskf", [P, AK], F32)
        mrow = keep.take("mrow", [1, B, KEYS], F32R)
        anyv = keep.take("anyv", [P, B], F32)
        ranyv = keep.take("ranyv", [P, B], F32)
        flag = keep.take("flag", [P, B], F32)
        desc = keep.take("desc", [P, CT, E], F32)
        slot0 = keep.take("slot0", [P, CT, E], F32)
        gate_all = keep.take("gate_all", [P, NT], F32)
        slot_all = keep.take("slot_all", [P, NT], U32)
        carry = keep.take("carry", [P, E], F32)

        sa = Arena(nc, keep.at, end)
        W0s = sa.take("W0s", [P, KB, D], F32)
        W0T = sa.take("W0T", [P, KB, D], F32)
        bcol = sa.take("bcol", [P, KB], F32)
        ctx_s = sa.take("ctx_s", [KH, 2 * B, D], F32)
        k0T = sa.take("k0T", [P, KB, AK], F32)
        xnA = sa.take("xnA", [P, 2 * CT, D], F32)
        xnT = sa.take("xnT", [P, CB, KB, CH], F32)
        PA = sa.take("PA", [P, 2 * CT, KEYS], F32)
        PTA = sa.take("PTA", [KH, CB, 2, CH], F32)
        nmA = sa.take("nmA", [P, 2 * CT], F32)
        nmsA = sa.take("nmsA", [P, 2 * CT], F32)
        denA = sa.take("denA", [P, 2 * CT], F32)
        rdenA = sa.take("rdenA", [P, 2 * CT], F32)
        coefA = sa.take("coefA", [P, 2 * CT], F32)

        sc = Arena(nc, keep.at, sa.at)
        Wkvs = sc.take("Wkvs", [P, KB, 2 * INNER], F32)
        Wqs = sc.take("Wqs", [P, KB, INNER], F32)
        Wouts = sc.take("Wouts", [P, HB, D], F32)
        brow = sc.take("brow", [1, E * D], F32)
        k1T = sc.take("k1T", [P, HB, AK], F32)

        sb = Arena(nc, sa.at, end)
        acc = sb.take("acc", [P, KB, T], F32)
        xT_hi = sb.take("xT_hi", [P, KB, T], F32R)
        xT_lo = sb.take("xT_lo", [P, KB, T], F32R)
        raw_g = sb.take("raw_g", [P, KB, HF], F32)
        raw_u = sb.take("raw_u", [P, KB, HF], F32)
        raw_d = sb.take("raw_d", [P, FB, D], F32)
        wsplit = [{k: sb.take(f"w_{k}{i}", [P, FB, D] if k[0] == "d" else [P, KB, HF], F32R)
                   for k in ("g_hi", "g_lo", "u_hi", "u_lo", "d_hi", "d_lo")} for i in range(2)]
        silu = [sb.take(f"silu{i}", [P, CH], F32) for i in range(2)]
        hid = [sb.take(f"hid{i}", [P, CH], F32) for i in range(2)]
        hid_hi = [sb.take(f"hid_hi{i}", [P, CH], F32R) for i in range(2)]
        hid_lo = [sb.take(f"hid_lo{i}", [P, CH], F32R) for i in range(2)]

        sd = Arena(nc, sa.at + 4 * KB * T, end)
        V1 = sd.take("V1", [KH, 2 * B, INNER], F32)
        yc = sd.take("yc", [P, KB, CH], F32)
        xnC = sd.take("xnC", [P, CT, D], F32)
        xnC2 = sd.take("xnC2", [P, CT, D], F32)
        xnTc = sd.take("xnTc", [P, KB, CH], F32)
        qT = sd.take("qT", [P, HB, CH], F32)
        kcur = sd.take("kcur", [P, HB, KEYS], F32)
        vcur = sd.take("vcur", [KH, 2, INNER], F32)
        mcur = sd.take("mcur", [1, KEYS], F32R)
        fcur = sd.take("fcur", [P, 1], F32)
        PC = [sd.take(f"PC{i}", [P, HEADS, KEYS], F32) for i in range(2)]
        PTC = sd.take("PTC", [KH, 2 * HEADS, P], F32)
        nmC = [sd.take(f"nmC{i}", [P, HEADS], F32) for i in range(2)]
        denC = [sd.take(f"denC{i}", [P, HEADS], F32) for i in range(2)]
        rdenC = [sd.take(f"rdenC{i}", [P, HEADS], F32) for i in range(2)]
        rdenF = [sd.take(f"rdenF{i}", [P, HEADS], F32) for i in range(2)]
        oT = sd.take("oT", [P, HB, P], F32)
        xn4 = sd.take("xn4", [P, CT, D], F32)
        xn4T = sd.take("xn4T", [P, KB, CH], F32)
        rt = {k: sd.take(f"rt_{k}", [P, CT, E], F32) for k in
              ("d", "e", "p", "top", "score", "one", "pre", "loc", "m1", "m2")}
        rs = {k: sd.take(f"rs_{k}", [P, CT], F32) for k in
              ("max", "sum", "rsum", "best", "loc", "first", "keep", "slot", "far")}
        slot_c = sd.take("slot_c", [P, CT], U32)
        ye_gath = sd.take("ye_gath", [P, NT, D], F32)
        coefD = sd.take("coefD", [P, NT], F32)
        we_raw = [sd.take(f"we_raw{i}", [P, KB, D], F32) for i in range(2)]
        weT = [sd.take(f"weT{i}", [P, KB, D], F32) for i in range(2)]
        xe = [sd.take(f"xe{i}", [P, CAP // P, D], F32) for i in range(2)]
        xeT = [sd.take(f"xeT{i}", [P, KB, CAP], F32) for i in range(2)]
        ye = [sd.take(f"ye{i}", [P, CAP // P, D], F32) for i in range(2)]

        bank = [stack.enter_context(nc.psum_tensor(f"bank{i}", [P, 512], F32)) for i in range(8)]

        x_in, ctx_in, w0_in, small_in, wc_in = (sem(n) for n in ("x_in", "ctx_in", "w0_in", "small_in", "wc_in"))
        consts_ready, acc_zeroed, cleared = sem("consts_ready"), sem("acc_zeroed"), sem("cleared")
        slots_zeroed = sem("slots_zeroed")
        tg_ready = sem("tg_ready")
        pool_steps, dve_steps = sem("pool_steps"), sem("dve_steps")
        prep_pe, prep_act, prep_dve = sem("prep_pe"), sem("prep_act"), sem("prep_dve")
        var_ready, rstd_ready = sem("var_ready"), sem("rstd_ready")
        a_ln1, a_xnT_ps, a_xnT, a_sc_ps, a_nmax, a_probs, a_pT_ps, a_pT_act, a_pT_dve, a_out_ps, a_ln2, a_x2T_ps = (
            sem(n) for n in ("a_ln1", "a_xnT_ps", "a_xnT", "a_sc_ps", "a_nmax", "a_probs", "a_pT_ps", "a_pT_act",
                             "a_pT_dve", "a_out_ps", "a_ln2", "a_x2T_ps"))
        xT_hi_ready, xT_lo_ready = sem("xT_hi_ready"), sem("xT_lo_ready")
        raw_in, raw_split, w_hi_ready = (sem(n) for n in ("raw_in", "raw_split", "w_hi_ready"))
        gate_ps, up_ps, silu_ready, hi_ready, lo_ready = (
            sem(n) for n in ("gate_ps", "up_ps", "silu_ready", "hi_ready", "lo_ready"))
        hid_ready = [sem(f"hid_ready{i}") for i in range(2)]
        down_done = [sem(f"down_done{i}") for i in range(2)]
        acc_added = [sem(f"acc_added{i}") for i in range(2)]
        c_prep_ps, c_prep_act, c_prep_dve = sem("c_prep_ps"), sem("c_prep_act"), sem("c_prep_dve")
        c_y, c_yT_ps, c_ln, c_xnT_ps, c_xnT, c_q_ps, c_q_act, c_q_dve, c_cur = (
            sem(n) for n in ("c_y", "c_yT_ps", "c_ln", "c_xnT_ps", "c_xnT", "c_q_ps", "c_q_act", "c_q_dve", "c_cur"))
        c_sim_ps, c_nmax, c_probs, c_rden, c_norm, c_pT_ps, c_pT_act, c_pT_dve, c_o_ps, c_o, c_out_ps, c_res = (
            sem(n) for n in ("c_sim_ps", "c_nmax", "c_probs", "c_rden", "c_norm", "c_pT_ps", "c_pT_act", "c_pT_dve",
                             "c_o_ps", "c_o", "c_out_ps", "c_res"))
        r_ln, r_xnT_ps, r_xnT, r_logit_ps, r_shift, r_exp, r_one, r_loc_ps, r_slot, scattered = (
            sem(n) for n in ("r_ln", "r_xnT_ps", "r_xnT", "r_logit_ps", "r_shift", "r_exp", "r_one", "r_loc_ps",
                             "r_slot", "scattered"))
        e_w_in = [sem(f"e_w_in{i}") for i in range(2)]
        e_x_in = [sem(f"e_x_in{i}") for i in range(2)]
        e_stored = [sem(f"e_stored{i}") for i in range(2)]
        e_wT_ps, e_wT, e_xT_ps, e_xT, e_y_ps, e_y = (
            sem(n) for n in ("e_wT_ps", "e_wT", "e_xT_ps", "e_xT", "e_y_ps", "e_y"))
        gathered, d_out, stored = sem("gathered"), sem("d_out"), sem("stored")

        block = stack.enter_context(nc.Block())
        BLK = 2 * NC * FB
        HALFBLK = NC * FB
        UNITS = 2 * NC

        def start_at_one(eng, sems):
            for s in sems:
                eng.sem_inc(s, 1)

        @block.sync
        def _(sp):
            start_at_one(sp, e_stored)
            for h in range(CB):
                sp.dma_start(x_res[:, h * CT:(h + 1) * CT, :], x_v[:, h * CT:(h + 1) * CT, :]).then_inc(x_in, 16)
            sp.wait_ge(x_in, 16 * CB)
            for h in range(CB, 2 * CB):
                sp.dma_start(x_res[:, h * CT:(h + 1) * CT, :], x_v[:, h * CT:(h + 1) * CT, :]).then_inc(x_in, 16)

            def load_half(e, half):
                f = slice(half * HF, (half + 1) * HF)
                sp.dma_start(raw_g[:], Wg_v[e, :, :, f]).then_inc(raw_in, 16)
                sp.dma_start(raw_u[:], Wu_v[e, :, :, f]).then_inc(raw_in, 16)
                sp.dma_start(raw_d[:], Wd_v[e, :, half * FB:(half + 1) * FB, :]).then_inc(raw_in, 16)

            load_half(0, 0)
            sp.wait_ge(xT_hi_ready, 4 * CB)
            sp.wait_ge(xT_lo_ready, 4 * CB)
            sp.dma_start(Wkvs[:], Wkv.rearrange("(k p) n -> p k n", p=P)).then_inc(wc_in, 16)
            sp.dma_start(Wqs[:], Wq.rearrange("(k p) n -> p k n", p=P)).then_inc(wc_in, 16)
            sp.dma_start(Wouts[:], Wout.rearrange("(k p) n -> p k n", p=P)).then_inc(wc_in, 16)
            sp.dma_start(brow[:], be.rearrange("(a e) d -> a (e d)", a=1)).then_inc(wc_in, 16)
            with sp.Fori(0, NE0 - 1) as e:
                sp.wait_ge(raw_split, 2 * e + 1)
                load_half(e, 1)
                sp.wait_ge(raw_split, 2 * e + 2)
                load_half(e + 1, 0)
            sp.wait_ge(raw_split, 2 * NE0 - 1)
            load_half(NE0 - 1, 1)

            sp.wait_ge(acc_added[0], 1 + 4 * NE0)
            sp.wait_ge(acc_added[1], 1 + 4 * NE0)
            for e in range(2):
                sp.dma_start(we_raw[e][:], We_v[e]).then_inc(e_w_in[e], 16)
            sp.wait_ge(scattered, 16 * NT)
            for e in range(2):
                sp.dma_start(xe[e][:], slots_in_v[e]).then_inc(e_x_in[e], 16)
            with sp.Fori(0, E // 2 - 1) as p:
                for i in range(2):
                    sp.wait_ge(e_wT_ps, 2 * p + i + 1)
                    sp.dma_start(we_raw[i][:], We_v[2 * p + 2 + i]).then_inc(e_w_in[i], 16)
                    sp.wait_ge(e_xT_ps, 2 * p + i + 1)
                    sp.dma_start(xe[i][:], slots_in_v[2 * p + 2 + i]).then_inc(e_x_in[i], 16)
                    sp.wait_ge(e_y, 2 * p + i + 1)
                    sp.dma_start(slots_out_v[2 * p + i], ye[i][:]).then_inc(e_stored[i], 16)
            for i in range(2):
                sp.wait_ge(e_y, E - 2 + i + 1)
                sp.dma_start(slots_out_v[E - 2 + i], ye[i][:]).then_inc(e_stored[i], 16)
            for c in range(NC):
                sp.wait_ge(d_out, c + 1)
                sp.dma_start(out_v[:, c * CT:(c + 1) * CT, :], x_res[:, c * CT:(c + 1) * CT, :]).then_inc(stored, 16)
            sp.wait_ge(stored, 16 * NC)

        @block.gpsimd
        def _(pool):
            steps = Steps(pool_steps)
            def wait_apart(s, value):
                if isinstance(value, int):
                    pool.wait_ge(s, value)
                else:
                    value = pool.to_reg(value)
                    pool.wait_ge(pool_steps, steps.value())
                    pool.wait_ge(s, value)

            steps.did(nc.gpsimd.memset(ident[:], 0.0))
            steps.did(nc.gpsimd.memset(before[:], 1.0))
            nc.gpsimd.memset(ones[:], 1.0)
            nc.gpsimd.memset(ones_r[:].bitcast(F32), 1.0)
            nc.gpsimd.memset(mhalf[:], -0.5)
            nc.gpsimd.memset(carry[:], 0.0)
            for k in range(E):
                nc.gpsimd.memset(desc[:, :, k:k + 1], float(E - k))
                steps.did(nc.gpsimd.memset(slot0[:, :, k:k + 1], float(CAP * k)))
            pool.wait_ge(pool_steps, steps.value())
            nc.gpsimd.affine_select(out=ident[:], in_=ident[:], compare_op=ALU.not_equal, fill=1.0, base=0,
                                    pattern=[[-1, P]], channel_multiplier=1)
            nc.gpsimd.affine_select(out=before[:], in_=before[:], compare_op=ALU.is_gt, fill=0.0, base=0,
                                    pattern=[[1, P]], channel_multiplier=-1).then_inc(consts_ready, 1)

            def power(n, count):
                pool.wait_ge(var_ready, count)
                nc.gpsimd.tensor_tensor(out=rstd[:, 0:n], in0=ve[:, 0:n], in1=mhalf[:, 0:n],
                                        op=ALU.pow).then_inc(rstd_ready, 1)

            def split(e, half, after_first=True):
                w = wsplit[half]
                pool.wait_ge(raw_in, 48 * (2 * e + half + 1))
                if half == 1:
                    wait_apart(down_done[1], 1 + e * (BLK // 2))
                elif after_first:
                    wait_apart(down_done[1], 1 + e * (BLK // 2) - HALFBLK // 2)
                nc.gpsimd.tensor_copy(w["g_hi"][:], raw_g[:])
                nc.gpsimd.tensor_copy(w["u_hi"][:], raw_u[:])
                nc.gpsimd.tensor_copy(w["d_hi"][:], raw_d[:]).then_inc(w_hi_ready, 1)
                pool.wait_ge(w_hi_ready, 2 * e + half + 1)
                nc.gpsimd.tensor_tensor(out=w["g_lo"][:], in0=raw_g[:], in1=w["g_hi"][:].bitcast(F32), op=ALU.subtract)
                nc.gpsimd.tensor_tensor(out=w["u_lo"][:], in0=raw_u[:], in1=w["u_hi"][:].bitcast(F32), op=ALU.subtract)
                nc.gpsimd.tensor_tensor(out=w["d_lo"][:], in0=raw_d[:], in1=w["d_hi"][:].bitcast(F32),
                                        op=ALU.subtract).then_inc(raw_split, 1)

            power(2 * CT, 1)
            nc.gpsimd.memset(acc[:], 0.0).then_inc(acc_zeroed, 1)
            pool.wait_ge(acc_zeroed, 1)
            pool.dma_start(slots_zero_v, acc[:].rearrange("p k (n d) -> p (k n) d", d=D)).then_inc(slots_zeroed, 16)
            power(2 * CT, 2)
            power(2 * CT, 3)
            split(0, 0, after_first=False)
            power(2 * CT, 4)
            with pool.Fori(0, NE0 - 1) as e:
                split(e, 1)
                split(e + 1, 0)
            split(NE0 - 1, 1)

            pool.wait_ge(slots_zeroed, 16)
            with pool.Fori(0, B) as b:
                pool.wait_ge(c_prep_act, B + HB // 2)
                pool.wait_ge(c_prep_dve, B + HB // 2)
                wait_apart(c_res, 1 + NT // B * b)
                nc.gpsimd.tensor_copy(kcur[:], k1T[:, :, bass.ts(b, KEYS)])
                nc.gpsimd.tensor_copy(vcur[:], V1[:, bass.ts(b, 2), :])
                nc.gpsimd.tensor_copy(fcur[:], flag[:, bass.ts(b, 1)])
                nc.gpsimd.tensor_copy(mcur[:], mrow[:, bass.ts(b, 1), :].rearrange("p b k -> p (b k)").bitcast(F32)).then_inc(c_cur, 1)
                with pool.Fori(0, CB) as ch:
                    c = b * CB + ch
                    power(CT, c * 3 + 5)
                    power(CT, c * 3 + 6)
                    for j in range(CT):
                        pool.wait_ge(c_rden, c * CT + j + 1)
                        nc.gpsimd.tensor_tensor(out=PC[j % 2][:], in0=PC[j % 2][:],
                                                in1=rdenF[j % 2][:].unsqueeze(2).to_broadcast([P, HEADS, KEYS]),
                                                op=ALU.mult).then_inc(c_norm, 1)
                    power(CT, c * 3 + 7)
                    wait_apart(r_slot, c + 1)
                    for j in range(CT):
                        pool.indirect_dma_start(out=slots_in, out_offset=bass.IndirectOffsetOnAxis(ap=slot_c[:, j:j + 1], axis=0),
                                                in_=xn4[:, j, :], in_offset=None, bounds_check=T - 1,
                                                oob_is_err=False).then_inc(scattered, 16)
            for i in range(2):
                pool.wait_ge(e_stored[i], 1 + 16 * (E // 2))
            pool.wait_ge(cleared, 1)
            for t in range(NT):
                pool.indirect_dma_start(out=ye_gath[:, t, :], out_offset=None, in_=slots_out,
                                        in_offset=bass.IndirectOffsetOnAxis(ap=slot_all[:, t:t + 1], axis=0),
                                        bounds_check=T - 1, oob_is_err=False).then_inc(gathered, 16)

        @block.scalar
        def _(act):
            act.dma_start(ctx_s[:], ctx_v).then_inc(ctx_in, 16)
            act.dma_start(W0s[:], W0.rearrange("(k p) e -> p k e", p=P)).then_inc(w0_in, 16)
            act.dma_start(bcol[:], b0.rearrange("(k p) -> p k", p=P), allow_slow_non_contiguous=True).then_inc(w0_in, 16)
            act.dma_start(graw[:, 0:2], g_xattn.rearrange("(a g) -> a g", a=1).partition_broadcast(P)).then_inc(small_in, 16)
            act.dma_start(graw[:, 2:4], g_ffn.rearrange("(a g) -> a g", a=1).partition_broadcast(P)).then_inc(small_in, 16)
            act.dma_start(gammac[:], gamma.rearrange("(k p) -> p k", p=P), allow_slow_non_contiguous=True).then_inc(small_in, 16)
            act.dma_start(betac[:], beta.rearrange("(k p) -> p k", p=P), allow_slow_non_contiguous=True).then_inc(small_in, 16)
            act.dma_start(wgr[:], wgate.rearrange("(k p) e -> p k e", p=P)).then_inc(small_in, 16)
            act.dma_start(mask8[:], mask.rearrange("(a b) k -> a (b k)", a=1).partition_broadcast(P)).then_inc(small_in, 16)
            act.wait_ge(small_in, 96)
            nc.scalar.activation(tg[:], graw[:], ACT.Tanh).then_inc(tg_ready, 1)

            act.wait_ge(prep_pe, 1)
            nc.scalar.copy(W0T[:].rearrange("p k d -> p (k d)"), bank[0][:]).then_inc(prep_act, 1)
            act.wait_ge(prep_pe, 2)
            nc.scalar.copy(ctxT[:, 0, :], bank[1][:, 0:AK]).then_inc(prep_act, 1)
            for i in range(2):
                act.wait_ge(prep_pe, 6 + i)
                nc.scalar.copy(V0[:, 2 * i:2 * i + 2, :].rearrange("p k d -> p (k d)"), bank[5 + i][0:KH, :]).then_inc(prep_act, 1)

            with act.Fori(0, B) as b:
                for h in range(CB):
                    for k in range(KB):
                        act.wait_ge(a_xnT_ps, 4 * b + 2 * h + k + 1)
                        nc.scalar.copy(xnT[:, h, k, :], bank[2 * h + k][:]).then_inc(a_xnT, 1)
                for h in range(CB):
                    act.wait_ge(a_nmax, 2 * b + h + 1)
                    for j in range(CT):
                        n = h * CT + j
                        nc.scalar.activation(PA[:, n, :], bank[4 + n // 2][:, n % 2 * 256:n % 2 * 256 + KEYS], ACT.Exp,
                                             bias=nmsA[:, n:n + 1], scale=D ** -0.5,
                                             accum_out=denA[:, n:n + 1]).then_inc(a_probs, 1)
                for h in range(CB):
                    act.wait_ge(a_pT_ps, 4 * b + 2 * h + 1)
                    nc.scalar.copy(PTA[:, h, 0, :], bank[2 * h][0:KH, :]).then_inc(a_pT_act, 1)
                for h in range(CB):
                    for k in range(KB):
                        act.wait_ge(a_x2T_ps, 4 * b + 2 * h + k + 1)
                        nc.scalar.copy(xT_hi[:, k, bass.ts(b * CB + h, CH)], bank[2 * h + k][:]).then_inc(xT_hi_ready, 1)

            with act.Fori(0, NE0) as e:
                for k in range(BLK):
                    act.wait_ge(gate_ps, e * BLK + k + 1)
                    act.wait_ge(hid_ready[k % 2], 1 + e * (BLK // 2) + k // 2)
                    nc.scalar.activation(silu[k % 2][:], bank[k % 2][:], ACT.Silu).then_inc(silu_ready, 1)

            for m in range(HB // 2):
                act.wait_ge(c_prep_ps, 2 * m + 1)
                nc.scalar.copy(k1T[:, 2 * m, :], bank[2 * m][:, 0:AK]).then_inc(c_prep_act, 1)
            for r in range(0, 2 * B, 2):
                act.wait_ge(c_prep_ps, HB + r + 1)
                nc.scalar.copy(V1[:, r, :], bank[4 + r][0:KH, :]).then_inc(c_prep_act, 1)
            act.wait_ge(acc_added[0], 1 + 4 * NE0)
            act.wait_ge(acc_added[1], 1 + 4 * NE0)
            with act.Fori(0, B) as b:
                with act.Fori(0, CB) as ch:
                    c = b * CB + ch
                    act.wait_ge(c_yT_ps, 1 + 2 * c)
                    nc.scalar.copy(yc[:], acc[:, :, bass.ts(c, CH)]).then_inc(c_y, 1)
                    for k in range(KB):
                        act.wait_ge(c_xnT_ps, 2 * c + k + 1)
                        nc.scalar.activation(xnTc[:, k, :], bank[k][:], ACT.Identity, bias=betac[:, k:k + 1],
                                             scale=gammac[:, k:k + 1]).then_inc(c_xnT, 1)
                    for m in range(0, HB, 2):
                        act.wait_ge(c_q_ps, HB * c + m + 1)
                        nc.scalar.mul(qT[:, m, :], bank[(7, 5, 6, 2)[m]][:], HD ** -0.5).then_inc(c_q_act, 1)

                    def exps(j):
                        act.wait_ge(c_nmax, c * CT + j + 1)
                        if j >= 2:
                            act.wait_ge(c_pT_ps, 1 + 4 * (c * CT + j - 1))
                        else:
                            act.wait_ge(c_pT_ps, 1 + 4 * c * CT)
                        for h in range(HEADS):
                            a = h // 2 % HPB
                            ins = nc.scalar.activation(PC[j % 2][:, h, :], bank[SIM[h // 4 * 2 + h % 2]][:, a * KEYS:(a + 1) * KEYS], ACT.Exp,
                                                       bias=nmC[j % 2][:, h:h + 1], accum_out=denC[j % 2][:, h:h + 1])
                        ins.then_inc(c_probs, 1)

                    exps(0)
                    for j in range(CT):
                        for g in (0, 2):
                            act.wait_ge(c_pT_ps, 1 + 4 * (c * CT + j) + g + 1)
                            nc.scalar.copy(PTC[:, 4 * g:4 * g + 4, :].rearrange("p a b -> p (a b)"),
                                           bank[0][0:KH, :]).then_inc(c_pT_act, 1)
                        if j + 1 < CT:
                            exps(j + 1)
                    for k in range(KB):
                        act.wait_ge(r_xnT_ps, 2 * c + k + 1)
                        nc.scalar.copy(xn4T[:, k, :], bank[k][:]).then_inc(r_xnT, 1)
                    act.wait_ge(r_shift, c + 1)
                    nc.scalar.activation(rt["e"][:], rt["d"][:], ACT.Exp).then_inc(r_exp, 1)

            with act.Fori(0, E // 2) as p:
                for i in range(2):
                    act.wait_ge(e_xT_ps, 2 * p + i + 1)
                    act.wait_ge(e_y_ps, 1 + 2 * p + i)
                    nc.scalar.copy(xeT[i][:].rearrange("p k s -> p (k s)"), bank[2 + i][:]).then_inc(e_xT, 1)

        @block.tensor
        def _(pe):
            start_at_one(pe, [*down_done, c_yT_ps, c_pT_ps, e_y_ps])
            mm, tr = nc.tensor.matmul, nc.tensor.transpose

            pe.wait_ge(consts_ready, 1)
            pe.wait_ge(w0_in, 32)
            for k in range(KB):
                for m in range(KB):
                    ins = tr(bank[0][:, k * D + m * P:k * D + (m + 1) * P], W0s[:, m, k * P:(k + 1) * P], ident[:])
            ins.then_inc(prep_pe, 1)
            pe.wait_ge(ctx_in, 16)
            for k in range(KB):
                for r in range(2 * B):
                    ins = tr(bank[1 + k][:, r * KH:(r + 1) * KH], ctx_s[:, r, k * P:(k + 1) * P], ident[0:KH, 0:KH])
                ins.then_inc(prep_pe, 1)
            pe.wait_ge(prep_act, 2)
            pe.wait_ge(prep_dve, 1)
            for m in range(KB):
                for k in range(KB):
                    ins = mm(bank[3 + m][:, 0:AK], W0T[:, k, m * P:(m + 1) * P], ctxT[:, k, :], start=k == 0, stop=k == KB - 1)
                ins.then_inc(prep_pe, 1)
            pe.wait_ge(prep_dve, 3)
            for i in range(2):
                for r in range(2):
                    for m in range(KB):
                        ins = tr(bank[5 + i][0:KH, r * D + m * P:r * D + (m + 1) * P],
                                 k0T[:, m, (2 * i + r) * KH:(2 * i + r + 1) * KH], ident[:])
                ins.then_inc(prep_pe, 1)
            for k in range(KB):
                for m in range(KB):
                    ins = mm(bank[1 + k][:, 0:AK], W0s[:, m, k * P:(k + 1) * P], k0T[:, m, :], start=m == 0, stop=m == KB - 1)
                ins.then_inc(prep_pe, 1)
            for m in range(KB):
                ins = mm(bank[7][0:1, 0:AK], bcol[:, m:m + 1], k0T[:, m, :], start=m == 0, stop=m == KB - 1)
            ins.then_inc(prep_pe, 1)
            pe.wait_ge(prep_act, 4)
            pe.wait_ge(prep_dve, 6)

            def transpose_chunk(src, first_bank, src_tile, signal):
                for k in range(KB):
                    for j in range(CT):
                        ins = tr(bank[first_bank + k][:, j * P:(j + 1) * P], src[:, src_tile + j, k * P:(k + 1) * P], ident[:])
                    ins.then_inc(signal, 1)

            with pe.Fori(0, B) as b:
                for h in range(CB):
                    pe.wait_ge(a_ln1, 2 * b + h + 1)
                    transpose_chunk(xnA, 2 * h, h * CT, a_xnT_ps)
                for h in range(CB):
                    pe.wait_ge(a_xnT, 4 * b + 2 * h + 2)
                    for j in range(CT):
                        n = h * CT + j
                        sco = bank[4 + n // 2][:, n % 2 * 256:n % 2 * 256 + KEYS]
                        for k in range(KB):
                            mm(sco, xnT[:, h, k, j * P:(j + 1) * P], A0[:, k, bass.ts(b, KEYS)], start=k == 0, stop=False)
                        ins = mm(sco, ones[0:1, :], r0[:, bass.ts(b, KEYS)], start=False, stop=True)
                        if j % 2:
                            ins.then_inc(a_sc_ps, 1)
                for h in range(CB):
                    pe.wait_ge(a_probs, 2 * CT * b + h * CT + CT)
                    for k in range(2):
                        for j in range(CT):
                            ins = tr(bank[2 * h + k][0:KH, j * P:(j + 1) * P], PA[:, h * CT + j, k * KH:(k + 1) * KH], ident[:])
                        ins.then_inc(a_pT_ps, 1)
                for h in range(CB):
                    pe.wait_ge(a_pT_act, 2 * b + h + 1)
                    pe.wait_ge(a_pT_dve, 2 * b + h + 1)
                    for j in range(CT):
                        n = h * CT + j
                        for k in range(2):
                            ins = mm(bank[4 + n // 2][:, n % 2 * D:(n % 2 + 1) * D], PTA[:, h, k, j * P:(j + 1) * P],
                                     V0[:, bass.ds(2 * b + k, 1), :].rearrange("p a d -> p (a d)"), start=k == 0, stop=k == 1)
                        if j % 2:
                            ins.then_inc(a_out_ps, 1)
                for h in range(CB):
                    pe.wait_ge(a_ln2, 2 * b + h + 1)
                    transpose_chunk(xnA, 2 * h, h * CT, a_x2T_ps)

            def three(pairs, ps, start, stop):
                n = 0
                for w_hi, w_lo, a_hi, a_lo in pairs:
                    for w, a in ((w_hi, a_hi), (w_hi, a_lo), (w_lo, a_hi)):
                        n += 1
                        ins = mm(ps, w, a, start=start and n == 1, stop=stop and n == 3 * len(pairs))
                return ins

            def gate_up(e, k):
                half, chunk, f = k // HALFBLK, k % HALFBLK // FB, k % FB
                w = wsplit[half]
                fs, ts = slice(f * P, (f + 1) * P), slice(chunk * CH, (chunk + 1) * CH)
                if k % HALFBLK == 0:
                    pe.wait_ge(raw_split, 2 * e + half + 1)
                pe.wait_ge(hid_ready[k % 2], 1 + e * (BLK // 2) + k // 2)
                for hi, lo, ps, signal in (("g_hi", "g_lo", bank[k % 2], gate_ps), ("u_hi", "u_lo", bank[2 + k % 2], up_ps)):
                    three([(w[hi][:, d, fs], w[lo][:, d, fs], xT_hi[:, d, ts], xT_lo[:, d, ts]) for d in range(KB)],
                          ps[:], True, True).then_inc(signal, 1)

            def down(e, k):
                half, f, u = k // HALFBLK, k % FB, k // FB
                w = wsplit[half]
                if f == 0:
                    pe.wait_ge(acc_added[u % 2], 1 + e * (UNITS // 2) + u // 2)
                ps = [bank[4 + 2 * (u % 2) + m] for m in range(KB)]
                hs = [slice(m * P, (m + 1) * P) for m in range(KB)]
                pe.wait_ge(hi_ready, e * BLK + k + 1)
                for m in range(KB):
                    mm(ps[m][:], w["d_hi"][:, f, hs[m]], hid_hi[k % 2][:], start=f == 0, stop=False)
                for m in range(KB):
                    mm(ps[m][:], w["d_lo"][:, f, hs[m]], hid_hi[k % 2][:], start=False, stop=False)
                pe.wait_ge(lo_ready, e * BLK + k + 1)
                mm(ps[0][:], w["d_hi"][:, f, hs[0]], hid_lo[k % 2][:], start=False, stop=f == FB - 1)
                ins = mm(ps[1][:], w["d_hi"][:, f, hs[1]], hid_lo[k % 2][:], start=False, stop=f == FB - 1)
                ins.then_inc(down_done[k % 2], 1)

            pe.wait_ge(xT_hi_ready, 4 * CB)
            pe.wait_ge(xT_lo_ready, 4 * CB)
            gate_up(0, 0)
            with pe.Fori(0, NE0) as e:
                for k in range(BLK):
                    if k + 1 < BLK:
                        gate_up(e, k + 1)
                    else:
                        with pe.If(e < NE0 - 1):
                            gate_up(e + 1, 0)
                    down(e, k)

            pe.wait_ge(wc_in, 64)
            for m in range(HB):
                for k in range(KB):
                    ins = mm(bank[m][:, 0:AK], Wkvs[:, k, m * P:(m + 1) * P], ctxT[:, k, :], start=k == 0, stop=k == KB - 1)
                ins.then_inc(c_prep_ps, 1)
            pe.wait_ge(acc_added[0], 1 + 4 * NE0)
            pe.wait_ge(acc_added[1], 1 + 4 * NE0)
            for r in range(2 * B):
                for k in range(KB):
                    ins = mm(bank[4 + r][0:KH, :], ctxT[:, k, r * KH:(r + 1) * KH], Wkvs[:, k, INNER:2 * INNER],
                             start=k == 0, stop=k == KB - 1)
                ins.then_inc(c_prep_ps, 1)
            pe.wait_ge(c_prep_act, 2 * B // 2 + HB // 2)
            pe.wait_ge(c_prep_dve, 2 * B // 2 + HB // 2)
            with pe.Fori(0, B) as b:
                with pe.Fori(0, CB) as ch:
                    c = b * CB + ch
                    pe.wait_ge(c_y, c + 1)
                    for j in range(CT):
                        for m in range(KB):
                            ins = tr(bank[j // 2][:, j % 2 * D + m * P:j % 2 * D + (m + 1) * P], yc[:, m, j * P:(j + 1) * P], ident[:])
                        if j % 2:
                            ins.then_inc(c_yT_ps, 1)
                    pe.wait_ge(c_ln, c + 1)
                    transpose_chunk(xnC2, 0, 0, c_xnT_ps)
                    pe.wait_ge(c_xnT, 2 * c + 2)
                    for m in range(HB):
                        for k in range(KB):
                            ins = mm(bank[(7, 5, 6, 2)[m]][:], Wqs[:, k, m * P:(m + 1) * P], xnTc[:, k, :], start=k == 0, stop=k == KB - 1)
                        ins.then_inc(c_q_ps, 1)
                    pe.wait_ge(c_q_act, 2 * c + 2)
                    pe.wait_ge(c_q_dve, 2 * c + 2)
                    pe.wait_ge(c_cur, b + 1)

                    def sim(j):
                        for a in range(HPB):
                            ks = slice(a * KEYS, (a + 1) * KEYS)
                            for s in SIM:
                                mm(bank[s][:, ks], ones_r[:], mcur[:], start=True, stop=False)
                            for i, s in enumerate(SIM):
                                h = i // 2 * 4 + 2 * a + i % 2
                                r = slice(h % 2 * HD, (h % 2 + 1) * HD)
                                ins = mm(bank[s][:, ks], qT[r, h // 2, j * P:(j + 1) * P], kcur[r, h // 2, :], start=False, stop=True)
                        ins.then_inc(c_sim_ps, 1)

                    sim(0)
                    for j in range(CT):
                        t = c * CT + j
                        if j + 1 < CT:
                            pe.wait_ge(c_probs, t + 1)
                            sim(j + 1)
                        pe.wait_ge(c_norm, t + 1)
                        for g in range(4):
                            if g >= 2:
                                pe.wait_ge(c_pT_act if g % 2 == 0 else c_pT_dve, 2 * t + 1)
                            for a in range(4):
                                n = 4 * g + a
                                ins = tr(bank[g % 2][0:KH, a * P:(a + 1) * P], PC[j % 2][:, n // 2, n % 2 * KH:(n % 2 + 1) * KH], ident[:])
                            ins.then_inc(c_pT_ps, 1)
                        pe.wait_ge(c_pT_act, 2 * t + 2)
                        pe.wait_ge(c_pT_dve, 2 * t + 2)
                        for h in range(HEADS):
                            for k in range(2):
                                ins = mm(bank[5][h % 2 * HD:(h % 2 + 1) * HD, h // 2 * P:(h // 2 + 1) * P],
                                         vcur[:, k, h * HD:(h + 1) * HD], PTC[:, 2 * h + k, :], start=k == 0, stop=k == 1)
                        ins.then_inc(c_o_ps, 1)
                        pe.wait_ge(c_o, t + 1)
                        for k in range(HB):
                            ins = mm(bank[7][:, 0:D], oT[:, k, :], Wouts[:, k, :], start=k == 0, stop=k == HB - 1)
                        ins.then_inc(c_out_ps, 1)

                    pe.wait_ge(r_ln, c + 1)
                    transpose_chunk(xn4, 0, 0, r_xnT_ps)
                    pe.wait_ge(r_xnT, 2 * c + 2)
                    for j in range(CT):
                        for k in range(KB):
                            ins = mm(bank[7][:, D + j * E:D + (j + 1) * E], xn4T[:, k, j * P:(j + 1) * P], wgr[:, k, :], start=k == 0, stop=k == KB - 1)
                    ins.then_inc(r_logit_ps, 1)
                    pe.wait_ge(r_one, c + 1)
                    one = rt["one"][:].rearrange("p j e -> p (j e)")
                    mm(bank[7][:, D + 64:D + 64 + CT * E], before[:], one, start=True, stop=True)
                    mm(bank[7][:, D + 128:D + 128 + CT * E], ones[:], one, start=True, stop=True).then_inc(r_loc_ps, 1)

            with pe.Fori(0, E // 2) as p:
                for i in range(2):
                    pe.wait_ge(e_w_in[i], 16 * (p + 1))
                    for k in range(KB):
                        for m in range(KB):
                            ins = tr(bank[i][:, k * D + m * P:k * D + (m + 1) * P], we_raw[i][:, m, k * P:(k + 1) * P], ident[:])
                    ins.then_inc(e_wT_ps, 1)
                    pe.wait_ge(e_x_in[i], 16 * (p + 1))
                    for k in range(KB):
                        for s in range(CAP // P):
                            ins = tr(bank[2 + i][:, k * CAP + s * P:k * CAP + (s + 1) * P], xe[i][:, s, k * P:(k + 1) * P], ident[:])
                    ins.then_inc(e_xT_ps, 1)
                    pe.wait_ge(e_wT, 2 * p + i + 1)
                    pe.wait_ge(e_xT, 2 * p + i + 1)
                    for s in range(CAP // P):
                        mm(bank[4 + i][:, s * D:(s + 1) * D], ones[0:1, :], brow[:, bass.ts(2 * p + i, D)], start=True, stop=False)
                        for k in range(KB):
                            ins = mm(bank[4 + i][:, s * D:(s + 1) * D], xeT[i][:, k, s * P:(s + 1) * P], weT[i][:, k, :],
                                     start=False, stop=k == KB - 1)
                    ins.then_inc(e_y_ps, 1)

        @block.vector
        def _(dve):
            start_at_one(dve, [*hid_ready, *acc_added, c_res])
            steps = Steps(dve_steps)

            def own():
                dve.wait_ge(dve_steps, steps.value())

            def wait_apart(s, value):
                if isinstance(value, int):
                    dve.wait_ge(s, value)
                else:
                    value = dve.to_reg(value)
                    dve.wait_ge(consts_ready, 1)
                    dve.wait_ge(s, value)

            def norm(srcs, dsts, count, signal=None, every=1):
                n = len(srcs)
                for i, s in enumerate(srcs):
                    ins = nc.vector.bn_stats(stats[:, i, :], s)
                steps.did(ins)
                wait_apart(dve_steps, steps.value())
                for i in range(n):
                    ins = nc.vector.bn_aggr(mv[:, i, :], stats[:, i, :])
                steps.did(ins)
                own()
                nc.vector.tensor_scalar(ve[:, 0:n], mv[:, 0:n, 1], EPS, None, ALU.add).then_inc(var_ready, 1)
                dve.wait_ge(rstd_ready, count)
                for i in range(n):
                    ins = nc.vector.tensor_scalar(dsts[i], srcs[i], mv[:, i, 0:1], rstd[:, i:i + 1], ALU.subtract, ALU.mult)
                    if signal is not None and (i + 1) % every == 0:
                        ins.then_inc(signal, 1)
                if signal is None:
                    steps.did(ins)

            def tiles(first, n):
                return [x_res[:, bass.ds(first + i, 1), :].rearrange("p a d -> p (a d)") for i in range(n)]

            dve.wait_ge(prep_pe, 3)
            nc.vector.tensor_copy(ctxT[:, 1, :], bank[2][:, 0:AK]).then_inc(prep_dve, 1)
            dve.wait_ge(w0_in, 32)
            for m in range(KB):
                dve.wait_ge(prep_pe, 4 + m)
                nc.vector.tensor_scalar(k0T[:, m, :], bank[3 + m][:, 0:AK], bcol[:, m:m + 1], None, ALU.add).then_inc(prep_dve, 1)
            for k in range(KB):
                dve.wait_ge(prep_pe, 8 + k)
                nc.vector.tensor_copy(A0[:, k, :], bank[1 + k][:, 0:AK]).then_inc(prep_dve, 1)
            dve.wait_ge(prep_pe, 10)
            nc.vector.tensor_copy(r0[:], bank[7][0:1, 0:AK]).then_inc(prep_dve, 1)
            dve.wait_ge(small_in, 96)
            steps.did(nc.vector.tensor_copy(maskf[:], mask8[:]))
            own()
            nc.vector.tensor_scalar(mrow[:], maskf[0:1, :].rearrange("p (b k) -> p b k", b=B), -MASKED, MASKED, ALU.mult, ALU.add)
            steps.did(nc.vector.reduce_max(anyv[:], maskf[:].rearrange("p (b k) -> p b k", b=B), AX.X))
            own()
            steps.did(nc.vector.reciprocal(ranyv[:], anyv[:]))
            own()
            steps.did(nc.vector.tensor_tensor(out=flag[:], in0=anyv[:], in1=ranyv[:], op=ALU.mult))
            dve.wait_ge(tg_ready, 1)

            with dve.Fori(0, B) as b:
                steps.enter(b, 9)
                wait_apart(x_in, 16 * CB * (b + 1))
                xs = tiles(b * 2 * CT, 2 * CT)
                norm(xs, [xnA[:, n, :] for n in range(2 * CT)], 2 * b + 1, a_ln1, CT)
                for h in range(CB):
                    for i in range(2):
                        dve.wait_ge(a_sc_ps, 4 * b + 2 * h + i + 1)
                        n = h * CT + 2 * i
                        ins = nc.vector.reduce_max(nmA[:, n:n + 2], bank[4 + n // 2][:].rearrange("p (a k) -> p a k", a=2)[:, :, 0:KEYS],
                                                   AX.X, negate=True)
                    steps.did(ins)
                    own()
                    nc.vector.tensor_scalar(nmsA[:, h * CT:(h + 1) * CT], nmA[:, h * CT:(h + 1) * CT], D ** -0.5, None,
                                            ALU.mult).then_inc(a_nmax, 1)
                for h in range(CB):
                    dve.wait_ge(a_pT_ps, 4 * b + 2 * h + 2)
                    nc.vector.tensor_copy(PTA[:, h, 1, :], bank[2 * h + 1][0:KH, :]).then_inc(a_pT_dve, 1)
                dve.wait_ge(a_probs, 2 * CT * (b + 1))
                steps.did(nc.vector.reciprocal(rdenA[:], denA[:]))
                own()
                steps.did(nc.vector.tensor_scalar(coefA[:], rdenA[:], tg[:, 0:1], None, ALU.mult))
                own()
                for n in range(2 * CT):
                    dve.wait_ge(a_out_ps, 4 * b + n // 2 + 1)
                    ins = nc.vector.scalar_tensor_tensor(out=xs[n], in0=bank[4 + n // 2][:, n % 2 * D:(n % 2 + 1) * D],
                                                         scalar=coefA[:, n:n + 1], in1=xs[n], op0=ALU.mult, op1=ALU.add)
                steps.did(ins)
                wait_apart(dve_steps, steps.value())
                norm(xs, [xnA[:, n, :] for n in range(2 * CT)], 2 * b + 2, a_ln2, CT)
                for h in range(CB):
                    for k in range(KB):
                        dve.wait_ge(xT_hi_ready, 4 * b + 2 * h + k + 1)
                        ts = bass.ts(b * CB + h, CH)
                        ins = nc.vector.tensor_tensor(out=xT_lo[:, k, ts], in0=bank[2 * h + k][:], in1=xT_hi[:, k, ts].bitcast(F32),
                                                      op=ALU.subtract)
                        ins.then_inc(xT_lo_ready, 1)
                steps.leave(B)

            dve.wait_ge(acc_zeroed, 1)
            dve.wait_ge(slots_zeroed, 16)

            def add_up(e, u):
                dve.wait_ge(down_done[1], 1 + e * (BLK // 2) + (u + 1) * FB // 2)
                ts = slice(u % NC * CH, (u % NC + 1) * CH)
                for m in range(KB):
                    ins = nc.vector.tensor_tensor(out=acc[:, m, ts], in0=bank[4 + 2 * (u % 2) + m][:], in1=acc[:, m, ts], op=ALU.add)
                ins.then_inc(acc_added[u % 2], 1)

            with dve.Fori(0, NE0) as e:
                for k in range(BLK):
                    i = k % 2
                    done = e * (BLK // 2) + k // 2
                    dve.wait_ge(up_ps, e * BLK + k + 1)
                    dve.wait_ge(silu_ready, e * BLK + k + 1)
                    nc.vector.tensor_tensor(out=hid[i][:], in0=bank[2 + i][:], in1=silu[i][:], op=ALU.mult).then_inc(hid_ready[i], 1)
                    dve.wait_ge(hid_ready[i], 1 + done + 1)
                    dve.wait_ge(down_done[i], 1 + done)
                    nc.vector.tensor_copy(hid_hi[i][:], hid[i][:]).then_inc(hi_ready, 1)
                    dve.wait_ge(hi_ready, e * BLK + k + 1)
                    nc.vector.tensor_tensor(out=hid_lo[i][:], in0=hid[i][:], in1=hid_hi[i][:].bitcast(F32),
                                            op=ALU.subtract).then_inc(lo_ready, 1)
                    if k and k % FB == 0:
                        add_up(e, k // FB - 1)
                add_up(e, UNITS - 1)

            for m in range(HB // 2):
                dve.wait_ge(c_prep_ps, 2 * m + 2)
                nc.vector.tensor_copy(k1T[:, 2 * m + 1, :], bank[2 * m + 1][:, 0:AK]).then_inc(c_prep_dve, 1)
            for r in range(1, 2 * B, 2):
                dve.wait_ge(c_prep_ps, HB + r + 1)
                nc.vector.tensor_copy(V1[:, r, :], bank[4 + r][0:KH, :]).then_inc(c_prep_dve, 1)
            steps.did(nc.vector.memset(ye_gath[:], 0.0))
            with dve.Fori(0, B) as b:
                steps.enter(b, CB * PER_CHUNK)
                with dve.Fori(0, CB) as ch:
                    outer = steps.start
                    steps.base, steps.n = (b * CB + ch) * PER_CHUNK + outer, 0
                    c = b * CB + ch
                    xs = tiles(c * CT, CT)
                    for j in range(CT):
                        dve.wait_ge(c_yT_ps, 1 + 2 * c + j // 2 + 1)
                        ins = nc.vector.scalar_tensor_tensor(out=xs[j], in0=bank[j // 2][:, j % 2 * D:(j % 2 + 1) * D],
                                                             scalar=tg[:, 2:3], in1=xs[j], op0=ALU.mult, op1=ALU.add)
                    steps.did(ins)
                    wait_apart(dve_steps, steps.value())
                    norm(xs, [xnC[:, j, :] for j in range(CT)], 3 * c + 5)
                    wait_apart(dve_steps, steps.value())
                    norm([xnC[:, j, :] for j in range(CT)], [xnC2[:, j, :] for j in range(CT)], 3 * c + 6, c_ln, CT)
                    for m in range(1, HB, 2):
                        dve.wait_ge(c_q_ps, HB * c + m + 1)
                        nc.vector.tensor_scalar(qT[:, m, :], bank[(7, 5, 6, 2)[m]][:], HD ** -0.5, None, ALU.mult).then_inc(c_q_dve, 1)

                    def maxes(j):
                        dve.wait_ge(c_sim_ps, c * CT + j + 1)
                        for i, s in enumerate(SIM):
                            h = i // 2 * 4 + i % 2
                            ins = nc.vector.reduce_max(nmC[j % 2][:, h:h + 3:2],
                                                       bank[s][:, 0:HPB * KEYS].rearrange("p (a k) -> p a k", a=HPB), AX.X, negate=True)
                        ins.then_inc(c_nmax, 1)

                    def dens(j):
                        dve.wait_ge(c_probs, c * CT + j + 1)
                        dve.wait_ge(c_cur, b + 1)
                        steps.did(nc.vector.reciprocal(rdenC[j % 2][:], denC[j % 2][:]))
                        own()
                        nc.vector.tensor_scalar(rdenF[j % 2][:], rdenC[j % 2][:], fcur[:], None, ALU.mult).then_inc(c_rden, 1)

                    maxes(0)
                    dens(0)
                    for j in range(CT):
                        t = c * CT + j
                        if j + 1 < CT:
                            maxes(j + 1)
                        for g in (1, 3):
                            dve.wait_ge(c_pT_ps, 1 + 4 * t + g + 1)
                            nc.vector.tensor_copy(PTC[:, 4 * g:4 * g + 4, :].rearrange("p a b -> p (a b)"),
                                                  bank[1][0:KH, :]).then_inc(c_pT_dve, 1)
                        dve.wait_ge(c_o_ps, t + 1)
                        nc.vector.tensor_copy(oT[:].rearrange("p k t -> p (k t)"), bank[5][:]).then_inc(c_o, 1)
                        if j + 1 < CT:
                            dens(j + 1)
                        dve.wait_ge(c_out_ps, t + 1)
                        nc.vector.scalar_tensor_tensor(out=xs[j], in0=bank[7][:, 0:D], scalar=tg[:, 1:2], in1=xs[j],
                                                       op0=ALU.mult, op1=ALU.add).then_inc(c_res, 1)
                    with dve.If(c > 0):
                        wait_apart(scattered, 16 * CT * c)
                    wait_apart(c_res, 1 + (c + 1) * CT)
                    norm(xs, [xn4[:, j, :] for j in range(CT)], 3 * c + 7, r_ln, CT)

                    def bc(v):
                        return v.unsqueeze(2).to_broadcast([P, CT, E])

                    dve.wait_ge(r_logit_ps, c + 1)
                    logits = bank[7][:, D:D + CT * E].rearrange("p (j e) -> p j e", j=CT)
                    steps.did(nc.vector.reduce_max(rs["max"][:], logits, AX.X))
                    own()
                    nc.vector.tensor_tensor(out=rt["d"][:], in0=logits, in1=bc(rs["max"][:]), op=ALU.subtract).then_inc(r_shift, 1)
                    dve.wait_ge(r_exp, c + 1)
                    steps.did(nc.vector.reduce_sum(rs["sum"][:], rt["e"][:], AX.X))
                    own()
                    steps.did(nc.vector.reciprocal(rs["rsum"][:], rs["sum"][:]))
                    own()
                    steps.did(nc.vector.tensor_tensor(out=rt["p"][:], in0=rt["e"][:], in1=bc(rs["rsum"][:]), op=ALU.mult))
                    own()
                    steps.did(nc.vector.reduce_max(rs["best"][:], rt["p"][:], AX.X))
                    own()
                    steps.did(nc.vector.tensor_tensor(out=rt["top"][:], in0=rt["p"][:], in1=bc(rs["best"][:]), op=ALU.is_equal))
                    own()
                    steps.did(nc.vector.tensor_tensor(out=rt["score"][:], in0=rt["top"][:], in1=desc[:], op=ALU.mult))
                    own()
                    steps.did(nc.vector.reduce_max(rs["first"][:], rt["score"][:], AX.X))
                    own()
                    nc.vector.tensor_tensor(out=rt["one"][:], in0=rt["score"][:], in1=bc(rs["first"][:]),
                                            op=ALU.is_equal).then_inc(r_one, 1)
                    dve.wait_ge(r_loc_ps, c + 1)
                    inside = bank[7][:, D + 64:D + 64 + CT * E].rearrange("p (j e) -> p j e", j=CT)
                    totals = bank[7][:, D + 128:D + 128 + CT * E].rearrange("p (j e) -> p j e", j=CT)
                    for j in range(CT):
                        nc.vector.tensor_copy(rt["pre"][:, j, :], carry[:])
                        steps.did(nc.vector.tensor_tensor(out=carry[:], in0=totals[:, j, :], in1=carry[:], op=ALU.add))
                        own()
                    steps.did(nc.vector.tensor_tensor(out=rt["loc"][:], in0=inside, in1=rt["pre"][:], op=ALU.add))
                    own()
                    nc.vector.tensor_tensor(out=rt["m1"][:], in0=rt["one"][:], in1=rt["loc"][:], op=ALU.mult)
                    steps.did(nc.vector.tensor_tensor(out=rt["m2"][:], in0=rt["one"][:], in1=slot0[:], op=ALU.mult))
                    own()
                    nc.vector.reduce_sum(rs["loc"][:], rt["m1"][:], AX.X)
                    steps.did(nc.vector.reduce_sum(rs["slot"][:], rt["m2"][:], AX.X))
                    own()
                    nc.vector.tensor_scalar(rs["keep"][:], rs["loc"][:], float(CAP), None, ALU.is_lt)
                    nc.vector.tensor_scalar(rs["far"][:], rs["loc"][:], float(CAP), float(DROPPED), ALU.is_ge, ALU.mult)
                    steps.did(nc.vector.tensor_tensor(out=rs["slot"][:], in0=rs["slot"][:], in1=rs["loc"][:], op=ALU.add))
                    own()
                    g_ts = bass.ts(c, CT)
                    nc.vector.tensor_tensor(out=gate_all[:, g_ts], in0=rs["best"][:], in1=rs["keep"][:], op=ALU.mult)
                    nc.vector.tensor_tensor(out=slot_c[:], in0=rs["slot"][:], in1=rs["far"][:], op=ALU.add).then_inc(r_slot, 1)
                    steps.did(nc.vector.tensor_tensor(out=slot_all[:, g_ts], in0=rs["slot"][:], in1=rs["far"][:], op=ALU.add))
                    own()
                    assert steps.n == PER_CHUNK, steps.n
                steps.base, steps.n = outer + NC * PER_CHUNK, 0

            own()
            nc.vector.tensor_scalar(coefD[:], gate_all[:], tg[:, 3:4], None, ALU.mult).then_inc(cleared, 1)
            with dve.Fori(0, E // 2) as p:
                for i in range(2):
                    dve.wait_ge(e_wT_ps, 2 * p + i + 1)
                    nc.vector.tensor_copy(weT[i][:].rearrange("p k s -> p (k s)"), bank[i][:]).then_inc(e_wT, 1)
                    dve.wait_ge(e_y_ps, 1 + 2 * p + i + 1)
                    dve.wait_ge(e_stored[i], 1 + 16 * p)
                    nc.vector.tensor_copy(ye[i][:].rearrange("p k s -> p (k s)"), bank[4 + i][:]).then_inc(e_y, 1)
            dve.wait_ge(cleared, 1)
            dve.wait_ge(gathered, 16 * NT)
            for t in range(NT):
                ins = nc.vector.scalar_tensor_tensor(out=x_res[:, t, :], in0=ye_gath[:, t, :], scalar=coefD[:, t:t + 1],
                                                     in1=x_res[:, t, :], op0=ALU.mult, op1=ALU.add)
                if t % CT == CT - 1:
                    ins.then_inc(d_out, 1)


PER_CHUNK = 29


_INS = ['x', 'ctx_1024', 'mask_BxS2_bk0', 'g_xattn', 'g_ffn', 'L0_xattn_W', 'L0_xattn_b', 'L0_ffn_Wg', 'L0_ffn_Wu', 'L0_ffn_Wd',
        'L1_xattn_ln_gamma', 'L1_xattn_ln_beta', 'L1_xattn_Wq', 'L1_xattn_Wkv', 'L1_xattn_Wout', 'L1_ffn_wg', 'L1_ffn_W', 'L1_ffn_b']
_OUTS = [((2, 1024, 256), 'float32')]


def kernel(**inputs):
    import numpy as _np
    import concourse.bacc as _bacc
    from concourse import mybir as _mybir
    from concourse.bass_utils import run_bass_kernel_spmd as _run

    nc = _bacc.Bacc("TRN2", target_bir_lowering=False, num_devices=1)
    arrays, args = {}, []
    for name in _INS:
        a = _np.ascontiguousarray(inputs[name])
        arrays[f"in_{name}_dram"] = a
        args.append(nc.dram_tensor(f"in_{name}_dram", a.shape, _mybir.dt.from_np(a.dtype), kind="ExternalInput").ap())
    for i, (shape, dtype) in enumerate(_OUTS):
        dt = _mybir.dt.from_np(_np.dtype(dtype))
        args.append(nc.dram_tensor(f"out_{i}_dram", shape, dt, kind="ExternalOutput").ap())
    flamingo_kernel(nc, *args)
    r = _run(nc, [arrays], core_ids=[0])
    got = tuple(r.results[0][f"out_{i}_dram"] for i in range(len(_OUTS)))
    return got[0]
```

```python
import numpy as np
import concourse.bass as bass
from concourse import mybir
from contextlib import ExitStack

F32 = mybir.dt.float32
F32R = mybir.dt.float32r
U32 = mybir.dt.uint32
U8 = mybir.dt.uint8
ALU = mybir.AluOpType
ACT = mybir.ActivationFunctionType
AX = mybir.AxisListType

P = 128
EPS = 1e-5
MASKED = -1e30


class Arena:

    def __init__(self, nc, start, end):
        self.nc, self.at, self.end = nc, start, end

    def take(self, name, shape, dt, size=4):
        n = size
        for d in shape[1:]:
            n *= d
        t = self.nc.alloc_sbuf_tensor_at(name, shape, dt, offset=self.at)
        self.at += -(-n // 32) * 32
        assert self.at <= self.end, (name, self.at, self.end)
        return t


class Steps:

    def __init__(self, sem):
        self.sem, self.base, self.n = sem, 0, 0

    def did(self, ins):
        ins.then_inc(self.sem, 1)
        self.n += 1

    def value(self):
        return self.base + self.n

    def round(self, trip, per_trip):
        self.base, self.n, self.per_trip = trip * per_trip, 0, per_trip

    def round_over(self):
        assert self.n == self.per_trip, (self.n, self.per_trip)

    def enter(self, trip, per_trip):
        self.start = self.base + self.n
        self.per_trip = per_trip
        self.base, self.n = trip * per_trip + self.start, 0

    def leave(self, trips):
        assert self.n == self.per_trip, (self.n, self.per_trip)
        self.base, self.n = self.start + trips * self.per_trip, 0


def wait_if(eng, sem, value):
    if not isinstance(value, int) or value > 0:
        eng.wait_ge(sem, value)


def flamingo_kernel(nc, x, ctx, mask, g_xattn, g_ffn, W0, b0, Wg, Wu, Wd, gamma, beta, Wq, Wkv, Wout, wgate, We, be, out):
    B, S, D = x.shape
    KEYS = ctx.shape[1]
    KH = KEYS // 2
    NE0, _, F = Wg.shape
    INNER = Wq.shape[1]
    HD = 64
    HEADS = INNER // HD
    E = wgate.shape[1]
    T = B * S
    NT = T // P
    CT = 4
    CH = CT * P
    NC = NT // CT
    CB = S // CH
    CAP = T // E
    KB = D // P
    HF = F // 2
    FB = HF // P
    HB = INNER // P
    AK = B * KEYS
    HH = HEADS // 2
    HPB = 2
    SIM = (2, 3, 4, 6)
    ROUTE_T = (5, 7)
    V_PS = (6, 7, 0, 1)
    DROPPED = 4 * T
    assert KH * 2 == KEYS and KB == 2 and CB == 2 and CAP == 2 * P and HB == 4

    x_v = x.rearrange("b (t p) d -> p (b t) d", p=P)
    out_v = out.rearrange("b (t p) d -> p (b t) d", p=P)
    ctx_v = ctx.rearrange("b (k r) d -> r (b k) d", r=KH)
    Wg_v = Wg.rearrange("e (k p) f -> e p k f", p=P)
    Wu_v = Wu.rearrange("e (k p) f -> e p k f", p=P)
    Wd_v = Wd.rearrange("e (k p) d -> e p k d", p=P)
    We_v = We.rearrange("e (k p) h -> e p k h", p=P)
    slots_in = nc.dram_tensor("slots_in", [T, D], F32).ap()
    slots_out = nc.dram_tensor("slots_out", [T, D], F32).ap()
    slots_in_v = slots_in.rearrange("(e k p) d -> e p k d", p=P, k=CAP // P)
    slots_out_v = slots_out.rearrange("(e k p) d -> e p k d", p=P, k=CAP // P)
    slots_zero_v = slots_in.rearrange("(n p) d -> p n d", p=P)

    with ExitStack() as stack:
        def sem(name):
            return stack.enter_context(nc.semaphore(name))

        base = -(-nc.sbuf_base // 32) * 32
        end = nc.sbuf_usable_end // 32 * 32
        keep = Arena(nc, base, end)
        x_res = keep.take("x_res", [P, NT, D], F32)
        ident = keep.take("ident", [P, P], F32)
        before = keep.take("before", [P, P], F32)
        ones = keep.take("ones", [P, P], F32)
        ones_r = keep.take("ones_r", [1, P], F32R)
        A0 = keep.take("A0", [P, KB, AK], F32)
        r0 = keep.take("r0", [1, AK], F32)
        V0 = keep.take("V0", [KH, 2 * B, D], F32)
        ctxT = keep.take("ctxT", [P, KB, AK], F32)
        graw = keep.take("graw", [P, 4], F32)
        tg = keep.take("tg", [P, 4], F32)
        mhalf = keep.take("mhalf", [P, 8], F32)
        gammac = keep.take("gammac", [P, KB], F32)
        betac = keep.take("betac", [P, KB], F32)
        LN_A, LN_FRONT, LN_FRONT2, LN_ROUTE = range(4)
        stats = [keep.take(f"stats{i}", [P, 8, 6], F32) for i in range(4)]
        mv = [keep.take(f"mv{i}", [P, 8, 2], F32) for i in range(4)]
        ve = [keep.take(f"ve{i}", [P, 8], F32) for i in range(4)]
        rstd = [keep.take(f"rstd{i}", [P, 8], F32) for i in range(4)]
        wgr = keep.take("wgr", [P, KB, E], F32)
        mask8 = keep.take("mask8", [P, AK], U8, size=1)
        maskf = keep.take("maskf", [P, AK], F32)
        mrow = keep.take("mrow", [1, B, KEYS], F32R)
        anyv = keep.take("anyv", [P, B], F32)
        ranyv = keep.take("ranyv", [P, B], F32)
        flag = keep.take("flag", [P, B], F32)
        desc = keep.take("desc", [P, CT, E], F32)
        slot0 = keep.take("slot0", [P, CT, E], F32)
        gate_all = keep.take("gate_all", [P, NT], F32)
        slot_all = keep.take("slot_all", [P, NT], U32)
        carry = keep.take("carry", [P, E], F32)

        sa = Arena(nc, keep.at, end)
        W0s = sa.take("W0s", [P, KB, D], F32)
        W0T = sa.take("W0T", [P, KB, D], F32)
        bcol = sa.take("bcol", [P, KB], F32)
        ctx_s = sa.take("ctx_s", [KH, 2 * B, D], F32)
        k0T = sa.take("k0T", [P, KB, AK], F32)
        xnA = sa.take("xnA", [P, 2 * CT, D], F32)
        xnT = sa.take("xnT", [P, CB, KB, CH], F32)
        PA = sa.take("PA", [P, 2 * CT, KEYS], F32)
        PTA = sa.take("PTA", [KH, CB, 2, CH], F32)
        nmA = sa.take("nmA", [P, 2 * CT], F32)
        nmsA = sa.take("nmsA", [P, 2 * CT], F32)
        denA = sa.take("denA", [P, 2 * CT], F32)
        rdenA = sa.take("rdenA", [P, 2 * CT], F32)
        coefA = sa.take("coefA", [P, 2 * CT], F32)

        sc = Arena(nc, keep.at, sa.at)
        Wkvs = sc.take("Wkvs", [P, KB, 2 * INNER], F32)
        Wqs = sc.take("Wqs", [P, KB, INNER], F32)
        Wouts = sc.take("Wouts", [P, HB, D], F32)
        brow = sc.take("brow", [1, E * D], F32)
        k1T = sc.take("k1T", [P, HB, AK], F32)

        sb = Arena(nc, sa.at, end)
        acc = sb.take("acc", [P, KB, T], F32)
        xT_hi = sb.take("xT_hi", [P, KB, T], F32R)
        xT_lo = sb.take("xT_lo", [P, KB, T], F32R)
        raw_g = sb.take("raw_g", [P, KB, HF], F32)
        raw_u = sb.take("raw_u", [P, KB, HF], F32)
        raw_d = sb.take("raw_d", [P, FB, D], F32)
        wsplit = [{k: sb.take(f"w_{k}{i}", [P, FB, D] if k[0] == "d" else [P, KB, HF], F32R)
                   for k in ("g_hi", "g_lo", "u_hi", "u_lo", "d_hi", "d_lo")} for i in range(2)]
        silu = [sb.take(f"silu{i}", [P, CH], F32) for i in range(2)]
        hid = [sb.take(f"hid{i}", [P, CH], F32) for i in range(2)]
        hid_hi = [sb.take(f"hid_hi{i}", [P, CH], F32R) for i in range(2)]
        hid_lo = [sb.take(f"hid_lo{i}", [P, CH], F32R) for i in range(2)]

        sd = Arena(nc, sa.at + 4 * KB * T, end)
        V1 = sd.take("V1", [KH, 2 * B, INNER], F32)
        yc = sd.take("yc", [P, KB, CH], F32)
        xnC = sd.take("xnC", [P, CT, D], F32)
        xnC2 = sd.take("xnC2", [P, CT, D], F32)
        xnTc = sd.take("xnTc", [P, KB, CH], F32)
        qT = sd.take("qT", [P, HB, CH], F32)
        kcur = sd.take("kcur", [P, HB, KEYS], F32)
        vcur = sd.take("vcur", [KH, 2, INNER], F32)
        PC = [sd.take(f"PC{i}", [P, HEADS, KEYS], F32) for i in range(2)]
        PTC = sd.take("PTC", [KH, 2 * HEADS, P], F32)
        nmC = [sd.take(f"nmC{i}", [P, HEADS], F32) for i in range(2)]
        denC = [sd.take(f"denC{i}", [P, HEADS], F32) for i in range(2)]
        rdenC = [sd.take(f"rdenC{i}", [P, HEADS], F32) for i in range(2)]
        oT = sd.take("oT", [P, HB, P], F32)
        xn4 = sd.take("xn4", [P, CT, D], F32)
        xn4T = sd.take("xn4T", [P, KB, CH], F32)
        rt = {k: sd.take(f"rt_{k}", [P, CT, E], F32) for k in
              ("d", "e", "p", "top", "score", "one", "pre", "loc", "m1", "m2")}
        rs = {k: sd.take(f"rs_{k}", [P, CT], F32) for k in
              ("max", "sum", "rsum", "best", "loc", "first", "keep", "slot", "far")}
        places = sd.take("places", [P, 2, CT, E], F32)
        slot_c = sd.take("slot_c", [P, CT], U32)
        warm = sd.take("warm", [P, 1], F32)
        ye_gath = sd.take("ye_gath", [P, NT, D], F32)
        coefD = sd.take("coefD", [P, NT], F32)
        we_raw = [sd.take(f"we_raw{i}", [P, KB, D], F32) for i in range(2)]
        weT = [sd.take(f"weT{i}", [P, KB, D], F32) for i in range(2)]
        xe = [sd.take(f"xe{i}", [P, CAP // P, D], F32) for i in range(2)]
        xeT = [sd.take(f"xeT{i}", [P, KB, CAP], F32) for i in range(2)]
        ye = [sd.take(f"ye{i}", [P, CAP // P, D], F32) for i in range(2)]

        bank = [stack.enter_context(nc.psum_tensor(f"bank{i}", [P, 512], F32)) for i in range(8)]

        x_in, ctx_in, w0_in, small_in, wc_in = (sem(n) for n in ("x_in", "ctx_in", "w0_in", "small_in", "wc_in"))
        consts_ready, acc_zeroed, cleared = sem("consts_ready"), sem("acc_zeroed"), sem("cleared")
        tg_ready = sem("tg_ready")
        pool_steps, dve_steps = sem("pool_steps"), sem("dve_steps")
        prep_pe, prep_act, prep_dve = sem("prep_pe"), sem("prep_act"), sem("prep_dve")
        var_ready = [sem(f"var_ready{i}") for i in range(4)]
        rstd_ready = [sem(f"rstd_ready{i}") for i in range(4)]
        front_steps, ln4_steps, route_steps = sem("front_steps"), sem("ln4_steps"), sem("route_steps")
        a_ln1, a_xnT_ps, a_xnT, a_sc_ps, a_nmax, a_probs, a_pT_ps, a_pT_act, a_pT_dve, a_out_ps, a_ln2, a_x2T_ps = (
            sem(n) for n in ("a_ln1", "a_xnT_ps", "a_xnT", "a_sc_ps", "a_nmax", "a_probs", "a_pT_ps", "a_pT_act",
                             "a_pT_dve", "a_out_ps", "a_ln2", "a_x2T_ps"))
        xT_hi_ready, xT_lo_ready = sem("xT_hi_ready"), sem("xT_lo_ready")
        raw_in, raw_split, w_hi_ready = (sem(n) for n in ("raw_in", "raw_split", "w_hi_ready"))
        gate_ps, up_ps, silu_ready, hi_ready, lo_ready = (
            sem(n) for n in ("gate_ps", "up_ps", "silu_ready", "hi_ready", "lo_ready"))
        hid_ready = [sem(f"hid_ready{i}") for i in range(2)]
        down_done = [sem(f"down_done{i}") for i in range(2)]
        acc_added = [sem(f"acc_added{i}") for i in range(2)]
        c_prep_ps, c_prep_act, c_prep_dve = sem("c_prep_ps"), sem("c_prep_act"), sem("c_prep_dve")
        c_yT_ps, c_ln, c_xnT_ps, c_xnT, c_q_ps, c_q_act, c_q_dve, c_x2 = (
            sem(n) for n in ("c_yT_ps", "c_ln", "c_xnT_ps", "c_xnT", "c_q_ps", "c_q_act", "c_q_dve", "c_x2"))
        y_in, kcur_in, vcur_in = sem("y_in"), sem("kcur_in"), sem("vcur_in")
        c_sim_ps, c_nmax, c_probs, c_rden, c_norm, c_pT_ps, c_pT_act, c_pT_dve, c_o_ps, c_o, c_out_ps, c_res = (
            sem(n) for n in ("c_sim_ps", "c_nmax", "c_probs", "c_rden", "c_norm", "c_pT_ps", "c_pT_act", "c_pT_dve",
                             "c_o_ps", "c_o", "c_out_ps", "c_res"))
        r_ln, r_xnT_ps, r_xnT, r_logit_ps, r_shift, r_exp, r_one, r_loc_ps, r_loc_read, r_slot, scattered = (
            sem(n) for n in ("r_ln", "r_xnT_ps", "r_xnT", "r_logit_ps", "r_shift", "r_exp", "r_one", "r_loc_ps",
                             "r_loc_read", "r_slot", "scattered"))
        e_w_in = [sem(f"e_w_in{i}") for i in range(2)]
        e_x_in = [sem(f"e_x_in{i}") for i in range(2)]
        e_stored = [sem(f"e_stored{i}") for i in range(2)]
        e_wT_ps, e_wT, e_xT_ps, e_xT, e_y_ps, e_y = (
            sem(n) for n in ("e_wT_ps", "e_wT", "e_xT_ps", "e_xT", "e_y_ps", "e_y"))
        gathered, d_out, stored = sem("gathered"), sem("d_out"), sem("stored")

        block = stack.enter_context(nc.Block())
        BLK = 2 * NC * FB
        HALFBLK = NC * FB
        UNITS = 2 * NC
        ZEROED = 16

        def batch_of(chunk):
            return chunk // CB

        def start_at_one(eng, sems):
            for s in sems:
                eng.sem_inc(s, 1)

        @block.sync
        def _(sp):
            start_at_one(sp, e_stored)
            for h in range(CB):
                sp.dma_start(x_res[:, h * CT:(h + 1) * CT, :], x_v[:, h * CT:(h + 1) * CT, :]).then_inc(x_in, 16)
            sp.wait_ge(x_in, 16 * CB)
            for h in range(CB, 2 * CB):
                sp.dma_start(x_res[:, h * CT:(h + 1) * CT, :], x_v[:, h * CT:(h + 1) * CT, :]).then_inc(x_in, 16)

            def load_half(e, half):
                f = slice(half * HF, (half + 1) * HF)
                sp.dma_start(raw_g[:], Wg_v[e, :, :, f]).then_inc(raw_in, 16)
                sp.dma_start(raw_u[:], Wu_v[e, :, :, f]).then_inc(raw_in, 16)
                sp.dma_start(raw_d[:], Wd_v[e, :, half * FB:(half + 1) * FB, :]).then_inc(raw_in, 16)

            load_half(0, 0)
            sp.wait_ge(xT_hi_ready, 4 * CB)
            sp.wait_ge(xT_lo_ready, 4 * CB)
            sp.dma_start(Wkvs[:], Wkv.rearrange("(k p) n -> p k n", p=P)).then_inc(wc_in, 16)
            sp.dma_start(Wqs[:], Wq.rearrange("(k p) n -> p k n", p=P)).then_inc(wc_in, 16)
            sp.dma_start(Wouts[:], Wout.rearrange("(k p) n -> p k n", p=P)).then_inc(wc_in, 16)
            sp.dma_start(brow[:], be.rearrange("(a e) d -> a (e d)", a=1)).then_inc(wc_in, 16)
            with sp.Fori(0, NE0 - 1) as e:
                sp.wait_ge(raw_split, 2 * e + 1)
                load_half(e, 1)
                sp.wait_ge(raw_split, 2 * e + 2)
                load_half(e + 1, 0)
            sp.wait_ge(raw_split, 2 * NE0 - 1)
            load_half(NE0 - 1, 1)

            sp.wait_ge(acc_added[0], 1 + 4 * NE0)
            sp.wait_ge(acc_added[1], 1 + 4 * NE0)
            for e in range(2):
                sp.dma_start(we_raw[e][:], We_v[e]).then_inc(e_w_in[e], 16)

            def expert_sums(f):
                if not isinstance(f, int) or f > 1:
                    sp.wait_ge(c_yT_ps, 2 * f)
                sp.dma_start(yc[:], acc[:, :, bass.ts(f, CH)]).then_inc(y_in, 16)

            def keys_and_values(chunk):
                b = batch_of(chunk)
                wait_if(sp, c_sim_ps, 2 * CT * chunk)
                sp.dma_start(kcur[:], k1T[:, :, bass.ts(b, KEYS)]).then_inc(kcur_in, 16)
                wait_if(sp, c_o_ps, CT * chunk)
                sp.dma_start(vcur[:], V1[:, bass.ts(b, 2), :]).then_inc(vcur_in, 16)

            expert_sums(1)
            sp.wait_ge(c_prep_act, B + HB // 2)
            sp.wait_ge(c_prep_dve, B + HB // 2)
            keys_and_values(0)
            with sp.Fori(1, NC - 1) as c:
                expert_sums(c + 1)
                keys_and_values(c)
            keys_and_values(NC - 1)

            sp.wait_ge(scattered, ZEROED + 16 * NT)
            for e in range(2):
                sp.dma_start(xe[e][:], slots_in_v[e]).then_inc(e_x_in[e], 16)
            with sp.Fori(0, E // 2 - 1) as p:
                for i in range(2):
                    sp.wait_ge(e_wT_ps, 2 * p + i + 1)
                    sp.dma_start(we_raw[i][:], We_v[2 * p + 2 + i]).then_inc(e_w_in[i], 16)
                    sp.wait_ge(e_xT_ps, 2 * p + i + 1)
                    sp.dma_start(xe[i][:], slots_in_v[2 * p + 2 + i]).then_inc(e_x_in[i], 16)
                    sp.wait_ge(e_y, 2 * p + i + 1)
                    sp.dma_start(slots_out_v[2 * p + i], ye[i][:]).then_inc(e_stored[i], 16)
            for i in range(2):
                sp.wait_ge(e_y, E - 2 + i + 1)
                sp.dma_start(slots_out_v[E - 2 + i], ye[i][:]).then_inc(e_stored[i], 16)
            for c in range(NC):
                sp.wait_ge(d_out, c + 1)
                sp.dma_start(out_v[:, c * CT:(c + 1) * CT, :], x_res[:, c * CT:(c + 1) * CT, :]).then_inc(stored, 16)
            sp.wait_ge(stored, 16 * NC)

        @block.gpsimd
        def _(pool):
            steps = Steps(pool_steps)
            def wait_apart(s, value):
                if isinstance(value, int):
                    pool.wait_ge(s, value)
                else:
                    value = pool.to_reg(value)
                    pool.wait_ge(pool_steps, steps.value())
                    pool.wait_ge(s, value)

            steps.did(nc.gpsimd.memset(ident[:], 0.0))
            steps.did(nc.gpsimd.memset(before[:], 1.0))
            nc.gpsimd.memset(ones[:], 1.0)
            nc.gpsimd.memset(ones_r[:].bitcast(F32), 1.0)
            nc.gpsimd.memset(mhalf[:], -0.5)
            nc.gpsimd.memset(carry[:], 0.0)
            for k in range(E):
                nc.gpsimd.memset(desc[:, :, k:k + 1], float(E - k))
                steps.did(nc.gpsimd.memset(slot0[:, :, k:k + 1], float(CAP * k)))
            pool.wait_ge(pool_steps, steps.value())
            nc.gpsimd.affine_select(out=ident[:], in_=ident[:], compare_op=ALU.not_equal, fill=1.0, base=0,
                                    pattern=[[-1, P]], channel_multiplier=1)
            nc.gpsimd.affine_select(out=before[:], in_=before[:], compare_op=ALU.is_gt, fill=0.0, base=0,
                                    pattern=[[1, P]], channel_multiplier=-1).then_inc(consts_ready, 1)

            def power(lane, n, count):
                pool.wait_ge(var_ready[lane], count)
                nc.gpsimd.tensor_tensor(out=rstd[lane][:, 0:n], in0=ve[lane][:, 0:n], in1=mhalf[:, 0:n],
                                        op=ALU.pow).then_inc(rstd_ready[lane], 1)

            def split(e, half, after_first=True):
                w = wsplit[half]
                pool.wait_ge(raw_in, 48 * (2 * e + half + 1))
                if half == 1:
                    wait_apart(down_done[1], 1 + e * (BLK // 2))
                elif after_first:
                    wait_apart(down_done[1], 1 + e * (BLK // 2) - HALFBLK // 2)
                nc.gpsimd.tensor_copy(w["g_hi"][:], raw_g[:])
                nc.gpsimd.tensor_copy(w["u_hi"][:], raw_u[:])
                nc.gpsimd.tensor_copy(w["d_hi"][:], raw_d[:]).then_inc(w_hi_ready, 1)
                pool.wait_ge(w_hi_ready, 2 * e + half + 1)
                nc.gpsimd.tensor_tensor(out=w["g_lo"][:], in0=raw_g[:], in1=w["g_hi"][:].bitcast(F32), op=ALU.subtract)
                nc.gpsimd.tensor_tensor(out=w["u_lo"][:], in0=raw_u[:], in1=w["u_hi"][:].bitcast(F32), op=ALU.subtract)
                nc.gpsimd.tensor_tensor(out=w["d_lo"][:], in0=raw_d[:], in1=w["d_hi"][:].bitcast(F32),
                                        op=ALU.subtract).then_inc(raw_split, 1)

            power(LN_A, 2 * CT, 1)
            nc.gpsimd.memset(acc[:], 0.0).then_inc(acc_zeroed, 1)
            pool.wait_ge(acc_zeroed, 1)
            pool.dma_start(slots_zero_v, acc[:].rearrange("p k (n d) -> p (k n) d", d=D)).then_inc(scattered, ZEROED)
            power(LN_A, 2 * CT, 2)
            power(LN_A, 2 * CT, 3)
            split(0, 0, after_first=False)
            power(LN_A, 2 * CT, 4)
            with pool.Fori(0, NE0 - 1) as e:
                split(e, 1)
                split(e + 1, 0)
            split(NE0 - 1, 1)

            def normalise(c, j):
                for half in range(2):
                    heads = slice(half * HH, (half + 1) * HH)
                    pool.wait_ge(c_rden, 2 * (c * CT + j) + half + 1)
                    nc.gpsimd.tensor_tensor(out=PC[j % 2][:, heads, :], in0=PC[j % 2][:, heads, :],
                                            in1=rdenC[j % 2][:, heads].unsqueeze(2).to_broadcast([P, HH, KEYS]),
                                            op=ALU.mult).then_inc(c_norm, 1)

            def scatter(r):
                wait_apart(r_slot, r + 1)
                for j in range(CT):
                    pool.indirect_dma_start(out=slots_in, out_offset=bass.IndirectOffsetOnAxis(ap=slot_c[:, j:j + 1], axis=0),
                                            in_=xn4[:, j, :], in_offset=None, bounds_check=T - 1,
                                            oob_is_err=False).then_inc(scattered, 16)

            def chunk(c, front, route):
                normalise(c, 0)
                normalise(c, 1)
                if front:
                    power(LN_FRONT, CT, c + 2)
                normalise(c, 2)
                normalise(c, 3)
                if front:
                    power(LN_FRONT2, CT, c + 2)
                if route:
                    scatter(c - 1)
                power(LN_ROUTE, CT, c + 1)

            pool.wait_ge(scattered, ZEROED)
            power(LN_FRONT, CT, 1)
            power(LN_FRONT2, CT, 1)
            nc.gpsimd.memset(ye_gath[:], 0.0).then_inc(cleared, 1)
            chunk(0, front=True, route=False)
            with pool.Fori(1, NC - 1) as c:
                chunk(c, front=True, route=True)
            chunk(NC - 1, front=False, route=True)
            scatter(NC - 1)

            for i in range(2):
                pool.wait_ge(e_stored[i], 1 + 16 * (E // 2))
            pool.wait_ge(cleared, 2)
            for t in range(NT):
                pool.indirect_dma_start(out=ye_gath[:, t, :], out_offset=None, in_=slots_out,
                                        in_offset=bass.IndirectOffsetOnAxis(ap=slot_all[:, t:t + 1], axis=0),
                                        bounds_check=T - 1, oob_is_err=False).then_inc(gathered, 16)

        @block.scalar
        def _(act):
            act.dma_start(ctx_s[:], ctx_v).then_inc(ctx_in, 16)
            act.dma_start(W0s[:], W0.rearrange("(k p) e -> p k e", p=P)).then_inc(w0_in, 16)
            act.dma_start(bcol[:], b0.rearrange("(k p) -> p k", p=P), allow_slow_non_contiguous=True).then_inc(w0_in, 16)
            act.dma_start(graw[:, 0:2], g_xattn.rearrange("(a g) -> a g", a=1).partition_broadcast(P)).then_inc(small_in, 16)
            act.dma_start(graw[:, 2:4], g_ffn.rearrange("(a g) -> a g", a=1).partition_broadcast(P)).then_inc(small_in, 16)
            act.dma_start(gammac[:], gamma.rearrange("(k p) -> p k", p=P), allow_slow_non_contiguous=True).then_inc(small_in, 16)
            act.dma_start(betac[:], beta.rearrange("(k p) -> p k", p=P), allow_slow_non_contiguous=True).then_inc(small_in, 16)
            act.dma_start(wgr[:], wgate.rearrange("(k p) e -> p k e", p=P)).then_inc(small_in, 16)
            act.dma_start(mask8[:], mask.rearrange("(a b) k -> a (b k)", a=1).partition_broadcast(P)).then_inc(small_in, 16)
            act.wait_ge(small_in, 96)
            nc.scalar.activation(tg[:], graw[:], ACT.Tanh).then_inc(tg_ready, 1)

            act.wait_ge(prep_pe, 1)
            nc.scalar.copy(W0T[:].rearrange("p k d -> p (k d)"), bank[0][:]).then_inc(prep_act, 1)
            act.wait_ge(prep_pe, 2)
            nc.scalar.copy(ctxT[:, 0, :], bank[1][:, 0:AK]).then_inc(prep_act, 1)
            for i in range(2):
                act.wait_ge(prep_pe, 6 + i)
                nc.scalar.copy(V0[:, 2 * i:2 * i + 2, :].rearrange("p k d -> p (k d)"), bank[5 + i][0:KH, :]).then_inc(prep_act, 1)

            with act.Fori(0, B) as b:
                for h in range(CB):
                    for k in range(KB):
                        act.wait_ge(a_xnT_ps, 4 * b + 2 * h + k + 1)
                        nc.scalar.copy(xnT[:, h, k, :], bank[2 * h + k][:]).then_inc(a_xnT, 1)
                for h in range(CB):
                    act.wait_ge(a_nmax, 2 * b + h + 1)
                    for j in range(CT):
                        n = h * CT + j
                        nc.scalar.activation(PA[:, n, :], bank[4 + n // 2][:, n % 2 * 256:n % 2 * 256 + KEYS], ACT.Exp,
                                             bias=nmsA[:, n:n + 1], scale=D ** -0.5,
                                             accum_out=denA[:, n:n + 1]).then_inc(a_probs, 1)
                for h in range(CB):
                    act.wait_ge(a_pT_ps, 4 * b + 2 * h + 1)
                    nc.scalar.copy(PTA[:, h, 0, :], bank[2 * h][0:KH, :]).then_inc(a_pT_act, 1)
                for h in range(CB):
                    for k in range(KB):
                        act.wait_ge(a_x2T_ps, 4 * b + 2 * h + k + 1)
                        nc.scalar.copy(xT_hi[:, k, bass.ts(b * CB + h, CH)], bank[2 * h + k][:]).then_inc(xT_hi_ready, 1)

            with act.Fori(0, NE0) as e:
                for k in range(BLK):
                    act.wait_ge(gate_ps, e * BLK + k + 1)
                    act.wait_ge(hid_ready[k % 2], 1 + e * (BLK // 2) + k // 2)
                    nc.scalar.activation(silu[k % 2][:], bank[k % 2][:], ACT.Silu).then_inc(silu_ready, 1)

            def xnT_out(f):
                for k in range(KB):
                    act.wait_ge(c_xnT_ps, KB * f + k + 1)
                    nc.scalar.activation(xnTc[:, k, :], bank[k][:], ACT.Identity, bias=betac[:, k:k + 1],
                                         scale=gammac[:, k:k + 1]).then_inc(c_xnT, 1)

            def q_out(f):
                for m in range(0, HB, 2):
                    act.wait_ge(c_q_ps, HB * f + m + 1)
                    nc.scalar.mul(qT[:, m, :], bank[SIM[m]][:], HD ** -0.5).then_inc(c_q_act, 1)

            def exps(c, j, half):
                t = c * CT + j
                act.wait_ge(c_nmax, 2 * t + half + 1)
                wait_if(act, c_pT_ps, 4 * (t - 1))
                for h in range(half * HH, (half + 1) * HH):
                    a = h // 2 % HPB
                    ins = nc.scalar.activation(PC[j % 2][:, h, :], bank[SIM[h // HH * 2 + h % 2]][:, a * KEYS:(a + 1) * KEYS], ACT.Exp,
                                               bias=nmC[j % 2][:, h:h + 1], accum_out=denC[j % 2][:, h:h + 1])
                ins.then_inc(c_probs, 1)

            def pT_out(c, j, g):
                act.wait_ge(c_pT_ps, 4 * (c * CT + j) + g + 1)
                nc.scalar.copy(PTC[:, 4 * g:4 * g + 4, :].rearrange("p a b -> p (a b)"), bank[0][0:KH, :]).then_inc(c_pT_act, 1)

            def xn4T_out(r):
                for k in range(KB):
                    act.wait_ge(r_xnT_ps, KB * r + k + 1)
                    nc.scalar.copy(xn4T[:, k, :], bank[ROUTE_T[k]][:]).then_inc(r_xnT, 1)

            def route_exp(r):
                act.wait_ge(r_shift, r + 1)
                nc.scalar.activation(rt["e"][:], rt["d"][:], ACT.Exp).then_inc(r_exp, 1)

            def chunk(c, front, route):
                f, r = c + 1, c - 1
                if route:
                    xn4T_out(r)
                for j in range(CT - 1):
                    exps(c, j + 1, 0)
                    pT_out(c, j, 0)
                    exps(c, j + 1, 1)
                    pT_out(c, j, 2)
                    if route and j == 0:
                        route_exp(r)
                pT_out(c, CT - 1, 0)
                pT_out(c, CT - 1, 2)
                if front:
                    xnT_out(f)
                    q_out(f)
                    exps(f, 0, 0)
                    exps(f, 0, 1)

            for m in range(0, HB, 2):
                act.wait_ge(c_prep_ps, m + 1)
                nc.scalar.copy(k1T[:, m, :], bank[m][:, 0:AK]).then_inc(c_prep_act, 1)
            for r in range(0, 2 * B, 2):
                act.wait_ge(c_prep_ps, HB + r + 1)
                nc.scalar.mul(V1[:, r, :], bank[V_PS[r]][0:KH, :], flag[0:KH, r // 2:r // 2 + 1]).then_inc(c_prep_act, 1)
            nc.scalar.activation(warm[:], tg[:, 0:1], ACT.Exp)
            xnT_out(0)
            q_out(0)
            exps(0, 0, 0)
            exps(0, 0, 1)
            chunk(0, front=True, route=False)
            with act.Fori(1, NC - 1) as c:
                chunk(c, front=True, route=True)
            chunk(NC - 1, front=False, route=True)
            xn4T_out(NC - 1)
            route_exp(NC - 1)

            with act.Fori(0, E // 2) as p:
                for i in range(2):
                    act.wait_ge(e_xT_ps, 2 * p + i + 1)
                    act.wait_ge(e_y_ps, 1 + 2 * p + i)
                    nc.scalar.copy(xeT[i][:].rearrange("p k s -> p (k s)"), bank[2 + i][:]).then_inc(e_xT, 1)

        @block.tensor
        def _(pe):
            start_at_one(pe, [*down_done, e_y_ps])
            mm, tr = nc.tensor.matmul, nc.tensor.transpose

            pe.wait_ge(consts_ready, 1)
            pe.wait_ge(w0_in, 32)
            for k in range(KB):
                for m in range(KB):
                    ins = tr(bank[0][:, k * D + m * P:k * D + (m + 1) * P], W0s[:, m, k * P:(k + 1) * P], ident[:])
            ins.then_inc(prep_pe, 1)
            pe.wait_ge(ctx_in, 16)
            for k in range(KB):
                for r in range(2 * B):
                    ins = tr(bank[1 + k][:, r * KH:(r + 1) * KH], ctx_s[:, r, k * P:(k + 1) * P], ident[0:KH, 0:KH])
                ins.then_inc(prep_pe, 1)
            pe.wait_ge(prep_act, 2)
            pe.wait_ge(prep_dve, 1)
            for m in range(KB):
                for k in range(KB):
                    ins = mm(bank[3 + m][:, 0:AK], W0T[:, k, m * P:(m + 1) * P], ctxT[:, k, :], start=k == 0, stop=k == KB - 1)
                ins.then_inc(prep_pe, 1)
            pe.wait_ge(prep_dve, 3)
            for i in range(2):
                for r in range(2):
                    for m in range(KB):
                        ins = tr(bank[5 + i][0:KH, r * D + m * P:r * D + (m + 1) * P],
                                 k0T[:, m, (2 * i + r) * KH:(2 * i + r + 1) * KH], ident[:])
                ins.then_inc(prep_pe, 1)
            for k in range(KB):
                for m in range(KB):
                    ins = mm(bank[1 + k][:, 0:AK], W0s[:, m, k * P:(k + 1) * P], k0T[:, m, :], start=m == 0, stop=m == KB - 1)
                ins.then_inc(prep_pe, 1)
            for m in range(KB):
                ins = mm(bank[7][0:1, 0:AK], bcol[:, m:m + 1], k0T[:, m, :], start=m == 0, stop=m == KB - 1)
            ins.then_inc(prep_pe, 1)
            pe.wait_ge(prep_act, 4)
            pe.wait_ge(prep_dve, 6)

            def transpose_chunk(src, banks, src_tile, signal):
                for k in range(KB):
                    for j in range(CT):
                        ins = tr(bank[banks[k]][:, j * P:(j + 1) * P], src[:, src_tile + j, k * P:(k + 1) * P], ident[:])
                    ins.then_inc(signal, 1)

            with pe.Fori(0, B) as b:
                for h in range(CB):
                    pe.wait_ge(a_ln1, 2 * b + h + 1)
                    transpose_chunk(xnA, (2 * h, 2 * h + 1), h * CT, a_xnT_ps)
                for h in range(CB):
                    pe.wait_ge(a_xnT, 4 * b + 2 * h + 2)
                    for j in range(CT):
                        n = h * CT + j
                        sco = bank[4 + n // 2][:, n % 2 * 256:n % 2 * 256 + KEYS]
                        for k in range(KB):
                            mm(sco, xnT[:, h, k, j * P:(j + 1) * P], A0[:, k, bass.ts(b, KEYS)], start=k == 0, stop=False)
                        ins = mm(sco, ones[0:1, :], r0[:, bass.ts(b, KEYS)], start=False, stop=True)
                        if j % 2:
                            ins.then_inc(a_sc_ps, 1)
                for h in range(CB):
                    pe.wait_ge(a_probs, 2 * CT * b + h * CT + CT)
                    for k in range(2):
                        for j in range(CT):
                            ins = tr(bank[2 * h + k][0:KH, j * P:(j + 1) * P], PA[:, h * CT + j, k * KH:(k + 1) * KH], ident[:])
                        ins.then_inc(a_pT_ps, 1)
                for h in range(CB):
                    pe.wait_ge(a_pT_act, 2 * b + h + 1)
                    pe.wait_ge(a_pT_dve, 2 * b + h + 1)
                    for j in range(CT):
                        n = h * CT + j
                        for k in range(2):
                            ins = mm(bank[4 + n // 2][:, n % 2 * D:(n % 2 + 1) * D], PTA[:, h, k, j * P:(j + 1) * P],
                                     V0[:, bass.ds(2 * b + k, 1), :].rearrange("p a d -> p (a d)"), start=k == 0, stop=k == 1)
                        if j % 2:
                            ins.then_inc(a_out_ps, 1)
                for h in range(CB):
                    pe.wait_ge(a_ln2, 2 * b + h + 1)
                    transpose_chunk(xnA, (2 * h, 2 * h + 1), h * CT, a_x2T_ps)

            def three(pairs, ps, start, stop):
                n = 0
                for w_hi, w_lo, a_hi, a_lo in pairs:
                    for w, a in ((w_hi, a_hi), (w_hi, a_lo), (w_lo, a_hi)):
                        n += 1
                        ins = mm(ps, w, a, start=start and n == 1, stop=stop and n == 3 * len(pairs))
                return ins

            def gate_up(e, k):
                half, chunk, f = k // HALFBLK, k % HALFBLK // FB, k % FB
                w = wsplit[half]
                fs, ts = slice(f * P, (f + 1) * P), slice(chunk * CH, (chunk + 1) * CH)
                if k % HALFBLK == 0:
                    pe.wait_ge(raw_split, 2 * e + half + 1)
                pe.wait_ge(hid_ready[k % 2], 1 + e * (BLK // 2) + k // 2)
                for hi, lo, ps, signal in (("g_hi", "g_lo", bank[k % 2], gate_ps), ("u_hi", "u_lo", bank[2 + k % 2], up_ps)):
                    three([(w[hi][:, d, fs], w[lo][:, d, fs], xT_hi[:, d, ts], xT_lo[:, d, ts]) for d in range(KB)],
                          ps[:], True, True).then_inc(signal, 1)

            def down(e, k):
                half, f, u = k // HALFBLK, k % FB, k // FB
                w = wsplit[half]
                if f == 0:
                    pe.wait_ge(acc_added[u % 2], 1 + e * (UNITS // 2) + u // 2)
                ps = [bank[4 + 2 * (u % 2) + m] for m in range(KB)]
                hs = [slice(m * P, (m + 1) * P) for m in range(KB)]
                pe.wait_ge(hi_ready, e * BLK + k + 1)
                for m in range(KB):
                    mm(ps[m][:], w["d_hi"][:, f, hs[m]], hid_hi[k % 2][:], start=f == 0, stop=False)
                for m in range(KB):
                    mm(ps[m][:], w["d_lo"][:, f, hs[m]], hid_hi[k % 2][:], start=False, stop=False)
                pe.wait_ge(lo_ready, e * BLK + k + 1)
                mm(ps[0][:], w["d_hi"][:, f, hs[0]], hid_lo[k % 2][:], start=False, stop=f == FB - 1)
                ins = mm(ps[1][:], w["d_hi"][:, f, hs[1]], hid_lo[k % 2][:], start=False, stop=f == FB - 1)
                ins.then_inc(down_done[k % 2], 1)

            pe.wait_ge(xT_hi_ready, 4 * CB)
            pe.wait_ge(xT_lo_ready, 4 * CB)
            gate_up(0, 0)
            with pe.Fori(0, NE0) as e:
                for k in range(BLK):
                    if k + 1 < BLK:
                        gate_up(e, k + 1)
                    else:
                        with pe.If(e < NE0 - 1):
                            gate_up(e + 1, 0)
                    down(e, k)

            pe.wait_ge(wc_in, 64)
            for m in range(HB):
                for k in range(KB):
                    ins = mm(bank[m][:, 0:AK], Wkvs[:, k, m * P:(m + 1) * P], ctxT[:, k, :], start=k == 0, stop=k == KB - 1)
                ins.then_inc(c_prep_ps, 1)
            def y_transposes(sums, first, banks):
                for j in range(CT):
                    for m in range(KB):
                        ins = tr(bank[banks[j // 2]][:, j % 2 * D + m * P:j % 2 * D + (m + 1) * P],
                                 sums[:, m, first + j * P:first + (j + 1) * P], ident[:])
                    if j % 2:
                        ins.then_inc(c_yT_ps, 1)

            def queries(f):
                for m in range(HB):
                    for k in range(KB):
                        ins = mm(bank[SIM[m]][:], Wqs[:, k, m * P:(m + 1) * P], xnTc[:, k, :], start=k == 0, stop=k == KB - 1)
                    ins.then_inc(c_q_ps, 1)

            def wait_apart(s, value):
                if not isinstance(value, int):
                    value = pe.to_reg(value)
                pe.wait_ge(consts_ready, 1)
                pe.wait_ge(s, value)

            def scores(c, j, half):
                b = batch_of(c)
                mask_row = mrow[:, bass.ds(b, 1), :].rearrange("p b k -> p (b k)")
                banks = SIM[2 * half:2 * half + 2]
                for a in range(HPB):
                    ks = slice(a * KEYS, (a + 1) * KEYS)
                    for s in banks:
                        mm(bank[s][:, ks], ones_r[:], mask_row, start=True, stop=False)
                    for i, s in enumerate(banks):
                        h = half * HH + 2 * a + i
                        r = slice(h % 2 * HD, (h % 2 + 1) * HD)
                        ins = mm(bank[s][:, ks], qT[r, h // 2, j * P:(j + 1) * P], kcur[r, h // 2, :], start=False, stop=True)
                ins.then_inc(c_sim_ps, 1)

            def scores_after_queries(c):
                wait_apart(kcur_in, 16 * c + 16)
                for half in range(2):
                    wait_apart(c_q_act, 2 * c + half + 1)
                    pe.wait_ge(c_q_dve, 2 * c + half + 1)
                    scores(c, 0, half)

            def scores_after_exps(c, j):
                for half in range(2):
                    wait_apart(c_probs, 2 * (c * CT + j - 1) + half + 1)
                    scores(c, j, half)

            def p_transposes(c, j, groups):
                t = c * CT + j
                pe.wait_ge(c_norm, 2 * t + groups[0] // 2 + 1)
                for g in groups:
                    if g >= 2:
                        pe.wait_ge(c_pT_act if g % 2 == 0 else c_pT_dve, 2 * t + 1)
                    for a in range(4):
                        n = 4 * g + a
                        ins = tr(bank[g % 2][0:KH, a * P:(a + 1) * P], PC[j % 2][:, n // 2, n % 2 * KH:(n % 2 + 1) * KH], ident[:])
                    ins.then_inc(c_pT_ps, 1)

            def attend(c, j):
                t = c * CT + j
                if j == 0:
                    pe.wait_ge(vcur_in, 16 * c + 16)
                for g in range(4):
                    pe.wait_ge(c_pT_act if g % 2 == 0 else c_pT_dve, 2 * t + 1 + g // 2)
                    for h in (2 * g, 2 * g + 1):
                        for k in range(2):
                            ins = mm(bank[5][h % 2 * HD:(h % 2 + 1) * HD, h // 2 * P:(h // 2 + 1) * P],
                                     vcur[:, k, h * HD:(h + 1) * HD], PTC[:, 2 * h + k, :], start=k == 0, stop=k == 1)
                ins.then_inc(c_o_ps, 1)

            def project(c, j):
                t = c * CT + j
                pe.wait_ge(c_o, t + 1)
                wait_if(pe, c_res, t)
                for k in range(HB):
                    ins = mm(bank[7][:, 0:D], oT[:, k, :], Wouts[:, k, :], start=k == 0, stop=k == HB - 1)
                ins.then_inc(c_out_ps, 1)

            def route_transposes(r):
                pe.wait_ge(r_ln, r + 1)
                transpose_chunk(xn4, ROUTE_T, 0, r_xnT_ps)

            def logits(r):
                pe.wait_ge(r_xnT, 2 * r + 2)
                for j in range(CT):
                    for k in range(KB):
                        ins = mm(bank[7][:, D + j * E:D + (j + 1) * E], xn4T[:, k, j * P:(j + 1) * P], wgr[:, k, :], start=k == 0, stop=k == KB - 1)
                ins.then_inc(r_logit_ps, 1)

            def locations(r):
                pe.wait_ge(r_one, r + 1)
                one = rt["one"][:].rearrange("p j e -> p (j e)")
                at = D + CT * E
                mm(bank[7][:, at:at + CT * E], before[:], one, start=True, stop=True)
                mm(bank[7][:, at + CT * E:at + 2 * CT * E], ones[:], one, start=True, stop=True).then_inc(r_loc_ps, 1)

            def chunk(c, front, route):
                f, r = c + 1, c - 1
                if route:
                    route_transposes(r)
                if front:
                    pe.wait_ge(y_in, 16 * f)
                    y_transposes(yc, 0, (0, 1))
                scores_after_exps(c, 1)
                if front:
                    pe.wait_ge(c_x2, f + 1)
                p_transposes(c, 0, (0, 1))
                if route:
                    logits(r)
                p_transposes(c, 0, (2, 3))
                attend(c, 0)
                scores_after_exps(c, 2)
                p_transposes(c, 1, (0, 1))
                if route:
                    pe.wait_ge(r_shift, r + 1)
                project(c, 0)
                p_transposes(c, 1, (2, 3))
                attend(c, 1)
                scores_after_exps(c, 3)
                p_transposes(c, 2, (0, 1))
                project(c, 1)
                p_transposes(c, 2, (2, 3))
                if route:
                    pe.wait_ge(c_res, c * CT + 2)
                    locations(r)
                attend(c, 2)
                p_transposes(c, 3, (0, 1))
                if route:
                    pe.wait_ge(r_loc_read, r + 1)
                project(c, 2)
                p_transposes(c, 3, (2, 3))
                attend(c, 3)
                if front:
                    pe.wait_ge(c_ln, f + 1)
                    transpose_chunk(xnC2, (0, 1), 0, c_xnT_ps)
                project(c, 3)
                if front:
                    pe.wait_ge(c_probs, 2 * CT * f)
                    pe.wait_ge(c_xnT, 2 * f + 2)
                    queries(f)
                    scores_after_queries(f)

            pe.wait_ge(acc_added[0], 1 + 4 * NE0)
            pe.wait_ge(acc_added[1], 1 + 4 * NE0)
            y_transposes(acc, 0, (4, 5))
            for r in range(2 * B):
                if r == 2:
                    pe.wait_ge(c_prep_act, 1)
                    pe.wait_ge(c_prep_dve, 1)
                for k in range(KB):
                    ins = mm(bank[V_PS[r]][0:KH, :], ctxT[:, k, r * KH:(r + 1) * KH], Wkvs[:, k, INNER:2 * INNER],
                             start=k == 0, stop=k == KB - 1)
                ins.then_inc(c_prep_ps, 1)
            pe.wait_ge(c_prep_act, B + HB // 2)
            pe.wait_ge(c_prep_dve, B + HB // 2)
            pe.wait_ge(c_ln, 1)
            transpose_chunk(xnC2, (0, 1), 0, c_xnT_ps)
            pe.wait_ge(c_xnT, 2)
            queries(0)
            scores_after_queries(0)
            chunk(0, front=True, route=False)
            with pe.Fori(1, NC - 1) as c:
                chunk(c, front=True, route=True)
            chunk(NC - 1, front=False, route=True)
            route_transposes(NC - 1)
            logits(NC - 1)
            locations(NC - 1)

            with pe.Fori(0, E // 2) as p:
                for i in range(2):
                    pe.wait_ge(e_w_in[i], 16 * (p + 1))
                    for k in range(KB):
                        for m in range(KB):
                            ins = tr(bank[i][:, k * D + m * P:k * D + (m + 1) * P], we_raw[i][:, m, k * P:(k + 1) * P], ident[:])
                    ins.then_inc(e_wT_ps, 1)
                    pe.wait_ge(e_x_in[i], 16 * (p + 1))
                    for k in range(KB):
                        for s in range(CAP // P):
                            ins = tr(bank[2 + i][:, k * CAP + s * P:k * CAP + (s + 1) * P], xe[i][:, s, k * P:(k + 1) * P], ident[:])
                    ins.then_inc(e_xT_ps, 1)
                    pe.wait_ge(e_wT, 2 * p + i + 1)
                    pe.wait_ge(e_xT, 2 * p + i + 1)
                    for s in range(CAP // P):
                        mm(bank[4 + i][:, s * D:(s + 1) * D], ones[0:1, :], brow[:, bass.ts(2 * p + i, D)], start=True, stop=False)
                        for k in range(KB):
                            ins = mm(bank[4 + i][:, s * D:(s + 1) * D], xeT[i][:, k, s * P:(s + 1) * P], weT[i][:, k, :],
                                     start=False, stop=k == KB - 1)
                    ins.then_inc(e_y_ps, 1)

        @block.vector
        def _(dve):
            start_at_one(dve, [*hid_ready, *acc_added])
            steps = Steps(dve_steps)

            front, ln4, route = Steps(front_steps), Steps(ln4_steps), Steps(route_steps)

            def own(done=steps):
                dve.wait_ge(done.sem, done.value())

            def wait_apart(s, value):
                if isinstance(value, int):
                    dve.wait_ge(s, value)
                else:
                    value = dve.to_reg(value)
                    dve.wait_ge(consts_ready, 1)
                    dve.wait_ge(s, value)

            def variances(srcs, lane, done):
                n = len(srcs)
                for i, s in enumerate(srcs):
                    ins = nc.vector.bn_stats(stats[lane][:, i, :], s)
                done.did(ins)
                wait_apart(done.sem, done.value())
                for i in range(n):
                    ins = nc.vector.bn_aggr(mv[lane][:, i, :], stats[lane][:, i, :])
                done.did(ins)
                own(done)
                nc.vector.tensor_scalar(ve[lane][:, 0:n], mv[lane][:, 0:n, 1], EPS, None, ALU.add).then_inc(var_ready[lane], 1)

            def normed(srcs, dsts, lane, count):
                dve.wait_ge(rstd_ready[lane], count)
                for i in range(len(srcs)):
                    ins = nc.vector.tensor_scalar(dsts[i], srcs[i], mv[lane][:, i, 0:1], rstd[lane][:, i:i + 1], ALU.subtract, ALU.mult)
                return ins

            def norm(srcs, dsts, count, signal):
                variances(srcs, LN_A, steps)
                for h in range(CB):
                    dve.wait_ge(rstd_ready[LN_A], count)
                    for i in range(h * CT, (h + 1) * CT):
                        ins = nc.vector.tensor_scalar(dsts[i], srcs[i], mv[LN_A][:, i, 0:1], rstd[LN_A][:, i:i + 1], ALU.subtract, ALU.mult)
                    ins.then_inc(signal, 1)

            def tiles(first, n):
                return [x_res[:, bass.ds(first + i, 1), :].rearrange("p a d -> p (a d)") for i in range(n)]

            dve.wait_ge(prep_pe, 3)
            nc.vector.tensor_copy(ctxT[:, 1, :], bank[2][:, 0:AK]).then_inc(prep_dve, 1)
            dve.wait_ge(w0_in, 32)
            for m in range(KB):
                dve.wait_ge(prep_pe, 4 + m)
                nc.vector.tensor_scalar(k0T[:, m, :], bank[3 + m][:, 0:AK], bcol[:, m:m + 1], None, ALU.add).then_inc(prep_dve, 1)
            for k in range(KB):
                dve.wait_ge(prep_pe, 8 + k)
                nc.vector.tensor_copy(A0[:, k, :], bank[1 + k][:, 0:AK]).then_inc(prep_dve, 1)
            dve.wait_ge(prep_pe, 10)
            nc.vector.tensor_copy(r0[:], bank[7][0:1, 0:AK]).then_inc(prep_dve, 1)
            dve.wait_ge(small_in, 96)
            steps.did(nc.vector.tensor_copy(maskf[:], mask8[:]))
            own()
            nc.vector.tensor_scalar(mrow[:], maskf[0:1, :].rearrange("p (b k) -> p b k", b=B), -MASKED, MASKED, ALU.mult, ALU.add)
            steps.did(nc.vector.reduce_max(anyv[:], maskf[:].rearrange("p (b k) -> p b k", b=B), AX.X))
            own()
            steps.did(nc.vector.reciprocal(ranyv[:], anyv[:]))
            own()
            steps.did(nc.vector.tensor_tensor(out=flag[:], in0=anyv[:], in1=ranyv[:], op=ALU.mult))
            dve.wait_ge(tg_ready, 1)

            with dve.Fori(0, B) as b:
                steps.enter(b, 9)
                wait_apart(x_in, 16 * CB * (b + 1))
                xs = tiles(b * 2 * CT, 2 * CT)
                norm(xs, [xnA[:, n, :] for n in range(2 * CT)], 2 * b + 1, a_ln1)
                for h in range(CB):
                    for i in range(2):
                        dve.wait_ge(a_sc_ps, 4 * b + 2 * h + i + 1)
                        n = h * CT + 2 * i
                        ins = nc.vector.reduce_max(nmA[:, n:n + 2], bank[4 + n // 2][:].rearrange("p (a k) -> p a k", a=2)[:, :, 0:KEYS],
                                                   AX.X, negate=True)
                    steps.did(ins)
                    own()
                    nc.vector.tensor_scalar(nmsA[:, h * CT:(h + 1) * CT], nmA[:, h * CT:(h + 1) * CT], D ** -0.5, None,
                                            ALU.mult).then_inc(a_nmax, 1)
                for h in range(CB):
                    dve.wait_ge(a_pT_ps, 4 * b + 2 * h + 2)
                    nc.vector.tensor_copy(PTA[:, h, 1, :], bank[2 * h + 1][0:KH, :]).then_inc(a_pT_dve, 1)
                dve.wait_ge(a_probs, 2 * CT * (b + 1))
                steps.did(nc.vector.reciprocal(rdenA[:], denA[:]))
                own()
                steps.did(nc.vector.tensor_scalar(coefA[:], rdenA[:], tg[:, 0:1], None, ALU.mult))
                own()
                for n in range(2 * CT):
                    dve.wait_ge(a_out_ps, 4 * b + n // 2 + 1)
                    ins = nc.vector.scalar_tensor_tensor(out=xs[n], in0=bank[4 + n // 2][:, n % 2 * D:(n % 2 + 1) * D],
                                                         scalar=coefA[:, n:n + 1], in1=xs[n], op0=ALU.mult, op1=ALU.add)
                steps.did(ins)
                wait_apart(dve_steps, steps.value())
                norm(xs, [xnA[:, n, :] for n in range(2 * CT)], 2 * b + 2, a_ln2)
                for h in range(CB):
                    for k in range(KB):
                        dve.wait_ge(xT_hi_ready, 4 * b + 2 * h + k + 1)
                        ts = bass.ts(b * CB + h, CH)
                        ins = nc.vector.tensor_tensor(out=xT_lo[:, k, ts], in0=bank[2 * h + k][:], in1=xT_hi[:, k, ts].bitcast(F32),
                                                      op=ALU.subtract)
                        ins.then_inc(xT_lo_ready, 1)
                steps.leave(B)

            dve.wait_ge(acc_zeroed, 1)
            dve.wait_ge(scattered, ZEROED)

            def add_up(e, u):
                dve.wait_ge(down_done[1], 1 + e * (BLK // 2) + (u + 1) * FB // 2)
                ts = slice(u % NC * CH, (u % NC + 1) * CH)
                for m in range(KB):
                    ins = nc.vector.tensor_tensor(out=acc[:, m, ts], in0=bank[4 + 2 * (u % 2) + m][:], in1=acc[:, m, ts], op=ALU.add)
                ins.then_inc(acc_added[u % 2], 1)

            with dve.Fori(0, NE0) as e:
                for k in range(BLK):
                    i = k % 2
                    done = e * (BLK // 2) + k // 2
                    dve.wait_ge(up_ps, e * BLK + k + 1)
                    dve.wait_ge(silu_ready, e * BLK + k + 1)
                    nc.vector.tensor_tensor(out=hid[i][:], in0=bank[2 + i][:], in1=silu[i][:], op=ALU.mult).then_inc(hid_ready[i], 1)
                    dve.wait_ge(hid_ready[i], 1 + done + 1)
                    dve.wait_ge(down_done[i], 1 + done)
                    nc.vector.tensor_copy(hid_hi[i][:], hid[i][:]).then_inc(hi_ready, 1)
                    dve.wait_ge(hi_ready, e * BLK + k + 1)
                    nc.vector.tensor_tensor(out=hid_lo[i][:], in0=hid[i][:], in1=hid_hi[i][:].bitcast(F32),
                                            op=ALU.subtract).then_inc(lo_ready, 1)
                    if k and k % FB == 0:
                        add_up(e, k // FB - 1)
                add_up(e, UNITS - 1)

            def bc(v):
                return v.unsqueeze(2).to_broadcast([P, CT, E])

            def add_experts(f, banks):
                front.round(f, FRONT_STEPS)
                for j, x in enumerate(tiles(f * CT, CT)):
                    dve.wait_ge(c_yT_ps, 2 * f + j // 2 + 1)
                    ins = nc.vector.scalar_tensor_tensor(out=x, in0=bank[banks[j // 2]][:, j % 2 * D:(j % 2 + 1) * D],
                                                         scalar=tg[:, 2:3], in1=x, op0=ALU.mult, op1=ALU.add)
                ins.then_inc(c_x2, 1)

            def front_variances(f):
                wait_apart(c_x2, f + 1)
                variances(tiles(f * CT, CT), LN_FRONT, front)

            def front_normed(f):
                front.did(normed(tiles(f * CT, CT), [xnC[:, j, :] for j in range(CT)], LN_FRONT, f + 1))

            def front_variances2(f):
                wait_apart(front.sem, front.value())
                variances([xnC[:, j, :] for j in range(CT)], LN_FRONT2, front)
                front.round_over()

            def front_normed2(f):
                normed([xnC[:, j, :] for j in range(CT)], [xnC2[:, j, :] for j in range(CT)], LN_FRONT2, f + 1).then_inc(c_ln, 1)

            def q_out(f, m):
                dve.wait_ge(c_q_ps, HB * f + m + 1)
                nc.vector.tensor_scalar(qT[:, m, :], bank[SIM[m]][:], HD ** -0.5, None, ALU.mult).then_inc(c_q_dve, 1)

            def maxes(c, j, half):
                dve.wait_ge(c_sim_ps, 2 * (c * CT + j) + half + 1)
                for i in range(2):
                    h = half * HH + i
                    ins = nc.vector.reduce_max(nmC[j % 2][:, h:h + 3:2],
                                               bank[SIM[2 * half + i]][:, 0:HPB * KEYS].rearrange("p (a k) -> p a k", a=HPB),
                                               AX.X, negate=True)
                ins.then_inc(c_nmax, 1)

            def dens(c, j, half):
                heads = slice(half * HH, (half + 1) * HH)
                dve.wait_ge(c_probs, 2 * (c * CT + j) + half + 1)
                nc.vector.reciprocal(rdenC[j % 2][:, heads], denC[j % 2][:, heads]).then_inc(c_rden, 1)

            def pT_out(c, j, g):
                dve.wait_ge(c_pT_ps, 4 * (c * CT + j) + g + 1)
                nc.vector.tensor_copy(PTC[:, 4 * g:4 * g + 4, :].rearrange("p a b -> p (a b)"), bank[1][0:KH, :]).then_inc(c_pT_dve, 1)

            def o_out(c, j):
                dve.wait_ge(c_o_ps, c * CT + j + 1)
                nc.vector.tensor_copy(oT[:].rearrange("p k t -> p (k t)"), bank[5][:]).then_inc(c_o, 1)

            def add_attention(c, j):
                dve.wait_ge(c_out_ps, c * CT + j + 1)
                x = tiles(c * CT + j, 1)[0]
                nc.vector.scalar_tensor_tensor(out=x, in0=bank[7][:, 0:D], scalar=tg[:, 1:2], in1=x,
                                               op0=ALU.mult, op1=ALU.add).then_inc(c_res, 1)

            def route_variances(r):
                ln4.round(r, LN4_STEPS)
                wait_apart(c_res, (r + 1) * CT)
                variances(tiles(r * CT, CT), LN_ROUTE, ln4)
                ln4.round_over()

            def route_normed(r):
                wait_apart(scattered, ZEROED + 16 * CT * r)
                normed(tiles(r * CT, CT), [xn4[:, j, :] for j in range(CT)], LN_ROUTE, r + 1).then_inc(r_ln, 1)

            def route_shift(r):
                route.round(r, ROUTE_STEPS)
                dve.wait_ge(r_logit_ps, r + 1)
                logits = bank[7][:, D:D + CT * E].rearrange("p (j e) -> p j e", j=CT)
                route.did(nc.vector.reduce_max(rs["max"][:], logits, AX.X))
                own(route)
                nc.vector.tensor_tensor(out=rt["d"][:], in0=logits, in1=bc(rs["max"][:]), op=ALU.subtract).then_inc(r_shift, 1)

            def route_choice(r):
                dve.wait_ge(r_exp, r + 1)
                route.did(nc.vector.reduce_sum(rs["sum"][:], rt["e"][:], AX.X))
                own(route)
                route.did(nc.vector.reciprocal(rs["rsum"][:], rs["sum"][:]))
                own(route)
                route.did(nc.vector.tensor_tensor(out=rt["p"][:], in0=rt["e"][:], in1=bc(rs["rsum"][:]), op=ALU.mult))
                own(route)
                route.did(nc.vector.reduce_max(rs["best"][:], rt["p"][:], AX.X))
                own(route)
                route.did(nc.vector.tensor_tensor(out=rt["top"][:], in0=rt["p"][:], in1=bc(rs["best"][:]), op=ALU.is_equal))
                own(route)
                route.did(nc.vector.tensor_tensor(out=rt["score"][:], in0=rt["top"][:], in1=desc[:], op=ALU.mult))
                own(route)
                route.did(nc.vector.reduce_max(rs["first"][:], rt["score"][:], AX.X))
                own(route)
                nc.vector.tensor_tensor(out=rt["one"][:], in0=rt["score"][:], in1=bc(rs["first"][:]),
                                        op=ALU.is_equal).then_inc(r_one, 1)

            def route_places(r):
                dve.wait_ge(r_loc_ps, r + 1)
                at = D + CT * E
                nc.vector.tensor_copy(places[:].rearrange("p a j e -> p (a j e)"), bank[7][:, at:at + 2 * CT * E]).then_inc(r_loc_read, 1)

            def route_slots(r):
                inside, totals = places[:, 0], places[:, 1]
                dve.wait_ge(r_loc_read, r + 1)
                for j in range(CT):
                    nc.vector.tensor_copy(rt["pre"][:, j, :], carry[:])
                    route.did(nc.vector.tensor_tensor(out=carry[:], in0=totals[:, j, :], in1=carry[:], op=ALU.add))
                    own(route)
                route.did(nc.vector.tensor_tensor(out=rt["loc"][:], in0=inside, in1=rt["pre"][:], op=ALU.add))
                own(route)
                nc.vector.tensor_tensor(out=rt["m1"][:], in0=rt["one"][:], in1=rt["loc"][:], op=ALU.mult)
                route.did(nc.vector.tensor_tensor(out=rt["m2"][:], in0=rt["one"][:], in1=slot0[:], op=ALU.mult))
                own(route)
                nc.vector.reduce_sum(rs["loc"][:], rt["m1"][:], AX.X)
                route.did(nc.vector.reduce_sum(rs["slot"][:], rt["m2"][:], AX.X))
                own(route)
                nc.vector.tensor_scalar(rs["keep"][:], rs["loc"][:], float(CAP), None, ALU.is_lt)
                nc.vector.tensor_scalar(rs["far"][:], rs["loc"][:], float(CAP), float(DROPPED), ALU.is_ge, ALU.mult)
                route.did(nc.vector.tensor_tensor(out=rs["slot"][:], in0=rs["slot"][:], in1=rs["loc"][:], op=ALU.add))
                own(route)
                g_ts = bass.ts(r, CT)
                nc.vector.tensor_tensor(out=gate_all[:, g_ts], in0=rs["best"][:], in1=rs["keep"][:], op=ALU.mult)
                nc.vector.tensor_tensor(out=slot_c[:], in0=rs["slot"][:], in1=rs["far"][:], op=ALU.add).then_inc(r_slot, 1)
                route.did(nc.vector.tensor_tensor(out=slot_all[:, g_ts], in0=rs["slot"][:], in1=rs["far"][:], op=ALU.add))
                route.round_over()

            def chunk(c, with_front, with_route):
                f, r = c + 1, c - 1
                if with_front:
                    add_experts(f, (0, 1))
                maxes(c, 1, 0)
                maxes(c, 1, 1)
                pT_out(c, 0, 1)
                dens(c, 1, 0)
                if with_route:
                    route_shift(r)
                pT_out(c, 0, 3)
                dens(c, 1, 1)
                if with_front:
                    front_variances(f)
                o_out(c, 0)
                maxes(c, 2, 0)
                maxes(c, 2, 1)
                pT_out(c, 1, 1)
                dens(c, 2, 0)
                add_attention(c, 0)
                pT_out(c, 1, 3)
                dens(c, 2, 1)
                if with_route:
                    route_choice(r)
                if with_front:
                    front_normed(f)
                o_out(c, 1)
                maxes(c, 3, 0)
                maxes(c, 3, 1)
                pT_out(c, 2, 1)
                dens(c, 3, 0)
                add_attention(c, 1)
                pT_out(c, 2, 3)
                dens(c, 3, 1)
                if with_route:
                    route_places(r)
                if with_front:
                    front_variances2(f)
                o_out(c, 2)
                pT_out(c, 3, 1)
                if with_route:
                    route_slots(r)
                add_attention(c, 2)
                if with_front:
                    front_normed2(f)
                pT_out(c, 3, 3)
                o_out(c, 3)
                add_attention(c, 3)
                route_variances(c)
                if with_front:
                    q_out(f, 1)
                route_normed(c)
                if with_front:
                    q_out(f, 3)
                    for half in range(2):
                        maxes(f, 0, half)
                    for half in range(2):
                        dens(f, 0, half)

            for m in range(1, HB, 2):
                dve.wait_ge(c_prep_ps, m + 1)
                nc.vector.tensor_copy(k1T[:, m, :], bank[m][:, 0:AK]).then_inc(c_prep_dve, 1)
            add_experts(0, (4, 5))
            front_variances(0)
            for r in range(1, 2 * B, 2):
                dve.wait_ge(c_prep_ps, HB + r + 1)
                nc.vector.tensor_scalar(V1[:, r, :], bank[V_PS[r]][0:KH, :], flag[0:KH, r // 2:r // 2 + 1], None,
                                        ALU.mult).then_inc(c_prep_dve, 1)
            front_normed(0)
            front_variances2(0)
            front_normed2(0)
            q_out(0, 1)
            q_out(0, 3)
            for half in range(2):
                maxes(0, 0, half)
            for half in range(2):
                dens(0, 0, half)
            chunk(0, True, False)
            with dve.Fori(1, NC - 1) as c:
                chunk(c, True, True)
            chunk(NC - 1, False, True)
            route_shift(NC - 1)
            route_choice(NC - 1)
            route_places(NC - 1)
            route_slots(NC - 1)

            own(route)
            nc.vector.tensor_scalar(coefD[:], gate_all[:], tg[:, 3:4], None, ALU.mult).then_inc(cleared, 1)
            with dve.Fori(0, E // 2) as p:
                for i in range(2):
                    dve.wait_ge(e_wT_ps, 2 * p + i + 1)
                    nc.vector.tensor_copy(weT[i][:].rearrange("p k s -> p (k s)"), bank[i][:]).then_inc(e_wT, 1)
                    dve.wait_ge(e_y_ps, 1 + 2 * p + i + 1)
                    dve.wait_ge(e_stored[i], 1 + 16 * p)
                    nc.vector.tensor_copy(ye[i][:].rearrange("p k s -> p (k s)"), bank[4 + i][:]).then_inc(e_y, 1)
            dve.wait_ge(cleared, 2)
            dve.wait_ge(gathered, 16 * NT)
            for t in range(NT):
                ins = nc.vector.scalar_tensor_tensor(out=x_res[:, t, :], in0=ye_gath[:, t, :], scalar=coefD[:, t:t + 1],
                                                     in1=x_res[:, t, :], op0=ALU.mult, op1=ALU.add)
                if t % CT == CT - 1:
                    ins.then_inc(d_out, 1)


FRONT_STEPS, LN4_STEPS, ROUTE_STEPS = 5, 2, 17


_INS = ['x', 'ctx_1024', 'mask_BxS2_bk0', 'g_xattn', 'g_ffn', 'L0_xattn_W', 'L0_xattn_b', 'L0_ffn_Wg', 'L0_ffn_Wu', 'L0_ffn_Wd',
        'L1_xattn_ln_gamma', 'L1_xattn_ln_beta', 'L1_xattn_Wq', 'L1_xattn_Wkv', 'L1_xattn_Wout', 'L1_ffn_wg', 'L1_ffn_W', 'L1_ffn_b']
_OUTS = [((2, 1024, 256), 'float32')]


def kernel(**inputs):
    import numpy as _np
    import concourse.bacc as _bacc
    from concourse import mybir as _mybir
    from concourse.bass_utils import run_bass_kernel_spmd as _run

    nc = _bacc.Bacc("TRN2", target_bir_lowering=False, num_devices=1)
    arrays, args = {}, []
    for name in _INS:
        a = _np.ascontiguousarray(inputs[name])
        arrays[f"in_{name}_dram"] = a
        args.append(nc.dram_tensor(f"in_{name}_dram", a.shape, _mybir.dt.from_np(a.dtype), kind="ExternalInput").ap())
    for i, (shape, dtype) in enumerate(_OUTS):
        dt = _mybir.dt.from_np(_np.dtype(dtype))
        args.append(nc.dram_tensor(f"out_{i}_dram", shape, dt, kind="ExternalOutput").ap())
    flamingo_kernel(nc, *args)
    r = _run(nc, [arrays], core_ids=[0])
    got = tuple(r.results[0][f"out_{i}_dram"] for i in range(len(_OUTS)))
    return got[0]
```

```python
import numpy as np
import concourse.bass as bass
from concourse import mybir
from contextlib import ExitStack

F32 = mybir.dt.float32
F32R = mybir.dt.float32r
U32 = mybir.dt.uint32
U8 = mybir.dt.uint8
ALU = mybir.AluOpType
ACT = mybir.ActivationFunctionType
AX = mybir.AxisListType

P = 128
EPS = 1e-5
MASKED = -1e30


class Arena:

    def __init__(self, nc, start, end):
        self.nc, self.at, self.end = nc, start, end

    def take(self, name, shape, dt, size=4):
        n = size
        for d in shape[1:]:
            n *= d
        t = self.nc.alloc_sbuf_tensor_at(name, shape, dt, offset=self.at)
        self.at += -(-n // 32) * 32
        assert self.at <= self.end, (name, self.at, self.end)
        return t


class Steps:

    def __init__(self, sem):
        self.sem, self.base, self.n = sem, 0, 0

    def did(self, ins):
        ins.then_inc(self.sem, 1)
        self.n += 1

    def value(self):
        return self.base + self.n

    def round(self, trip, per_trip):
        self.base, self.n, self.per_trip = trip * per_trip, 0, per_trip

    def round_over(self):
        assert self.n == self.per_trip, (self.n, self.per_trip)

    def enter(self, trip, per_trip):
        self.start = self.base + self.n
        self.per_trip = per_trip
        self.base, self.n = trip * per_trip + self.start, 0

    def leave(self, trips):
        assert self.n == self.per_trip, (self.n, self.per_trip)
        self.base, self.n = self.start + trips * self.per_trip, 0


def wait_if(eng, sem, value):
    if not isinstance(value, int) or value > 0:
        eng.wait_ge(sem, value)


def flamingo_kernel(nc, x, ctx, mask, g_xattn, g_ffn, W0, b0, Wg, Wu, Wd, gamma, beta, Wq, Wkv, Wout, wgate, We, be, out):
    B, S, D = x.shape
    KEYS = ctx.shape[1]
    KH = KEYS // 2
    NE0, _, F = Wg.shape
    INNER = Wq.shape[1]
    HD = 64
    HEADS = INNER // HD
    E = wgate.shape[1]
    T = B * S
    NT = T // P
    CT = 4
    CH = CT * P
    NC = NT // CT
    CB = S // CH
    CAP = T // E
    KB = D // P
    HF = F // 2
    FB = HF // P
    HB = INNER // P
    AK = B * KEYS
    HH = HEADS // 2
    HPB = 2
    T_PS, PT_PS, SC_PS, AV_PS = (0, 3), (1, 2), (4, 5), (6, 7)
    X2T_PS = ((0, 3), (0, 3), (1, 3), (6, 7))
    SIM = (2, 3, 4, 6)
    ROUTE_T = (5, 7)
    V_PS = (6, 7, 0, 1)
    WE_PS = (2, 3, 6)
    DROPPED = 4 * T
    assert KH * 2 == KEYS and KB == 2 and CB == 2 and CAP == 2 * P and HB == 4

    x_v = x.rearrange("b (t p) d -> p (b t) d", p=P)
    out_v = out.rearrange("b (t p) d -> p (b t) d", p=P)
    ctx_v = ctx.rearrange("b (k r) d -> r (b k) d", r=KH)
    Wg_v = Wg.rearrange("e (k p) f -> e p k f", p=P)
    Wu_v = Wu.rearrange("e (k p) f -> e p k f", p=P)
    Wd_v = Wd.rearrange("e (k p) d -> e p k d", p=P)
    We_v = We.rearrange("e (k p) h -> e p k h", p=P)
    ROW = 2 * D + 2
    R_XN, R_X, R_GATE, R_TOKEN = slice(0, D), slice(D, 2 * D), slice(2 * D, 2 * D + 1), slice(2 * D + 1, ROW)
    K_X, K_GATE, K_TOKEN = slice(0, D), slice(D, D + 1), slice(D + 1, D + 2)
    EB = 4
    slots = nc.dram_tensor("slots", [T, ROW], F32).ap()
    slots_v = slots.rearrange("(e k p) r -> e p k r", p=P, k=CAP // P)
    slots_kept_v = slots[:, D:ROW].rearrange("(e k p) r -> p e k r", p=P, k=CAP // P)
    out_rows = out.rearrange("b s d -> (b s) d")

    with ExitStack() as stack:
        def sem(name):
            return stack.enter_context(nc.semaphore(name))

        base = -(-nc.sbuf_base // 32) * 32
        end = nc.sbuf_usable_end // 32 * 32
        keep = Arena(nc, base, end)
        x_res = keep.take("x_res", [P, NT, D], F32)
        ident = keep.take("ident", [P, P], F32)
        before = keep.take("before", [P, P], F32)
        ones = keep.take("ones", [P, P], F32)
        ones_r = keep.take("ones_r", [1, P], F32R)
        A0 = keep.take("A0", [P, KB, AK], F32)
        r0 = keep.take("r0", [1, AK], F32)
        V0 = keep.take("V0", [KH, 2 * B, D], F32)
        ctxT = keep.take("ctxT", [P, KB, AK], F32)
        graw = keep.take("graw", [P, 4], F32)
        tg = keep.take("tg", [P, 4], F32)
        mhalf = keep.take("mhalf", [P, 8], F32)
        gammac = keep.take("gammac", [P, KB], F32)
        betac = keep.take("betac", [P, KB], F32)
        LANES = NC + 3
        LN_FRONT, LN_FRONT2, LN_ROUTE = range(NC, LANES)
        stats = [keep.take(f"stats{i}", [P, CT, 6], F32) for i in range(LANES)]
        mv = [keep.take(f"mv{i}", [P, CT, 2], F32) for i in range(LANES)]
        ve = [keep.take(f"ve{i}", [P, CT], F32) for i in range(LANES)]
        rstd = [keep.take(f"rstd{i}", [P, CT], F32) for i in range(LANES)]
        wgr = keep.take("wgr", [P, KB, E], F32)
        mask8 = keep.take("mask8", [P, AK], U8, size=1)
        maskf = keep.take("maskf", [P, AK], F32)
        mrow = keep.take("mrow", [1, B, HPB, KEYS], F32R)
        anyv = keep.take("anyv", [P, B], F32)
        ranyv = keep.take("ranyv", [P, B], F32)
        flag = keep.take("flag", [P, B], F32)
        tg_ffn = keep.take("tg_ffn", [P, 2], F32)
        desc = keep.take("desc", [P, CT, E], F32)
        slot0 = keep.take("slot0", [P, CT, E], F32)
        token_id = keep.take("token_id", [P, NT], U32)
        empty_row = keep.take("empty_row", [P, ROW], F32)
        chosen = keep.take("chosen", [P, E], F32)

        sa = Arena(nc, keep.at, end)
        W0s = sa.take("W0s", [P, KB, D], F32)
        W0T = sa.take("W0T", [P, KB, D], F32)
        bcol = sa.take("bcol", [P, KB], F32)
        ctx_s = sa.take("ctx_s", [KH, 2 * B, D], F32)
        k0T = sa.take("k0T", [P, KB, AK], F32)
        xnA = sa.take("xnA", [P, NT, D], F32)
        xnT = sa.take("xnT", [P, 2, KB, CH], F32)
        PA = sa.take("PA", [P, 2 * CT, KEYS], F32)
        PTA = sa.take("PTA", [KH, 2, 2, CH], F32)
        nmA, nmsA, denA, rdenA, coefA = (sa.take(n, [P, NT], F32) for n in ("nmA", "nmsA", "denA", "rdenA", "coefA"))

        sc = Arena(nc, keep.at, sa.at)
        Wkvs = sc.take("Wkvs", [P, KB, 2 * INNER], F32)
        Wqs = sc.take("Wqs", [P, KB, INNER], F32)
        Wouts = sc.take("Wouts", [P, HB, D], F32)
        k1T = sc.take("k1T", [P, HB, AK], F32)
        we_raw = [sc.take(f"we_raw{e}", [P, KB, D], F32) for e in range(E)]

        sb = Arena(nc, sa.at, end)
        acc = sb.take("acc", [P, KB, T], F32)
        xT_hi = sb.take("xT_hi", [P, KB, T], F32R)
        xT_lo = sb.take("xT_lo", [P, KB, T], F32R)
        raw_g = sb.take("raw_g", [P, KB, HF], F32)
        raw_u = sb.take("raw_u", [P, KB, HF], F32)
        raw_d = sb.take("raw_d", [P, FB, D], F32)
        wsplit = [{k: sb.take(f"w_{k}{i}", [P, FB, D] if k[0] == "d" else [P, KB, HF], F32R)
                   for k in ("g_hi", "g_lo", "u_hi", "u_lo", "d_hi", "d_lo")} for i in range(2)]
        silu = [sb.take(f"silu{i}", [P, CH], F32) for i in range(2)]
        hid = [sb.take(f"hid{i}", [P, CH], F32) for i in range(2)]
        hid_hi = [sb.take(f"hid_hi{i}", [P, CH], F32R) for i in range(2)]
        hid_lo = [sb.take(f"hid_lo{i}", [P, CH], F32R) for i in range(2)]

        sd = Arena(nc, sa.at + 4 * KB * T, end)
        weT = sd.take("weT", [P, E, KB, D], F32)
        be_all = sd.take("be_all", [P, E, D], F32)
        attention_at = sd.at
        V1 = sd.take("V1", [KH, 2 * B, INNER], F32)
        yc = sd.take("yc", [P, KB, CH], F32)
        xnC = sd.take("xnC", [P, CT, D], F32)
        xnC2 = sd.take("xnC2", [P, CT, D], F32)
        xnTc = sd.take("xnTc", [P, KB, CH], F32)
        qT = sd.take("qT", [P, HB, CH], F32)
        kcur = sd.take("kcur", [P, HB, KEYS], F32)
        vcur = sd.take("vcur", [KH, 2, INNER], F32)
        PC = [sd.take(f"PC{i}", [P, HEADS, KEYS], F32) for i in range(2)]
        PTC = sd.take("PTC", [KH, 2 * HEADS, P], F32)
        nmC = [sd.take(f"nmC{i}", [P, HEADS], F32) for i in range(2)]
        denC = [sd.take(f"denC{i}", [P, HEADS], F32) for i in range(2)]
        rdenC = [sd.take(f"rdenC{i}", [P, HEADS], F32) for i in range(2)]
        oT = sd.take("oT", [P, HB, P], F32)
        route_at = sd.at
        rows = sd.take("rows", [P, CT, ROW], F32)
        xn4T = sd.take("xn4T", [P, KB, CH], F32)
        rt = {k: sd.take(f"rt_{k}", [P, CT, E], F32) for k in
              ("d", "e", "p", "top", "score", "one", "before", "m1", "m2")}
        rs = {k: sd.take(f"rs_{k}", [P, CT], F32) for k in
              ("max", "sum", "rsum", "best", "loc", "first", "slot", "far")}
        rt_count = sd.take("rt_count", [P, E], F32)
        slot_c = sd.take("slot_c", [P, CT], U32)
        warm = sd.take("warm", [P, 1], F32)

        se = Arena(nc, attention_at, route_at)
        xe = [se.take(f"xe{i}", [P, CAP // P, D], F32) for i in range(EB)]
        xeT = [se.take(f"xeT{i}", [P, KB, CAP], F32) for i in range(EB)]
        kept = se.take("kept", [P, E, CAP // P, ROW - D], F32)
        yb = [se.take(f"yb{i}", [P, CAP // P, D], F32) for i in range(2)]
        ye = se.take("ye", [P, E, CAP // P, D], F32)

        bank = [stack.enter_context(nc.psum_tensor(f"bank{i}", [P, 512], F32)) for i in range(8)]

        x_in = [sem(f"x_in{u}") for u in range(NC)]
        ctx_in, w0_in, small_in, wc_in = (sem(n) for n in ("ctx_in", "w0_in", "small_in", "wc_in"))
        consts_ready, acc_zeroed = sem("consts_ready"), sem("acc_zeroed")
        tg_ready = sem("tg_ready")
        pool_steps, dve_steps = sem("pool_steps"), sem("dve_steps")
        prep_pe, prep_act, prep_dve = sem("prep_pe"), sem("prep_act"), sem("prep_dve")
        var_ready = [sem(f"var_ready{i}") for i in range(LANES)]
        rstd_ready = [sem(f"rstd_ready{i}") for i in range(LANES)]
        front_steps, ln4_steps, route_steps = sem("front_steps"), sem("ln4_steps"), sem("route_steps")
        a_ln1, a_xnT_ps, a_xnT, a_sc_ps, a_nmax, a_probs, a_pT_ps, a_pT, a_out_ps, a_res, a_ln2, a_x2T_ps = (
            sem(n) for n in ("a_ln1", "a_xnT_ps", "a_xnT", "a_sc_ps", "a_nmax", "a_probs", "a_pT_ps", "a_pT",
                             "a_out_ps", "a_res", "a_ln2", "a_x2T_ps"))
        xT_hi_ready, xT_lo_ready = sem("xT_hi_ready"), sem("xT_lo_ready")
        raw_in, raw_split, w_hi_ready = (sem(n) for n in ("raw_in", "raw_split", "w_hi_ready"))
        gate_ps, up_ps, silu_ready, hi_ready, lo_ready = (
            sem(n) for n in ("gate_ps", "up_ps", "silu_ready", "hi_ready", "lo_ready"))
        hid_ready = [sem(f"hid_ready{i}") for i in range(2)]
        down_done = [sem(f"down_done{i}") for i in range(2)]
        acc_added = [sem(f"acc_added{i}") for i in range(2)]
        c_prep_ps, c_prep_act, c_prep_dve = sem("c_prep_ps"), sem("c_prep_act"), sem("c_prep_dve")
        c_yT_ps, c_ln, c_xnT_ps, c_xnT, c_q_ps, c_q_act, c_q_dve, c_x2 = (
            sem(n) for n in ("c_yT_ps", "c_ln", "c_xnT_ps", "c_xnT", "c_q_ps", "c_q_act", "c_q_dve", "c_x2"))
        y_in, kcur_in, vcur_in = sem("y_in"), sem("kcur_in"), sem("vcur_in")
        c_sim_ps, c_nmax, c_probs, c_rden, c_norm, c_pT_ps, c_pT_act, c_pT_dve, c_o_ps, c_o, c_out_ps, c_res = (
            sem(n) for n in ("c_sim_ps", "c_nmax", "c_probs", "c_rden", "c_norm", "c_pT_ps", "c_pT_act", "c_pT_dve",
                             "c_o_ps", "c_o", "c_out_ps", "c_res"))
        r_ln, r_xnT_ps, r_xnT, r_logit_ps, r_shift, r_exp, r_one, r_loc_ps, r_loc_read, r_x, r_slot, scattered = (
            sem(n) for n in ("r_ln", "r_xnT_ps", "r_xnT", "r_logit_ps", "r_shift", "r_exp", "r_one", "r_loc_ps",
                             "r_loc_read", "r_x", "r_slot", "scattered"))
        e_wT_ps, e_wT, be_in = sem("e_wT_ps"), sem("e_wT"), sem("be_in")
        e_x_in, e_kept_in = [sem(f"e_x_in{i}") for i in range(EB)], [sem(f"e_kept_in{i}") for i in range(2)]
        e_xT_ps, e_xT, e_y_ps, e_yb, e_y = (sem(n) for n in ("e_xT_ps", "e_xT", "e_y_ps", "e_yb", "e_y"))
        x_stored, stored = sem("x_stored"), sem("stored")

        block = stack.enter_context(nc.Block())
        BLK = 2 * NC * FB
        HALFBLK = NC * FB
        UNITS = 2 * NC
        ZEROED = 16

        def batch_of(chunk):
            return chunk // CB

        def start_at_one(eng, sems):
            for s in sems:
                eng.sem_inc(s, 1)

        @block.sync
        def _(sp):
            for u in range(NC):
                sp.dma_start(x_res[:, u * CT:(u + 1) * CT, :], x_v[:, u * CT:(u + 1) * CT, :]).then_inc(x_in[u], 16)

            def load_half(e, half):
                f = slice(half * HF, (half + 1) * HF)
                sp.dma_start(raw_g[:], Wg_v[e, :, :, f]).then_inc(raw_in, 16)
                sp.dma_start(raw_u[:], Wu_v[e, :, :, f]).then_inc(raw_in, 16)
                sp.dma_start(raw_d[:], Wd_v[e, :, half * FB:(half + 1) * FB, :]).then_inc(raw_in, 16)

            load_half(0, 0)
            sp.wait_ge(xT_hi_ready, 4 * CB)
            sp.wait_ge(xT_lo_ready, 4 * CB)
            sp.dma_start(Wkvs[:], Wkv.rearrange("(k p) n -> p k n", p=P)).then_inc(wc_in, 16)
            sp.dma_start(Wqs[:], Wq.rearrange("(k p) n -> p k n", p=P)).then_inc(wc_in, 16)
            sp.dma_start(Wouts[:], Wout.rearrange("(k p) n -> p k n", p=P)).then_inc(wc_in, 16)
            for e in range(E):
                sp.dma_start(we_raw[e][:], We_v[e]).then_inc(wc_in, 16)
            with sp.Fori(0, NE0 - 1) as e:
                sp.wait_ge(raw_split, 2 * e + 1)
                load_half(e, 1)
                sp.wait_ge(raw_split, 2 * e + 2)
                load_half(e + 1, 0)
            sp.wait_ge(raw_split, 2 * NE0 - 1)
            load_half(NE0 - 1, 1)

            sp.wait_ge(acc_added[0], 1 + 4 * NE0)
            sp.wait_ge(acc_added[1], 1 + 4 * NE0)

            def expert_sums(f):
                if not isinstance(f, int) or f > 1:
                    sp.wait_ge(c_yT_ps, 2 * f)
                sp.dma_start(yc[:], acc[:, :, bass.ts(f, CH)]).then_inc(y_in, 16)

            def keys_and_values(chunk):
                b = batch_of(chunk)
                wait_if(sp, c_sim_ps, 2 * CT * chunk)
                sp.dma_start(kcur[:], k1T[:, :, bass.ts(b, KEYS)]).then_inc(kcur_in, 16)
                wait_if(sp, c_o_ps, CT * chunk)
                sp.dma_start(vcur[:], V1[:, bass.ts(b, 2), :]).then_inc(vcur_in, 16)

            def residual_out(chunk):
                sp.wait_ge(c_res, CT * (chunk + 1))
                sp.dma_start(out_v[:, bass.ts(chunk, CT), :], x_res[:, bass.ts(chunk, CT), :]).then_inc(x_stored, 16)

            expert_sums(1)
            sp.dma_start(be_all[:].rearrange("p e d -> p (e d)"),
                         be.rearrange("(a e) d -> a (e d)", a=1).partition_broadcast(P)).then_inc(be_in, 16)
            sp.wait_ge(c_prep_act, B + HB // 2)
            sp.wait_ge(c_prep_dve, B + HB // 2)
            keys_and_values(0)
            with sp.Fori(1, NC - 1) as c:
                expert_sums(c + 1)
                keys_and_values(c)
                residual_out(c - 1)
            keys_and_values(NC - 1)
            residual_out(NC - 2)
            residual_out(NC - 1)

            sp.wait_ge(scattered, ZEROED + 16 * NT)
            def load_group(g):
                for i in range(EB):
                    if g > 0:
                        sp.wait_ge(e_xT_ps, EB * (g - 1) + i + 1)
                    sp.dma_start(xe[i][:], slots_v[EB * g + i, :, :, R_XN]).then_inc(e_x_in[i], 16)
                    if g == 0 and i == 0:
                        sp.dma_start(kept[:, 0:EB], slots_kept_v[:, 0:EB]).then_inc(e_kept_in[0], 16)
                    if g == 0 and i == EB - 1:
                        sp.dma_start(kept[:, EB:E], slots_kept_v[:, EB:E]).then_inc(e_kept_in[1], 16)

            for g in range(E // EB):
                load_group(g)
            sp.wait_ge(x_stored, 16 * NC)

        @block.gpsimd
        def _(pool):
            steps = Steps(pool_steps)
            def wait_apart(s, value):
                if isinstance(value, int):
                    pool.wait_ge(s, value)
                else:
                    value = pool.to_reg(value)
                    pool.wait_ge(pool_steps, steps.value())
                    pool.wait_ge(s, value)

            steps.did(nc.gpsimd.memset(ident[:], 0.0))
            steps.did(nc.gpsimd.memset(before[:], 1.0))
            nc.gpsimd.memset(ones[:], 1.0)
            nc.gpsimd.memset(ones_r[:].bitcast(F32), 1.0)
            nc.gpsimd.memset(mhalf[:], -0.5)
            nc.gpsimd.memset(chosen[:], 0.0)
            nc.gpsimd.memset(empty_row[:], 0.0)
            nc.gpsimd.iota(token_id[:], pattern=[[P, NT]], base=0, channel_multiplier=1)
            for k in range(E):
                nc.gpsimd.memset(desc[:, :, k:k + 1], float(E - k))
                steps.did(nc.gpsimd.memset(slot0[:, :, k:k + 1], float(CAP * k)))
            pool.wait_ge(pool_steps, steps.value())
            nc.gpsimd.affine_select(out=ident[:], in_=ident[:], compare_op=ALU.not_equal, fill=1.0, base=0,
                                    pattern=[[-1, P]], channel_multiplier=1)
            nc.gpsimd.affine_select(out=before[:], in_=before[:], compare_op=ALU.is_gt, fill=0.0, base=0,
                                    pattern=[[1, P]], channel_multiplier=-1).then_inc(consts_ready, 1)

            def power(lane, n, count):
                pool.wait_ge(var_ready[lane], count)
                nc.gpsimd.tensor_tensor(out=rstd[lane][:, 0:n], in0=ve[lane][:, 0:n], in1=mhalf[:, 0:n],
                                        op=ALU.pow).then_inc(rstd_ready[lane], 1)

            def split(e, half, after_first=True):
                w = wsplit[half]
                pool.wait_ge(raw_in, 48 * (2 * e + half + 1))
                if half == 1:
                    wait_apart(down_done[1], 1 + e * (BLK // 2))
                elif after_first:
                    wait_apart(down_done[1], 1 + e * (BLK // 2) - HALFBLK // 2)
                nc.gpsimd.tensor_copy(w["g_hi"][:], raw_g[:])
                nc.gpsimd.tensor_copy(w["u_hi"][:], raw_u[:])
                nc.gpsimd.tensor_copy(w["d_hi"][:], raw_d[:]).then_inc(w_hi_ready, 1)
                pool.wait_ge(w_hi_ready, 2 * e + half + 1)
                nc.gpsimd.tensor_tensor(out=w["g_lo"][:], in0=raw_g[:], in1=w["g_hi"][:].bitcast(F32), op=ALU.subtract)
                nc.gpsimd.tensor_tensor(out=w["u_lo"][:], in0=raw_u[:], in1=w["u_hi"][:].bitcast(F32), op=ALU.subtract)
                nc.gpsimd.tensor_tensor(out=w["d_lo"][:], in0=raw_d[:], in1=w["d_hi"][:].bitcast(F32),
                                        op=ALU.subtract).then_inc(raw_split, 1)

            for u in range(NC):
                power(u, CT, 1)
            nc.gpsimd.memset(acc[:], 0.0).then_inc(acc_zeroed, 1)
            split(0, 0, after_first=False)
            for u in range(NC):
                power(u, CT, 2)
            pool.wait_ge(acc_zeroed, 1)
            nc.gpsimd.memset(empty_row[:, R_TOKEN].bitcast(U32), DROPPED).then_inc(acc_zeroed, 1)
            pool.wait_ge(acc_zeroed, 2)
            pool.dma_start(slots.rearrange("(n p) r -> p n r", p=P), empty_row[:].unsqueeze(1).to_broadcast([P, NT, ROW])).then_inc(scattered, ZEROED)
            with pool.Fori(0, NE0 - 1) as e:
                split(e, 1)
                split(e + 1, 0)
            split(NE0 - 1, 1)

            def normalise(c, j):
                for half in range(2):
                    heads = slice(half * HH, (half + 1) * HH)
                    pool.wait_ge(c_rden, 2 * (c * CT + j) + half + 1)
                    nc.gpsimd.tensor_tensor(out=PC[j % 2][:, heads, :], in0=PC[j % 2][:, heads, :],
                                            in1=rdenC[j % 2][:, heads].unsqueeze(2).to_broadcast([P, HH, KEYS]),
                                            op=ALU.mult).then_inc(c_norm, 1)

            def scatter(r):
                wait_apart(r_x, r + 1)
                wait_apart(r_slot, r + 1)
                for j in range(CT):
                    pool.indirect_dma_start(out=slots, out_offset=bass.IndirectOffsetOnAxis(ap=slot_c[:, j:j + 1], axis=0),
                                            in_=rows[:, j, :], in_offset=None, bounds_check=T - 1,
                                            oob_is_err=False).then_inc(scattered, 16)

            def chunk(c, front, route):
                normalise(c, 0)
                normalise(c, 1)
                if front:
                    power(LN_FRONT, CT, c + 2)
                normalise(c, 2)
                normalise(c, 3)
                if front:
                    power(LN_FRONT2, CT, c + 2)
                if route:
                    scatter(c - 1)
                power(LN_ROUTE, CT, c + 1)

            pool.wait_ge(scattered, ZEROED)
            power(LN_FRONT, CT, 1)
            power(LN_FRONT2, CT, 1)
            chunk(0, front=True, route=False)
            with pool.Fori(1, NC - 1) as c:
                chunk(c, front=True, route=True)
            chunk(NC - 1, front=False, route=True)
            scatter(NC - 1)

            pool.wait_ge(x_stored, 16 * NC)
            for e in range(E):
                pool.wait_ge(e_y, e + 1)
                for s in range(CAP // P):
                    pool.indirect_dma_start(out=out_rows,
                                            out_offset=bass.IndirectOffsetOnAxis(ap=kept[:, e, s, K_TOKEN].bitcast(U32), axis=0),
                                            in_=ye[:, e, s, :], in_offset=None, bounds_check=T - 1,
                                            oob_is_err=False).then_inc(stored, 16)
            pool.wait_ge(stored, 16 * NT)

        @block.scalar
        def _(act):
            act.dma_start(ctx_s[:], ctx_v).then_inc(ctx_in, 16)
            act.dma_start(W0s[:], W0.rearrange("(k p) e -> p k e", p=P)).then_inc(w0_in, 16)
            act.dma_start(bcol[:], b0.rearrange("(k p) -> p k", p=P), allow_slow_non_contiguous=True).then_inc(w0_in, 16)
            act.dma_start(graw[:, 0:2], g_xattn.rearrange("(a g) -> a g", a=1).partition_broadcast(P)).then_inc(small_in, 16)
            act.dma_start(graw[:, 2:4], g_ffn.rearrange("(a g) -> a g", a=1).partition_broadcast(P)).then_inc(small_in, 16)
            act.dma_start(gammac[:], gamma.rearrange("(k p) -> p k", p=P), allow_slow_non_contiguous=True).then_inc(small_in, 16)
            act.dma_start(betac[:], beta.rearrange("(k p) -> p k", p=P), allow_slow_non_contiguous=True).then_inc(small_in, 16)
            act.dma_start(wgr[:], wgate.rearrange("(k p) e -> p k e", p=P)).then_inc(small_in, 16)
            act.dma_start(mask8[:], mask.rearrange("(a b) k -> a (b k)", a=1).partition_broadcast(P)).then_inc(small_in, 16)
            act.wait_ge(small_in, 96)
            nc.scalar.activation(tg[:], graw[:], ACT.Tanh).then_inc(tg_ready, 1)

            act.wait_ge(prep_pe, 1)
            nc.scalar.copy(W0T[:].rearrange("p k d -> p (k d)"), bank[0][:]).then_inc(prep_act, 1)
            act.wait_ge(prep_pe, 2)
            nc.scalar.copy(ctxT[:, 0, :], bank[1][:, 0:AK]).then_inc(prep_act, 1)
            def a_xnT_out(u):
                for k in range(KB):
                    act.wait_ge(a_xnT_ps, KB * u + k + 1)
                    nc.scalar.copy(xnT[:, u % 2, k, :], bank[T_PS[k]][:]).then_inc(a_xnT, 1)

            def a_exps(u):
                act.wait_ge(a_nmax, u + 1)
                for j in range(CT):
                    n = u * CT + j
                    ins = nc.scalar.activation(PA[:, u % 2 * CT + j, :], bank[SC_PS[j // 2]][:, j % 2 * 256:j % 2 * 256 + KEYS], ACT.Exp,
                                               bias=nmsA[:, n:n + 1], scale=D ** -0.5, accum_out=denA[:, n:n + 1])
                ins.then_inc(a_probs, 1)

            def a_pT_out(u):
                for k in range(2):
                    act.wait_ge(a_pT_ps, 2 * u + k + 1)
                    nc.scalar.copy(PTA[:, u % 2, k, :], bank[PT_PS[k]][0:KH, :]).then_inc(a_pT, 1)

            def xT_hi_out(u):
                for k in range(KB):
                    act.wait_ge(a_x2T_ps, KB * u + k + 1)
                    nc.scalar.copy(xT_hi[:, k, u * CH:(u + 1) * CH], bank[X2T_PS[u][k]][:]).then_inc(xT_hi_ready, 1)

            a_xnT_out(0)
            for i in range(2):
                act.wait_ge(prep_pe, 6 + i)
                nc.scalar.copy(V0[:, 2 * i:2 * i + 2, :].rearrange("p k d -> p (k d)"), bank[5 + i][0:KH, :]).then_inc(prep_act, 1)

            a_xnT_out(1)
            for u in range(NC):
                a_exps(u)
                a_pT_out(u)
                if u + 2 < NC:
                    a_xnT_out(u + 2)
                if u >= 2:
                    xT_hi_out(u - 2)
            xT_hi_out(NC - 2)
            xT_hi_out(NC - 1)

            with act.Fori(0, NE0) as e:
                for k in range(BLK):
                    act.wait_ge(gate_ps, e * BLK + k + 1)
                    act.wait_ge(hid_ready[k % 2], 1 + e * (BLK // 2) + k // 2)
                    nc.scalar.activation(silu[k % 2][:], bank[k % 2][:], ACT.Silu).then_inc(silu_ready, 1)

            def xnT_out(f):
                for k in range(KB):
                    act.wait_ge(c_xnT_ps, KB * f + k + 1)
                    nc.scalar.activation(xnTc[:, k, :], bank[k][:], ACT.Identity, bias=betac[:, k:k + 1],
                                         scale=gammac[:, k:k + 1]).then_inc(c_xnT, 1)

            def q_out(f):
                for m in range(0, HB, 2):
                    act.wait_ge(c_q_ps, HB * f + m + 1)
                    nc.scalar.mul(qT[:, m, :], bank[SIM[m]][:], HD ** -0.5).then_inc(c_q_act, 1)

            def exps(c, j, half):
                t = c * CT + j
                act.wait_ge(c_nmax, 2 * t + half + 1)
                wait_if(act, c_pT_ps, 4 * (t - 1))
                for h in range(half * HH, (half + 1) * HH):
                    a = h // 2 % HPB
                    ins = nc.scalar.activation(PC[j % 2][:, h, :], bank[SIM[h // HH * 2 + h % 2]][:, a * KEYS:(a + 1) * KEYS], ACT.Exp,
                                               bias=nmC[j % 2][:, h:h + 1], accum_out=denC[j % 2][:, h:h + 1])
                ins.then_inc(c_probs, 1)

            def pT_out(c, j, g):
                act.wait_ge(c_pT_ps, 4 * (c * CT + j) + g + 1)
                nc.scalar.copy(PTC[:, 4 * g:4 * g + 4, :].rearrange("p a b -> p (a b)"), bank[0][0:KH, :]).then_inc(c_pT_act, 1)

            def xn4T_out(r):
                for k in range(KB):
                    act.wait_ge(r_xnT_ps, KB * r + k + 1)
                    nc.scalar.copy(xn4T[:, k, :], bank[ROUTE_T[k]][:]).then_inc(r_xnT, 1)

            def x_rows(r):
                act.wait_ge(c_res, CT * (r + 1))
                act.wait_ge(scattered, ZEROED + 16 * CT * r)
                nc.scalar.copy(rows[:, :, R_X], x_res[:, bass.ts(r, CT), :]).then_inc(r_x, 1)

            def route_exp(r):
                act.wait_ge(r_shift, r + 1)
                nc.scalar.activation(rt["e"][:], rt["d"][:], ACT.Exp).then_inc(r_exp, 1)

            def chunk(c, front, route):
                f, r = c + 1, c - 1
                if route:
                    xn4T_out(r)
                for j in range(CT - 1):
                    exps(c, j + 1, 0)
                    pT_out(c, j, 0)
                    exps(c, j + 1, 1)
                    pT_out(c, j, 2)
                    if route and j == 1:
                        route_exp(r)
                pT_out(c, CT - 1, 0)
                pT_out(c, CT - 1, 2)
                if front:
                    xnT_out(f)
                    q_out(f)
                    exps(f, 0, 0)
                    exps(f, 0, 1)
                x_rows(c)

            for m in range(0, HB, 2):
                act.wait_ge(c_prep_ps, m + 1)
                nc.scalar.copy(k1T[:, m, :], bank[m][:, 0:AK]).then_inc(c_prep_act, 1)
            for r in range(0, 2 * B, 2):
                act.wait_ge(c_prep_ps, HB + r + 1)
                nc.scalar.copy(V1[:, r, :], bank[V_PS[r]][0:KH, :]).then_inc(c_prep_act, 1)
            for e in range(E):
                act.wait_ge(e_wT_ps, e + 1)
                nc.scalar.copy(weT[:, e, :, :].rearrange("p k d -> p (k d)"), bank[WE_PS[e % len(WE_PS)]][:]).then_inc(e_wT, 1)
            nc.scalar.activation(warm[:], tg[:, 0:1], ACT.Exp)
            xnT_out(0)
            q_out(0)
            exps(0, 0, 0)
            exps(0, 0, 1)
            chunk(0, front=True, route=False)
            with act.Fori(1, NC - 1) as c:
                chunk(c, front=True, route=True)
            chunk(NC - 1, front=False, route=True)
            xn4T_out(NC - 1)
            route_exp(NC - 1)

            with act.Fori(0, E // EB) as p:
                for i in range(EB):
                    act.wait_ge(e_xT_ps, EB * p + i + 1)
                    nc.scalar.copy(xeT[i][:].rearrange("p k s -> p (k s)"), bank[i][:]).then_inc(e_xT, 1)

        @block.tensor
        def _(pe):
            start_at_one(pe, down_done)
            mm, tr = nc.tensor.matmul, nc.tensor.transpose

            pe.wait_ge(consts_ready, 1)
            pe.wait_ge(w0_in, 32)
            for k in range(KB):
                for m in range(KB):
                    ins = tr(bank[0][:, k * D + m * P:k * D + (m + 1) * P], W0s[:, m, k * P:(k + 1) * P], ident[:])
            ins.then_inc(prep_pe, 1)
            pe.wait_ge(ctx_in, 16)
            for k in range(KB):
                for r in range(2 * B):
                    ins = tr(bank[1 + k][:, r * KH:(r + 1) * KH], ctx_s[:, r, k * P:(k + 1) * P], ident[0:KH, 0:KH])
                ins.then_inc(prep_pe, 1)
            pe.wait_ge(prep_act, 2)
            pe.wait_ge(prep_dve, 1)
            for m in range(KB):
                for k in range(KB):
                    ins = mm(bank[3 + m][:, 0:AK], W0T[:, k, m * P:(m + 1) * P], ctxT[:, k, :], start=k == 0, stop=k == KB - 1)
                ins.then_inc(prep_pe, 1)
            def transpose_chunk(src, banks, src_tile, signal):
                for k in range(KB):
                    for j in range(CT):
                        ins = tr(bank[banks[k]][:, j * P:(j + 1) * P], src[:, src_tile + j, k * P:(k + 1) * P], ident[:])
                    ins.then_inc(signal, 1)

            def x1_transposes(u):
                wait_if(pe, a_xnT, KB * u)
                pe.wait_ge(a_ln1, u + 1)
                transpose_chunk(xnA, T_PS, u * CT, a_xnT_ps)

            pe.wait_ge(prep_dve, 3)
            x1_transposes(0)
            for i in range(2):
                for r in range(2):
                    for m in range(KB):
                        ins = tr(bank[5 + i][0:KH, r * D + m * P:r * D + (m + 1) * P],
                                 k0T[:, m, (2 * i + r) * KH:(2 * i + r + 1) * KH], ident[:])
                ins.then_inc(prep_pe, 1)
            for k in range(KB):
                for m in range(KB):
                    ins = mm(bank[1 + k][:, 0:AK], W0s[:, m, k * P:(k + 1) * P], k0T[:, m, :], start=m == 0, stop=m == KB - 1)
                ins.then_inc(prep_pe, 1)
            for m in range(KB):
                ins = mm(bank[7][0:1, 0:AK], bcol[:, m:m + 1], k0T[:, m, :], start=m == 0, stop=m == KB - 1)
            ins.then_inc(prep_pe, 1)
            def a_scores(u):
                b = u // CB
                wait_if(pe, a_probs, u)
                pe.wait_ge(a_xnT, KB * u + KB)
                for j in range(CT):
                    sco = bank[SC_PS[j // 2]][:, j % 2 * 256:j % 2 * 256 + KEYS]
                    ks = slice(b * KEYS, (b + 1) * KEYS)
                    for k in range(KB):
                        mm(sco, xnT[:, u % 2, k, j * P:(j + 1) * P], A0[:, k, ks], start=k == 0, stop=False)
                    ins = mm(sco, ones[0:1, :], r0[:, ks], start=False, stop=True)
                    if j % 2:
                        ins.then_inc(a_sc_ps, 1)

            def a_p_transposes(u):
                pe.wait_ge(a_probs, u + 1)
                for k in range(2):
                    for j in range(CT):
                        ins = tr(bank[PT_PS[k]][0:KH, j * P:(j + 1) * P], PA[:, u % 2 * CT + j, k * KH:(k + 1) * KH], ident[:])
                    ins.then_inc(a_pT_ps, 1)

            def a_attend(u):
                pe.wait_ge(a_pT, 2 * u + 2)
                wait_if(pe, a_res, u)
                for j in range(CT):
                    for k in range(2):
                        ins = mm(bank[AV_PS[j // 2]][:, j % 2 * D:(j % 2 + 1) * D], PTA[:, u % 2, k, j * P:(j + 1) * P],
                                 V0[:, u // CB * 2 + k, :], start=k == 0, stop=k == 1)
                    if j % 2:
                        ins.then_inc(a_out_ps, 1)

            def x2_transposes(u):
                pe.wait_ge(a_xnT, KB * NC)
                wait_if(pe, xT_lo_ready, KB * min(u, NC - 2))
                pe.wait_ge(a_ln2, u + 1)
                transpose_chunk(xnA, X2T_PS[u], u * CT, a_x2T_ps)

            x1_transposes(1)
            pe.wait_ge(prep_act, 4)
            pe.wait_ge(prep_dve, 6)
            a_scores(0)
            for u in range(NC):
                a_p_transposes(u)
                if u + 2 < NC:
                    x1_transposes(u + 2)
                else:
                    x2_transposes(u - 2)
                if u + 1 < NC:
                    a_scores(u + 1)
                a_attend(u)
            x2_transposes(NC - 2)

            def three(pairs, ps, start, stop):
                n = 0
                for w_hi, w_lo, a_hi, a_lo in pairs:
                    for w, a in ((w_hi, a_hi), (w_hi, a_lo), (w_lo, a_hi)):
                        n += 1
                        ins = mm(ps, w, a, start=start and n == 1, stop=stop and n == 3 * len(pairs))
                return ins

            def gate_up(e, k):
                half, chunk, f = k // HALFBLK, k % HALFBLK // FB, k % FB
                w = wsplit[half]
                fs, ts = slice(f * P, (f + 1) * P), slice(chunk * CH, (chunk + 1) * CH)
                if k == 1:
                    pe.wait_ge(xT_lo_ready, KB * (NC - 1))
                if k == FB:
                    pe.wait_ge(xT_lo_ready, KB * NC)
                if k % HALFBLK == 0:
                    pe.wait_ge(raw_split, 2 * e + half + 1)
                pe.wait_ge(hid_ready[k % 2], 1 + e * (BLK // 2) + k // 2)
                for hi, lo, ps, signal in (("g_hi", "g_lo", bank[k % 2], gate_ps), ("u_hi", "u_lo", bank[2 + k % 2], up_ps)):
                    three([(w[hi][:, d, fs], w[lo][:, d, fs], xT_hi[:, d, ts], xT_lo[:, d, ts]) for d in range(KB)],
                          ps[:], True, True).then_inc(signal, 1)

            def down(e, k):
                half, f, u = k // HALFBLK, k % FB, k // FB
                w = wsplit[half]
                if f == 0:
                    pe.wait_ge(acc_added[u % 2], 1 + e * (UNITS // 2) + u // 2)
                ps = [bank[4 + 2 * (u % 2) + m] for m in range(KB)]
                hs = [slice(m * P, (m + 1) * P) for m in range(KB)]
                pe.wait_ge(hi_ready, e * BLK + k + 1)
                for m in range(KB):
                    mm(ps[m][:], w["d_hi"][:, f, hs[m]], hid_hi[k % 2][:], start=f == 0, stop=False)
                for m in range(KB):
                    mm(ps[m][:], w["d_lo"][:, f, hs[m]], hid_hi[k % 2][:], start=False, stop=False)
                pe.wait_ge(lo_ready, e * BLK + k + 1)
                mm(ps[0][:], w["d_hi"][:, f, hs[0]], hid_lo[k % 2][:], start=False, stop=f == FB - 1)
                ins = mm(ps[1][:], w["d_hi"][:, f, hs[1]], hid_lo[k % 2][:], start=False, stop=f == FB - 1)
                ins.then_inc(down_done[k % 2], 1)

            pe.wait_ge(xT_lo_ready, KB * (NC - 2))
            gate_up(0, 0)
            x2_transposes(NC - 1)
            with pe.Fori(0, NE0) as e:
                for k in range(BLK):
                    if k + 1 < BLK:
                        gate_up(e, k + 1)
                    else:
                        with pe.If(e < NE0 - 1):
                            gate_up(e + 1, 0)
                    down(e, k)

            pe.wait_ge(wc_in, 48)
            for m in range(HB):
                for k in range(KB):
                    ins = mm(bank[m][:, 0:AK], Wkvs[:, k, m * P:(m + 1) * P], ctxT[:, k, :], start=k == 0, stop=k == KB - 1)
                ins.then_inc(c_prep_ps, 1)
            def y_transposes(sums, first, banks):
                for j in range(CT):
                    for m in range(KB):
                        ins = tr(bank[banks[j // 2]][:, j % 2 * D + m * P:j % 2 * D + (m + 1) * P],
                                 sums[:, m, first + j * P:first + (j + 1) * P], ident[:])
                    if j % 2:
                        ins.then_inc(c_yT_ps, 1)

            def queries(f):
                for m in range(HB):
                    for k in range(KB):
                        ins = mm(bank[SIM[m]][:], Wqs[:, k, m * P:(m + 1) * P], xnTc[:, k, :], start=k == 0, stop=k == KB - 1)
                    ins.then_inc(c_q_ps, 1)

            def wait_apart(s, value):
                if not isinstance(value, int):
                    value = pe.to_reg(value)
                pe.wait_ge(consts_ready, 1)
                pe.wait_ge(s, value)

            def scores(c, j, half):
                b = batch_of(c)
                mask_row = mrow[:, bass.ds(b, 1), :, :].rearrange("p b a k -> p (b a k)")
                banks = SIM[2 * half:2 * half + 2]
                for s in banks:
                    mm(bank[s][:, 0:HPB * KEYS], ones_r[:], mask_row, start=True, stop=False)
                for a in range(HPB):
                    ks = slice(a * KEYS, (a + 1) * KEYS)
                    for i, s in enumerate(banks):
                        h = half * HH + 2 * a + i
                        r = slice(h % 2 * HD, (h % 2 + 1) * HD)
                        ins = mm(bank[s][:, ks], qT[r, h // 2, j * P:(j + 1) * P], kcur[r, h // 2, :], start=False, stop=a == HPB - 1)
                ins.then_inc(c_sim_ps, 1)

            def scores_after_queries(c):
                wait_apart(kcur_in, 16 * c + 16)
                for half in range(2):
                    wait_apart(c_q_act, 2 * c + half + 1)
                    pe.wait_ge(c_q_dve, 2 * c + half + 1)
                    scores(c, 0, half)

            def scores_after_exps(c, j):
                for half in range(2):
                    wait_apart(c_probs, 2 * (c * CT + j - 1) + half + 1)
                    scores(c, j, half)

            def p_transposes(c, j, groups):
                t = c * CT + j
                pe.wait_ge(c_norm, 2 * t + groups[0] // 2 + 1)
                for g in groups:
                    if g >= 2:
                        pe.wait_ge(c_pT_act if g % 2 == 0 else c_pT_dve, 2 * t + 1)
                    for a in range(4):
                        n = 4 * g + a
                        ins = tr(bank[g % 2][0:KH, a * P:(a + 1) * P], PC[j % 2][:, n // 2, n % 2 * KH:(n % 2 + 1) * KH], ident[:])
                    ins.then_inc(c_pT_ps, 1)

            def attend(c, j):
                t = c * CT + j
                if j == 0:
                    pe.wait_ge(vcur_in, 16 * c + 16)
                for g in range(4):
                    pe.wait_ge(c_pT_act if g % 2 == 0 else c_pT_dve, 2 * t + 1 + g // 2)
                    for h in (2 * g, 2 * g + 1):
                        for k in range(2):
                            ins = mm(bank[5][h % 2 * HD:(h % 2 + 1) * HD, h // 2 * P:(h // 2 + 1) * P],
                                     vcur[:, k, h * HD:(h + 1) * HD], PTC[:, 2 * h + k, :], start=k == 0, stop=k == 1)
                ins.then_inc(c_o_ps, 1)

            def project(c, j):
                t = c * CT + j
                pe.wait_ge(c_o, t + 1)
                wait_if(pe, c_res, t)
                for k in range(HB):
                    ins = mm(bank[7][:, 0:D], oT[:, k, :], Wouts[:, k, :], start=k == 0, stop=k == HB - 1)
                ins.then_inc(c_out_ps, 1)

            def route_transposes(r):
                pe.wait_ge(r_ln, r + 1)
                transpose_chunk(rows, ROUTE_T, 0, r_xnT_ps)

            def logits(r, tile):
                pe.wait_ge(r_xnT, 2 * r + 2)
                for j in tile:
                    for k in range(KB):
                        ins = mm(bank[7][:, D + j * E:D + (j + 1) * E], xn4T[:, k, j * P:(j + 1) * P], wgr[:, k, :], start=k == 0, stop=k == KB - 1)
                    ins.then_inc(r_logit_ps, 1)

            def locations(r):
                pe.wait_ge(r_one, r + 1)
                at = D + CT * E
                mm(bank[7][:, at:at + CT * E], before[:], rt["one"][:].rearrange("p j e -> p (j e)"), start=True, stop=False)
                for j in range(1, CT):
                    mm(bank[7][:, at + j * E:at + CT * E], ones[:], rt["one"][:, 0:CT - j, :].rearrange("p j e -> p (j e)"), start=False, stop=False)
                mm(bank[7][:, at:at + CT * E], ones[:], rt["before"][:].rearrange("p j e -> p (j e)"), start=False, stop=True).then_inc(r_loc_ps, 1)

            def chunk(c, front, route):
                f, r = c + 1, c - 1
                if front:
                    pe.wait_ge(y_in, 16 * f)
                    y_transposes(yc, 0, (0, 1))
                if route:
                    route_transposes(r)
                scores_after_exps(c, 1)
                if front:
                    pe.wait_ge(c_x2, f + 1)
                p_transposes(c, 0, (0, 1))
                if route:
                    logits(r, (0,))
                p_transposes(c, 0, (2, 3))
                if route:
                    logits(r, (1,))
                attend(c, 0)
                if route:
                    logits(r, (2,))
                scores_after_exps(c, 2)
                if route:
                    logits(r, (3,))
                p_transposes(c, 1, (0, 1))
                if route:
                    pe.wait_ge(r_shift, r + 1)
                project(c, 0)
                p_transposes(c, 1, (2, 3))
                attend(c, 1)
                scores_after_exps(c, 3)
                p_transposes(c, 2, (0, 1))
                project(c, 1)
                p_transposes(c, 2, (2, 3))
                if route:
                    pe.wait_ge(c_res, c * CT + 2)
                    locations(r)
                attend(c, 2)
                p_transposes(c, 3, (0, 1))
                if route:
                    pe.wait_ge(r_loc_read, r + 1)
                project(c, 2)
                p_transposes(c, 3, (2, 3))
                attend(c, 3)
                if front:
                    pe.wait_ge(c_ln, f + 1)
                    transpose_chunk(xnC2, (0, 1), 0, c_xnT_ps)
                project(c, 3)
                if front:
                    pe.wait_ge(c_probs, 2 * CT * f)
                    pe.wait_ge(c_xnT, 2 * f + 2)
                    queries(f)
                    scores_after_queries(f)

            pe.wait_ge(acc_added[0], 1 + 4 * NE0)
            pe.wait_ge(acc_added[1], 1 + 4 * NE0)
            y_transposes(acc, 0, (4, 5))
            for r in range(2 * B):
                if r == 2:
                    pe.wait_ge(c_prep_act, 1)
                    pe.wait_ge(c_prep_dve, 1)
                for k in range(KB):
                    ins = mm(bank[V_PS[r]][0:KH, :], ctxT[:, k, r * KH:(r + 1) * KH], Wkvs[:, k, INNER:2 * INNER],
                             start=k == 0, stop=k == KB - 1)
                ins.then_inc(c_prep_ps, 1)
            pe.wait_ge(c_prep_act, B + HB // 2)
            pe.wait_ge(c_prep_dve, B + HB // 2)
            pe.wait_ge(wc_in, 16 * (3 + E))
            for e in range(E):
                n = len(WE_PS)
                if e >= n:
                    pe.wait_ge(e_wT, e - n + 1)
                for k in range(KB):
                    for m in range(KB):
                        ins = tr(bank[WE_PS[e % n]][:, k * D + m * P:k * D + (m + 1) * P], we_raw[e][:, m, k * P:(k + 1) * P], ident[:])
                ins.then_inc(e_wT_ps, 1)
            pe.wait_ge(e_wT, E)
            pe.wait_ge(c_ln, 1)
            transpose_chunk(xnC2, (0, 1), 0, c_xnT_ps)
            pe.wait_ge(c_xnT, 2)
            queries(0)
            scores_after_queries(0)
            chunk(0, front=True, route=False)
            with pe.Fori(1, NC - 1) as c:
                chunk(c, front=True, route=True)
            chunk(NC - 1, front=False, route=True)
            route_transposes(NC - 1)
            logits(NC - 1, range(CT))
            locations(NC - 1)

            with pe.Fori(0, E // EB) as p:
                def slot_transposes(i):
                    pe.wait_ge(e_x_in[i], 16 * p + 16)
                    for k in range(KB):
                        for s in range(CAP // P):
                            ins = tr(bank[i][:, k * CAP + s * P:k * CAP + (s + 1) * P], xe[i][:, s, k * P:(k + 1) * P], ident[:])
                    ins.then_inc(e_xT_ps, 1)

                slot_transposes(0)
                for i in range(EB):
                    if i + 1 < EB:
                        slot_transposes(i + 1)
                    pe.wait_ge(e_yb, EB * p + i + 1)
                    pe.wait_ge(e_xT, EB * p + i + 1)
                    for s in range(CAP // P):
                        for k in range(KB):
                            ins = mm(bank[4 + i][:, s * D:(s + 1) * D], xeT[i][:, k, s * P:(s + 1) * P],
                                     weT[:, bass.ds(EB * p + i, 1), k, :].rearrange("p a d -> p (a d)"), start=k == 0, stop=k == KB - 1)
                    ins.then_inc(e_y_ps, 1)

        @block.vector
        def _(dve):
            start_at_one(dve, [*hid_ready, *acc_added])
            dve.sem_inc(e_yb, EB)
            steps = Steps(dve_steps)

            front, ln4, route = Steps(front_steps), Steps(ln4_steps), Steps(route_steps)

            def own(done=steps):
                dve.wait_ge(done.sem, done.value())

            def wait_apart(s, value):
                if isinstance(value, int):
                    dve.wait_ge(s, value)
                else:
                    value = dve.to_reg(value)
                    dve.wait_ge(consts_ready, 1)
                    dve.wait_ge(s, value)

            def variances(srcs, lane, done):
                n = len(srcs)
                for i, s in enumerate(srcs):
                    ins = nc.vector.bn_stats(stats[lane][:, i, :], s)
                done.did(ins)
                wait_apart(done.sem, done.value())
                for i in range(n):
                    ins = nc.vector.bn_aggr(mv[lane][:, i, :], stats[lane][:, i, :])
                done.did(ins)
                own(done)
                nc.vector.tensor_scalar(ve[lane][:, 0:n], mv[lane][:, 0:n, 1], EPS, None, ALU.add).then_inc(var_ready[lane], 1)

            def normed(srcs, dsts, lane, count):
                dve.wait_ge(rstd_ready[lane], count)
                for i in range(len(srcs)):
                    ins = nc.vector.tensor_scalar(dsts[i], srcs[i], mv[lane][:, i, 0:1], rstd[lane][:, i:i + 1], ALU.subtract, ALU.mult)
                return ins

            def tiles(first, n):
                return [x_res[:, bass.ds(first + i, 1), :].rearrange("p a d -> p (a d)") for i in range(n)]

            def unit(u):
                return tiles(u * CT, CT)

            def unit_norms(u):
                return [xnA[:, u * CT + j, :] for j in range(CT)]

            def ln1_variances(u):
                dve.wait_ge(x_in[u], 16)
                variances(unit(u), u, steps)

            def ln1_normed(u):
                normed(unit(u), unit_norms(u), u, 1).then_inc(a_ln1, 1)

            def ln2_variances(u):
                dve.wait_ge(a_res, u + 1)
                variances(unit(u), u, steps)

            def ln2_normed(u):
                dve.wait_ge(a_xnT_ps, KB * u + KB)
                normed(unit(u), unit_norms(u), u, 2).then_inc(a_ln2, 1)

            ln1_variances(0)
            ln1_variances(1)
            ln1_normed(0)
            dve.wait_ge(prep_pe, 3)
            nc.vector.tensor_copy(ctxT[:, 1, :], bank[2][:, 0:AK]).then_inc(prep_dve, 1)
            ln1_normed(1)
            dve.wait_ge(w0_in, 32)
            for m in range(KB):
                dve.wait_ge(prep_pe, 4 + m)
                nc.vector.tensor_scalar(k0T[:, m, :], bank[3 + m][:, 0:AK], bcol[:, m:m + 1], None, ALU.add).then_inc(prep_dve, 1)
                if m == 0:
                    ln1_variances(2)
            ln1_variances(3)
            ln1_normed(2)
            for k in range(KB):
                dve.wait_ge(prep_pe, 8 + k)
                nc.vector.tensor_copy(A0[:, k, :], bank[1 + k][:, 0:AK]).then_inc(prep_dve, 1)
            dve.wait_ge(prep_pe, 10)
            nc.vector.tensor_copy(r0[:], bank[7][0:1, 0:AK]).then_inc(prep_dve, 1)
            ln1_normed(3)

            def a_maxes(u):
                for i in range(2):
                    dve.wait_ge(a_sc_ps, 2 * u + i + 1)
                    n = u * CT + 2 * i
                    ins = nc.vector.reduce_max(nmA[:, n:n + 2], bank[SC_PS[i]][:].rearrange("p (a k) -> p a k", a=2)[:, :, 0:KEYS],
                                               AX.X, negate=True)
                steps.did(ins)
                own()
                us = slice(u * CT, (u + 1) * CT)
                nc.vector.tensor_scalar(nmsA[:, us], nmA[:, us], D ** -0.5, None, ALU.mult).then_inc(a_nmax, 1)

            def a_add(u):
                us = slice(u * CT, (u + 1) * CT)
                dve.wait_ge(a_probs, u + 1)
                steps.did(nc.vector.reciprocal(rdenA[:, us], denA[:, us]))
                own()
                steps.did(nc.vector.tensor_scalar(coefA[:, us], rdenA[:, us], tg[:, 0:1], None, ALU.mult))
                own()
                for j, x in enumerate(unit(u)):
                    dve.wait_ge(a_out_ps, 2 * u + j // 2 + 1)
                    ins = nc.vector.scalar_tensor_tensor(out=x, in0=bank[AV_PS[j // 2]][:, j % 2 * D:(j % 2 + 1) * D],
                                                         scalar=coefA[:, u * CT + j:u * CT + j + 1], in1=x, op0=ALU.mult, op1=ALU.add)
                ins.then_inc(a_res, 1)

            def xT_lo_out(u):
                for k in range(KB):
                    dve.wait_ge(xT_hi_ready, KB * u + k + 1)
                    ts = slice(u * CH, (u + 1) * CH)
                    nc.vector.tensor_tensor(out=xT_lo[:, k, ts], in0=bank[X2T_PS[u][k]][:], in1=xT_hi[:, k, ts].bitcast(F32),
                                            op=ALU.subtract).then_inc(xT_lo_ready, 1)

            dve.wait_ge(tg_ready, 1)
            a_maxes(0)
            dve.wait_ge(small_in, 96)
            steps.did(nc.vector.tensor_copy(maskf[:], mask8[:]))
            own()
            for a in range(HPB):
                nc.vector.tensor_scalar(mrow[:, :, a, :], maskf[0:1, :].rearrange("p (b k) -> p b k", b=B), -MASKED, MASKED, ALU.mult, ALU.add)
            steps.did(nc.vector.reduce_max(anyv[:], maskf[:].rearrange("p (b k) -> p b k", b=B), AX.X))
            own()
            steps.did(nc.vector.reciprocal(ranyv[:], anyv[:]))
            own()
            steps.did(nc.vector.tensor_tensor(out=flag[:], in0=anyv[:], in1=ranyv[:], op=ALU.mult))
            own()
            steps.did(nc.vector.tensor_scalar(tg_ffn[:], tg[:, 2:4], flag[:, 0:1], flag[:, 1:2], ALU.mult, ALU.mult))
            own()
            a_maxes(1)
            a_add(0)
            ln2_variances(0)
            a_maxes(2)
            ln2_normed(0)
            a_add(1)
            ln2_variances(1)
            a_maxes(3)
            xT_lo_out(0)
            ln2_normed(1)
            a_add(2)
            ln2_variances(2)
            xT_lo_out(1)
            ln2_normed(2)
            a_add(3)
            ln2_variances(3)
            xT_lo_out(2)
            ln2_normed(3)
            xT_lo_out(3)

            dve.wait_ge(acc_zeroed, 1)

            def add_up(e, u):
                dve.wait_ge(down_done[1], 1 + e * (BLK // 2) + (u + 1) * FB // 2)
                ts = slice(u % NC * CH, (u % NC + 1) * CH)
                for m in range(KB):
                    ins = nc.vector.tensor_tensor(out=acc[:, m, ts], in0=bank[4 + 2 * (u % 2) + m][:], in1=acc[:, m, ts], op=ALU.add)
                ins.then_inc(acc_added[u % 2], 1)

            with dve.Fori(0, NE0) as e:
                for k in range(BLK):
                    i = k % 2
                    done = e * (BLK // 2) + k // 2
                    dve.wait_ge(up_ps, e * BLK + k + 1)
                    dve.wait_ge(silu_ready, e * BLK + k + 1)
                    nc.vector.tensor_tensor(out=hid[i][:], in0=bank[2 + i][:], in1=silu[i][:], op=ALU.mult).then_inc(hid_ready[i], 1)
                    dve.wait_ge(hid_ready[i], 1 + done + 1)
                    dve.wait_ge(down_done[i], 1 + done)
                    nc.vector.tensor_copy(hid_hi[i][:], hid[i][:]).then_inc(hi_ready, 1)
                    dve.wait_ge(hi_ready, e * BLK + k + 1)
                    nc.vector.tensor_tensor(out=hid_lo[i][:], in0=hid[i][:], in1=hid_hi[i][:].bitcast(F32),
                                            op=ALU.subtract).then_inc(lo_ready, 1)
                    if k and k % FB == 0:
                        add_up(e, k // FB - 1)
                add_up(e, UNITS - 1)

            def bc(v):
                return v.unsqueeze(2).to_broadcast([P, CT, E])

            def add_experts(f, banks, of):
                for j in of:
                    x = tiles(f * CT + j, 1)[0]
                    dve.wait_ge(c_yT_ps, 2 * f + j // 2 + 1)
                    ins = nc.vector.scalar_tensor_tensor(out=x, in0=bank[banks[j // 2]][:, j % 2 * D:(j % 2 + 1) * D],
                                                         scalar=tg_ffn[:, 0:1], in1=x, op0=ALU.mult, op1=ALU.add)
                return ins

            def front_variances(f):
                wait_apart(c_x2, f + 1)
                variances(tiles(f * CT, CT), LN_FRONT, front)

            def front_normed(f):
                front.did(normed(tiles(f * CT, CT), [xnC[:, j, :] for j in range(CT)], LN_FRONT, f + 1))

            def front_variances2(f):
                wait_apart(front.sem, front.value())
                variances([xnC[:, j, :] for j in range(CT)], LN_FRONT2, front)
                front.round_over()

            def front_normed2(f):
                normed([xnC[:, j, :] for j in range(CT)], [xnC2[:, j, :] for j in range(CT)], LN_FRONT2, f + 1).then_inc(c_ln, 1)

            def q_out(f, m):
                dve.wait_ge(c_q_ps, HB * f + m + 1)
                nc.vector.tensor_scalar(qT[:, m, :], bank[SIM[m]][:], HD ** -0.5, None, ALU.mult).then_inc(c_q_dve, 1)

            def maxes(c, j, half):
                dve.wait_ge(c_sim_ps, 2 * (c * CT + j) + half + 1)
                for i in range(2):
                    h = half * HH + i
                    ins = nc.vector.reduce_max(nmC[j % 2][:, h:h + 3:2],
                                               bank[SIM[2 * half + i]][:, 0:HPB * KEYS].rearrange("p (a k) -> p a k", a=HPB),
                                               AX.X, negate=True)
                ins.then_inc(c_nmax, 1)

            def dens(c, j, half):
                heads = slice(half * HH, (half + 1) * HH)
                dve.wait_ge(c_probs, 2 * (c * CT + j) + half + 1)
                nc.vector.reciprocal(rdenC[j % 2][:, heads], denC[j % 2][:, heads]).then_inc(c_rden, 1)

            def pT_out(c, j, g):
                dve.wait_ge(c_pT_ps, 4 * (c * CT + j) + g + 1)
                nc.vector.tensor_copy(PTC[:, 4 * g:4 * g + 4, :].rearrange("p a b -> p (a b)"), bank[1][0:KH, :]).then_inc(c_pT_dve, 1)

            def o_out(c, j):
                dve.wait_ge(c_o_ps, c * CT + j + 1)
                nc.vector.tensor_copy(oT[:].rearrange("p k t -> p (k t)"), bank[5][:]).then_inc(c_o, 1)

            def add_attention(c, j):
                dve.wait_ge(c_out_ps, c * CT + j + 1)
                x = tiles(c * CT + j, 1)[0]
                nc.vector.scalar_tensor_tensor(out=x, in0=bank[7][:, 0:D], scalar=tg[:, 1:2], in1=x,
                                               op0=ALU.mult, op1=ALU.add).then_inc(c_res, 1)

            def route_variances(r):
                ln4.round(r, LN4_STEPS)
                wait_apart(c_res, (r + 1) * CT)
                variances(tiles(r * CT, CT), LN_ROUTE, ln4)
                ln4.round_over()

            def route_normed(r):
                wait_apart(scattered, ZEROED + 16 * CT * r)
                normed(tiles(r * CT, CT), [rows[:, j, R_XN] for j in range(CT)], LN_ROUTE, r + 1).then_inc(r_ln, 1)

            def route_shift(r):
                route.round(r, ROUTE_STEPS)
                dve.wait_ge(r_logit_ps, CT * r + CT)
                logits = bank[7][:, D:D + CT * E].rearrange("p (j e) -> p j e", j=CT)
                route.did(nc.vector.reduce_max(rs["max"][:], logits, AX.X))
                own(route)
                nc.vector.tensor_tensor(out=rt["d"][:], in0=logits, in1=bc(rs["max"][:]), op=ALU.subtract).then_inc(r_shift, 1)

            def route_choice(r):
                dve.wait_ge(r_exp, r + 1)
                route.did(nc.vector.reduce_sum(rs["sum"][:], rt["e"][:], AX.X))
                own(route)
                route.did(nc.vector.reciprocal(rs["rsum"][:], rs["sum"][:]))
                own(route)
                route.did(nc.vector.tensor_tensor(out=rt["p"][:], in0=rt["e"][:], in1=bc(rs["rsum"][:]), op=ALU.mult))
                own(route)
                route.did(nc.vector.reduce_max(rs["best"][:], rt["p"][:], AX.X))
                own(route)
                route.did(nc.vector.tensor_tensor(out=rt["top"][:], in0=rt["p"][:], in1=bc(rs["best"][:]), op=ALU.is_equal))
                own(route)
                route.did(nc.vector.tensor_tensor(out=rt["score"][:], in0=rt["top"][:], in1=desc[:], op=ALU.mult))
                own(route)
                route.did(nc.vector.reduce_max(rs["first"][:], rt["score"][:], AX.X))
                own(route)
                nc.vector.tensor_copy(rt["before"][:], chosen[:].unsqueeze(1).to_broadcast([P, CT, E]))
                nc.vector.tensor_tensor(out=rt["one"][:], in0=rt["score"][:], in1=bc(rs["first"][:]),
                                        op=ALU.is_equal).then_inc(r_one, 1)
                dve.wait_ge(r_one, r + 1)
                nc.vector.tensor_tensor(out=rt["m2"][:], in0=rt["one"][:], in1=slot0[:], op=ALU.mult)
                route.did(nc.vector.reduce_sum(rt_count[:], rt["one"][:].rearrange("p j e -> p e j"), AX.X))
                own(route)
                nc.vector.reduce_sum(rs["slot"][:], rt["m2"][:], AX.X)
                nc.vector.tensor_scalar(rows[:, :, R_GATE], rs["best"][:].unsqueeze(2), tg_ffn[:, 1:2], None, ALU.mult)
                nc.vector.tensor_copy(rows[:, :, R_TOKEN].bitcast(U32), token_id[:, bass.ts(r, CT)].unsqueeze(2))
                route.did(nc.vector.tensor_tensor(out=chosen[:], in0=rt_count[:], in1=chosen[:], op=ALU.add))

            def route_places(r):
                dve.wait_ge(r_loc_ps, r + 1)
                at = D + CT * E
                nc.vector.tensor_tensor(out=rt["m1"][:].rearrange("p j e -> p (j e)"), in0=bank[7][:, at:at + CT * E],
                                        in1=rt["one"][:].rearrange("p j e -> p (j e)"), op=ALU.mult).then_inc(r_loc_read, 1)

            def route_slots(r):
                dve.wait_ge(r_loc_read, r + 1)
                route.did(nc.vector.reduce_sum(rs["loc"][:], rt["m1"][:], AX.X))
                own(route)
                nc.vector.tensor_scalar(rs["far"][:], rs["loc"][:], float(CAP), float(DROPPED), ALU.is_ge, ALU.mult)
                route.did(nc.vector.tensor_tensor(out=rs["slot"][:], in0=rs["slot"][:], in1=rs["loc"][:], op=ALU.add))
                own(route)
                nc.vector.tensor_tensor(out=slot_c[:], in0=rs["slot"][:], in1=rs["far"][:], op=ALU.add).then_inc(r_slot, 1)
                route.round_over()

            def chunk(c, with_front, with_route):
                f, r = c + 1, c - 1
                if with_front:
                    front.round(f, FRONT_STEPS)
                    add_experts(f, (0, 1), (0, 1))
                dens(c, 0, 1)
                maxes(c, 1, 0)
                if with_front:
                    add_experts(f, (0, 1), (2, 3)).then_inc(c_x2, 1)
                maxes(c, 1, 1)
                pT_out(c, 0, 1)
                dens(c, 1, 0)
                pT_out(c, 0, 3)
                dens(c, 1, 1)
                if with_front:
                    front_variances(f)
                o_out(c, 0)
                maxes(c, 2, 0)
                maxes(c, 2, 1)
                if with_route:
                    route_shift(r)
                pT_out(c, 1, 1)
                dens(c, 2, 0)
                add_attention(c, 0)
                pT_out(c, 1, 3)
                dens(c, 2, 1)
                if with_route:
                    route_choice(r)
                if with_front:
                    front_normed(f)
                o_out(c, 1)
                maxes(c, 3, 0)
                maxes(c, 3, 1)
                pT_out(c, 2, 1)
                dens(c, 3, 0)
                add_attention(c, 1)
                pT_out(c, 2, 3)
                dens(c, 3, 1)
                if with_route:
                    route_places(r)
                if with_front:
                    front_variances2(f)
                o_out(c, 2)
                pT_out(c, 3, 1)
                add_attention(c, 2)
                if with_front:
                    front_normed2(f)
                pT_out(c, 3, 3)
                if with_route:
                    route_slots(r)
                o_out(c, 3)
                add_attention(c, 3)
                route_variances(c)
                if with_front:
                    q_out(f, 1)
                route_normed(c)
                if with_front:
                    q_out(f, 3)
                    for half in range(2):
                        maxes(f, 0, half)
                    dens(f, 0, 0)

            for m in range(1, HB, 2):
                dve.wait_ge(c_prep_ps, m + 1)
                nc.vector.tensor_copy(k1T[:, m, :], bank[m][:, 0:AK]).then_inc(c_prep_dve, 1)
            front.round(0, FRONT_STEPS)
            add_experts(0, (4, 5), range(CT)).then_inc(c_x2, 1)
            front_variances(0)
            for r in range(1, 2 * B, 2):
                dve.wait_ge(c_prep_ps, HB + r + 1)
                nc.vector.tensor_copy(V1[:, r, :], bank[V_PS[r]][0:KH, :]).then_inc(c_prep_dve, 1)
            front_normed(0)
            front_variances2(0)
            front_normed2(0)
            q_out(0, 1)
            q_out(0, 3)
            for half in range(2):
                maxes(0, 0, half)
            dens(0, 0, 0)
            chunk(0, True, False)
            with dve.Fori(1, NC - 1) as c:
                chunk(c, True, True)
            chunk(NC - 1, False, True)
            route_shift(NC - 1)
            route_choice(NC - 1)
            route_places(NC - 1)
            route_slots(NC - 1)

            dve.wait_ge(be_in, 16)
            for half in range(2):
                dve.wait_ge(e_kept_in[half], 16)
            with dve.Fori(0, E // EB) as p:
                for i in range(EB):
                    e = EB * p + i
                    dve.wait_ge(e_y_ps, e + 1)
                    nc.vector.tensor_tensor(out=yb[i % 2][:], in0=bank[4 + i][:].rearrange("p (s d) -> p s d", d=D),
                                            in1=be_all[:, bass.ds(e, 1), :].to_broadcast([P, CAP // P, D]), op=ALU.add).then_inc(e_yb, 1)
                    dve.wait_ge(e_yb, EB + e + 1)
                    for s in range(CAP // P):
                        row = kept[:, bass.ds(e, 1), s, :].rearrange("p a r -> p (a r)")
                        ins = nc.vector.scalar_tensor_tensor(out=ye[:, bass.ds(e, 1), s, :].rearrange("p a d -> p (a d)"), in0=yb[i % 2][:, s, :],
                                                             scalar=row[:, K_GATE], in1=row[:, K_X], op0=ALU.mult, op1=ALU.add)
                    ins.then_inc(e_y, 1)


FRONT_STEPS, LN4_STEPS, ROUTE_STEPS = 5, 2, 12


_INS = ['x', 'ctx_1024', 'mask_BxS2_bk0', 'g_xattn', 'g_ffn', 'L0_xattn_W', 'L0_xattn_b', 'L0_ffn_Wg', 'L0_ffn_Wu', 'L0_ffn_Wd',
        'L1_xattn_ln_gamma', 'L1_xattn_ln_beta', 'L1_xattn_Wq', 'L1_xattn_Wkv', 'L1_xattn_Wout', 'L1_ffn_wg', 'L1_ffn_W', 'L1_ffn_b']
_OUTS = [((2, 1024, 256), 'float32')]


def kernel(**inputs):
    import numpy as _np
    import concourse.bacc as _bacc
    from concourse import mybir as _mybir
    from concourse.bass_utils import run_bass_kernel_spmd as _run

    nc = _bacc.Bacc("TRN2", target_bir_lowering=False, num_devices=1)
    arrays, args = {}, []
    for name in _INS:
        a = _np.ascontiguousarray(inputs[name])
        arrays[f"in_{name}_dram"] = a
        args.append(nc.dram_tensor(f"in_{name}_dram", a.shape, _mybir.dt.from_np(a.dtype), kind="ExternalInput").ap())
    for i, (shape, dtype) in enumerate(_OUTS):
        dt = _mybir.dt.from_np(_np.dtype(dtype))
        args.append(nc.dram_tensor(f"out_{i}_dram", shape, dt, kind="ExternalOutput").ap())
    flamingo_kernel(nc, *args)
    r = _run(nc, [arrays], core_ids=[0])
    got = tuple(r.results[0][f"out_{i}_dram"] for i in range(len(_OUTS)))
    return got[0]
```
